# Optimizing a Trainium2 kernel written in Bass

```python
import numpy as np
import jax
import jax.numpy as jnp

def _softmax(x, axis=-1):
    return jax.nn.softmax(x, axis=axis)

def _gelu(x):
    return jax.nn.gelu(x, approximate=True)

def _silu(x):
    return jax.nn.silu(x)

def _sigmoid(x):
    return jax.nn.sigmoid(x)

def _layernorm(x, axis=-1, eps=1e-05):
    m = jnp.mean(x, axis=axis, keepdims=True)
    v = jnp.var(x, axis=axis, keepdims=True)
    return (x - m) / jnp.sqrt(v + eps)

def _scatter_add(tgt, idx, src, axis=0):
    return tgt.at[idx].add(src)

def _segment_sum(src, seg, n):
    return jax.ops.segment_sum(src, seg, n)
kernel_name = 'mk_hybrid_d1_jaxref_r8_db2805'

def setup_inputs(seed: int=0):
    np.random.seed(seed)
    _w = jnp.asarray

    def _L0_attn_a_setup():
        import jax, jax.numpy as jnp
        import numpy as np
        B, T, C, H, N_LAYER, LAYER_ID = (4, 256, 128, 16, 12, 6)
        N = C // H
        Q = 32

        def _forward(x, time_maa_x, time_maa_w, time_maa_k, time_maa_v, time_maa_r, maa_w1, maa_w2, decay_w1, decay_w2, time_decay, time_faaaa, Wr, Wk, Wv, Wo, ln_g, ln_b):
            b, t, c = x.shape
            nc = t // Q
            xx = jnp.pad(x, ((0, 0), (1, 0), (0, 0)))[:, :-1] - x
            xxx = x + xx * time_maa_x
            m = jnp.tanh(xxx @ maa_w1).reshape(b, t, 4, -1)
            m = jnp.einsum('btfd,fdc->fbtc', m, maa_w2)
            mw, mk, mv, mr = (m[0], m[1], m[2], m[3])
            xw = x + xx * (time_maa_w + mw)
            xk = x + xx * (time_maa_k + mk)
            xv = x + xx * (time_maa_v + mv)
            xr = x + xx * (time_maa_r + mr)
            r = (xr @ Wr).reshape(b, t, H, N).transpose(0, 2, 1, 3)
            k = (xk @ Wk).reshape(b, t, H, N).transpose(0, 2, 1, 3)
            v = (xv @ Wv).reshape(b, t, H, N).transpose(0, 2, 1, 3)
            w = time_decay + jnp.tanh(xw @ decay_w1) @ decay_w2
            w = w.reshape(b, t, H, N).transpose(0, 2, 1, 3).mean(axis=-1)
            w_log = -jnp.exp(w)
            wc = w_log.reshape(b, H, nc, Q, 1)
            wc_cum = jnp.cumsum(wc, axis=-2)
            shifted = jnp.pad(wc_cum, ((0, 0), (0, 0), (0, 0), (1, 0), (0, 0)))[..., :-1, :]
            ws_log = wc.sum(axis=-2, keepdims=True)
            w_inter = jnp.exp(ws_log - wc_cum)
            w_intra = jnp.exp(wc_cum - wc)
            ws = jnp.exp(ws_log)
            A = shifted - jnp.swapaxes(wc_cum, -1, -2)
            strict = jnp.tril(jnp.ones((Q, Q), dtype=bool), -1)
            w_mask = jnp.where(strict, jnp.exp(jnp.where(strict, A, 0.0)), 0.0)
            rr = r.reshape(b, H, nc, Q, N)
            kk = k.reshape(b, H, nc, Q, N)
            vv = v.reshape(b, H, nc, Q, N)
            kv = jnp.einsum('bhcqn,bhcqm->bhcnm', kk * w_inter, vv)

            def step(state, inp):
                ws_i, kv_i = inp
                return (ws_i * state + kv_i, state)
            _, states = jax.lax.scan(step, jnp.zeros((b, H, N, N), x.dtype), (jnp.moveaxis(ws, 2, 0), jnp.moveaxis(kv, 2, 0)))
            states = jnp.moveaxis(states, 0, 2)
            inter = jnp.einsum('bhcqn,bhcnm->bhcqm', rr * w_intra, states)
            scores = jnp.einsum('bhcqn,bhckn->bhcqk', rr, kk) * w_mask
            diag = jnp.sum(rr * (time_faaaa * kk), axis=-1)
            intra = jnp.einsum('bhcqk,bhckm->bhcqm', scores, vv) + diag[..., None] * vv
            y = (inter + intra).reshape(b, H, t, N).transpose(0, 2, 1, 3).reshape(b, t, c)
            mu = y.mean(axis=-1, keepdims=True)
            var = ((y - mu) ** 2).mean(axis=-1, keepdims=True)
            y = (y - mu) / jnp.sqrt(var + 1e-05) * ln_g + ln_b
            return y @ Wo
        key = jax.random.key(seed)
        ks = jax.random.split(key, 9)
        r0 = LAYER_ID / (N_LAYER - 1)
        r1 = 1.0 - LAYER_ID / N_LAYER
        ddd = (jnp.arange(C, dtype=jnp.float32) / C)[None, None, :]
        h = jnp.arange(C, dtype=jnp.float32)
        s = 1.0 / np.sqrt(C)
        return {'x': jax.random.normal(ks[0], (B, T, C), jnp.float32), 'time_maa_x': 1.0 - ddd ** r1, 'time_maa_w': 1.0 - ddd ** r1, 'time_maa_k': 1.0 - ddd ** r1, 'time_maa_v': 1.0 - (ddd ** r1 + 0.3 * r0), 'time_maa_r': 1.0 - ddd ** (0.5 * r1), 'maa_w1': jax.random.uniform(ks[1], (C, 4 * 32), jnp.float32, minval=-0.01, maxval=0.01), 'maa_w2': jax.random.uniform(ks[2], (4, 32, C), jnp.float32, minval=-0.01, maxval=0.01), 'decay_w1': jax.random.uniform(ks[3], (C, 64), jnp.float32, minval=-0.01, maxval=0.01), 'decay_w2': jax.random.uniform(ks[4], (64, C), jnp.float32, minval=-0.01, maxval=0.01), 'time_decay': (-6.0 + 5.0 * (h / (C - 1)) ** (0.7 + 1.3 * r0))[None, None, :], 'time_faaaa': (r0 * (1.0 - h / (C - 1))).reshape(1, H, 1, 1, N), 'Wr': jax.random.normal(ks[5], (C, C), jnp.float32) * s, 'Wk': jax.random.normal(ks[6], (C, C), jnp.float32) * s, 'Wv': jax.random.normal(ks[7], (C, C), jnp.float32) * s, 'Wo': jax.random.normal(ks[8], (C, C), jnp.float32) * s, 'ln_g': jnp.ones((C,), jnp.float32), 'ln_b': jnp.zeros((C,), jnp.float32)}
    _L0_attn_a_in = _L0_attn_a_setup()

    def _L0_attn_b_setup():
        import jax, jax.numpy as jnp
        import numpy as np
        from math import log2, ceil
        HEADS, DIM_HEAD, BLOCK, EPS = (16, 64, 16, 1e-08)
        key = jax.random.key(seed)
        k1, k2, k3, k4 = jax.random.split(key, 4)
        b, n, dim = (4, 512, 128)
        inner = HEADS * DIM_HEAD
        return {'x': jax.random.normal(k1, (b, n, dim), jnp.float32), 'w_qkv': jax.random.normal(k2, (inner * 3, dim), jnp.float32) * 0.02, 'w_out': jax.random.normal(k3, (dim, inner), jnp.float32) * 0.02, 'b_out': jax.random.normal(k4, (dim,), jnp.float32) * 0.02}
    _L0_attn_b_in = _L0_attn_b_setup()

    def _L0_ffn_setup():
        import jax, jax.numpy as jnp
        import numpy as np
        H = 128
        I = 256
        E = 32
        B, S = (4, 256)

        def _grouped_mm(a, w, group_sizes):
            return jax.lax.ragged_dot(a, w, group_sizes)

        def _swiglu(x, gw, uw, dw):
            return jax.nn.silu(x @ gw) * (x @ uw) @ dw
        key = jax.random.key(seed)
        ks = jax.random.split(key, 8)
        scale = 0.02
        inp = {'hidden_states': jax.random.normal(ks[0], (B, S, H), dtype=jnp.float32), 'gate_w': jax.random.normal(ks[1], (H, E), dtype=jnp.float32) * scale, 'shared_gate_w': jax.random.normal(ks[2], (H, I), dtype=jnp.float32) * scale, 'shared_up_w': jax.random.normal(ks[3], (H, I), dtype=jnp.float32) * scale, 'shared_down_w': jax.random.normal(ks[4], (I, H), dtype=jnp.float32) * scale, 'routed_gate_w': jax.random.normal(ks[5], (E, H, I), dtype=jnp.float32) * scale, 'routed_up_w': jax.random.normal(ks[6], (E, H, I), dtype=jnp.float32) * scale, 'routed_down_w': jax.random.normal(ks[7], (E, I, H), dtype=jnp.float32) * scale}
        return inp
    _L0_ffn_in = _L0_ffn_setup()
    _d = {'L0_attn_a_x': _L0_attn_a_in['x'], 'L0_attn_a_time_maa_x': _L0_attn_a_in['time_maa_x'], 'L0_attn_a_time_maa_w': _L0_attn_a_in['time_maa_w'], 'L0_attn_a_time_maa_k': _L0_attn_a_in['time_maa_k'], 'L0_attn_a_time_maa_v': _L0_attn_a_in['time_maa_v'], 'L0_attn_a_time_maa_r': _L0_attn_a_in['time_maa_r'], 'L0_attn_a_maa_w1': _L0_attn_a_in['maa_w1'], 'L0_attn_a_maa_w2': _L0_attn_a_in['maa_w2'], 'L0_attn_a_decay_w1': _L0_attn_a_in['decay_w1'], 'L0_attn_a_decay_w2': _L0_attn_a_in['decay_w2'], 'L0_attn_a_time_decay': _L0_attn_a_in['time_decay'], 'L0_attn_a_time_faaaa': _L0_attn_a_in['time_faaaa'], 'L0_attn_a_Wr': _L0_attn_a_in['Wr'], 'L0_attn_a_Wk': _L0_attn_a_in['Wk'], 'L0_attn_a_Wv': _L0_attn_a_in['Wv'], 'L0_attn_a_Wo': _L0_attn_a_in['Wo'], 'L0_attn_a_ln_g': _L0_attn_a_in['ln_g'], 'L0_attn_a_ln_b': _L0_attn_a_in['ln_b'], 'L0_attn_b_w_qkv': _L0_attn_b_in['w_qkv'], 'L0_attn_b_w_out': _L0_attn_b_in['w_out'], 'L0_attn_b_b_out': _L0_attn_b_in['b_out'], 'L0_ffn_gate_w': _L0_ffn_in['gate_w'], 'L0_ffn_shared_gate_w': _L0_ffn_in['shared_gate_w'], 'L0_ffn_shared_up_w': _L0_ffn_in['shared_up_w'], 'L0_ffn_shared_down_w': _L0_ffn_in['shared_down_w'], 'L0_ffn_routed_gate_w': _L0_ffn_in['routed_gate_w'], 'L0_ffn_routed_up_w': _L0_ffn_in['routed_up_w'], 'L0_ffn_routed_down_w': _L0_ffn_in['routed_down_w']}
    _x0 = _d['L0_attn_a_x']
    _d['L0_attn_a_x'] = jax.random.normal(jax.random.fold_in(jax.random.key(seed), 1), (2, 1024, 128), dtype=_x0.dtype)
    del _x0
    return _d

def reference(L0_attn_a_x, L0_attn_a_time_maa_x, L0_attn_a_time_maa_w, L0_attn_a_time_maa_k, L0_attn_a_time_maa_v, L0_attn_a_time_maa_r, L0_attn_a_maa_w1, L0_attn_a_maa_w2, L0_attn_a_decay_w1, L0_attn_a_decay_w2, L0_attn_a_time_decay, L0_attn_a_time_faaaa, L0_attn_a_Wr, L0_attn_a_Wk, L0_attn_a_Wv, L0_attn_a_Wo, L0_attn_a_ln_g, L0_attn_a_ln_b, L0_attn_b_w_qkv, L0_attn_b_w_out, L0_attn_b_b_out, L0_ffn_gate_w, L0_ffn_shared_gate_w, L0_ffn_shared_up_w, L0_ffn_shared_down_w, L0_ffn_routed_gate_w, L0_ffn_routed_up_w, L0_ffn_routed_down_w):

    def _L0_attn_a_ref(x, time_maa_x, time_maa_w, time_maa_k, time_maa_v, time_maa_r, maa_w1, maa_w2, decay_w1, decay_w2, time_decay, time_faaaa, Wr, Wk, Wv, Wo, ln_g, ln_b):
        import jax, jax.numpy as jnp
        import numpy as np
        B, T, C, H, N_LAYER, LAYER_ID = (4, 256, 128, 16, 12, 6)
        N = C // H
        Q = 32

        def _forward(x, time_maa_x, time_maa_w, time_maa_k, time_maa_v, time_maa_r, maa_w1, maa_w2, decay_w1, decay_w2, time_decay, time_faaaa, Wr, Wk, Wv, Wo, ln_g, ln_b):
            b, t, c = x.shape
            nc = t // Q
            xx = jnp.pad(x, ((0, 0), (1, 0), (0, 0)))[:, :-1] - x
            xxx = x + xx * time_maa_x
            m = jnp.tanh(xxx @ maa_w1).reshape(b, t, 4, -1)
            m = jnp.einsum('btfd,fdc->fbtc', m, maa_w2)
            mw, mk, mv, mr = (m[0], m[1], m[2], m[3])
            xw = x + xx * (time_maa_w + mw)
            xk = x + xx * (time_maa_k + mk)
            xv = x + xx * (time_maa_v + mv)
            xr = x + xx * (time_maa_r + mr)
            r = (xr @ Wr).reshape(b, t, H, N).transpose(0, 2, 1, 3)
            k = (xk @ Wk).reshape(b, t, H, N).transpose(0, 2, 1, 3)
            v = (xv @ Wv).reshape(b, t, H, N).transpose(0, 2, 1, 3)
            w = time_decay + jnp.tanh(xw @ decay_w1) @ decay_w2
            w = w.reshape(b, t, H, N).transpose(0, 2, 1, 3).mean(axis=-1)
            w_log = -jnp.exp(w)
            wc = w_log.reshape(b, H, nc, Q, 1)
            wc_cum = jnp.cumsum(wc, axis=-2)
            shifted = jnp.pad(wc_cum, ((0, 0), (0, 0), (0, 0), (1, 0), (0, 0)))[..., :-1, :]
            ws_log = wc.sum(axis=-2, keepdims=True)
            w_inter = jnp.exp(ws_log - wc_cum)
            w_intra = jnp.exp(wc_cum - wc)
            ws = jnp.exp(ws_log)
            A = shifted - jnp.swapaxes(wc_cum, -1, -2)
            strict = jnp.tril(jnp.ones((Q, Q), dtype=bool), -1)
            w_mask = jnp.where(strict, jnp.exp(jnp.where(strict, A, 0.0)), 0.0)
            rr = r.reshape(b, H, nc, Q, N)
            kk = k.reshape(b, H, nc, Q, N)
            vv = v.reshape(b, H, nc, Q, N)
            kv = jnp.einsum('bhcqn,bhcqm->bhcnm', kk * w_inter, vv)

            def step(state, inp):
                ws_i, kv_i = inp
                return (ws_i * state + kv_i, state)
            _, states = jax.lax.scan(step, jnp.zeros((b, H, N, N), x.dtype), (jnp.moveaxis(ws, 2, 0), jnp.moveaxis(kv, 2, 0)))
            states = jnp.moveaxis(states, 0, 2)
            inter = jnp.einsum('bhcqn,bhcnm->bhcqm', rr * w_intra, states)
            scores = jnp.einsum('bhcqn,bhckn->bhcqk', rr, kk) * w_mask
            diag = jnp.sum(rr * (time_faaaa * kk), axis=-1)
            intra = jnp.einsum('bhcqk,bhckm->bhcqm', scores, vv) + diag[..., None] * vv
            y = (inter + intra).reshape(b, H, t, N).transpose(0, 2, 1, 3).reshape(b, t, c)
            mu = y.mean(axis=-1, keepdims=True)
            var = ((y - mu) ** 2).mean(axis=-1, keepdims=True)
            y = (y - mu) / jnp.sqrt(var + 1e-05) * ln_g + ln_b
            return y @ Wo
        return _forward(x, time_maa_x, time_maa_w, time_maa_k, time_maa_v, time_maa_r, maa_w1, maa_w2, decay_w1, decay_w2, time_decay, time_faaaa, Wr, Wk, Wv, Wo, ln_g, ln_b)

    def _L0_attn_b_ref(x, w_qkv, w_out, b_out):
        import jax, jax.numpy as jnp
        import numpy as np
        from math import log2, ceil
        HEADS, DIM_HEAD, BLOCK, EPS = (16, 64, 16, 1e-08)
        b, n, dim = x.shape
        pad_to_len = 2 ** ceil(log2(n))
        if pad_to_len != n:
            x = jnp.pad(x, ((0, 0), (0, pad_to_len - n), (0, 0)))
        qkv = x @ w_qkv.T
        q, k, v = jnp.split(qkv, 3, axis=-1)

        def split_heads(t):
            return t.reshape(b, pad_to_len, HEADS, DIM_HEAD).transpose(0, 2, 1, 3).reshape(b * HEADS, pad_to_len, DIM_HEAD)
        q = split_heads(q) * DIM_HEAD ** (-0.5)
        k = split_heads(k)
        v = split_heads(v)
        num_levels = int(log2(pad_to_len // BLOCK)) - 1
        qkvs = [(q, k, v)]
        for _ in range(num_levels):
            q = q.reshape(q.shape[0], -1, 2, DIM_HEAD).mean(2)
            k = k.reshape(k.shape[0], -1, 2, DIM_HEAD).mean(2)
            v = v.reshape(v.shape[0], -1, 2, DIM_HEAD).sum(2)
            qkvs.append((q, k, v))
        neg_max = -jnp.finfo(x.dtype).max
        idx = jnp.arange(pad_to_len)
        Ysum = jnp.zeros((b * HEADS, pad_to_len, DIM_HEAD), x.dtype)
        Asum = jnp.zeros((b * HEADS, pad_to_len), x.dtype)
        for lvl, (ql, kl, vl) in enumerate(qkvs):
            B = ql.shape[0]
            nb = ql.shape[1] // BLOCK
            ql = ql.reshape(B, nb, BLOCK, DIM_HEAD)
            kl = kl.reshape(B, nb, BLOCK, DIM_HEAD)
            vl = vl.reshape(B, nb, BLOCK, DIM_HEAD)
            if lvl == 0:
                S = jnp.einsum('bnid,bnjd->bnij', ql, kl)
                S = jnp.where(jnp.triu(jnp.ones((BLOCK, BLOCK), bool), 1), neg_max, S)
                S = S - S.max(-1, keepdims=True)
                A = jnp.exp(S)
                y = jnp.einsum('bnij,bnjd->bnid', A, vl).reshape(B, pad_to_len, DIM_HEAD)
                Av = A.sum(-1).reshape(B, pad_to_len)
            else:
                q2 = ql.reshape(B, nb // 2, 2, BLOCK, DIM_HEAD)[:, :, 1]
                k1b = kl.reshape(B, nb // 2, 2, BLOCK, DIM_HEAD)[:, :, 0]
                v1b = vl.reshape(B, nb // 2, 2, BLOCK, DIM_HEAD)[:, :, 0]
                S = jnp.einsum('bnid,bnjd->bnij', q2, k1b)
                S = S - S.max(-1, keepdims=True)
                A = jnp.exp(S)
                y = jnp.einsum('bnij,bnjd->bnid', A, v1b)
                Av = A.sum(-1)
                y = jnp.pad(y[:, :, None], ((0, 0), (0, 0), (1, 0), (0, 0), (0, 0))).reshape(B, -1, DIM_HEAD)
                Av = jnp.pad(Av[:, :, None], ((0, 0), (0, 0), (1, 0), (0, 0))).reshape(B, -1)
                y = jnp.repeat(y, 2 ** lvl, axis=1)
                Av = jnp.repeat(Av, 2 ** lvl, axis=1)
            seq_key = (idx >> lvl << lvl) + (2 ** lvl - 1)
            keep = seq_key <= idx
            Ysum = Ysum + jnp.where(keep[None, :, None], y, 0.0)
            Asum = Asum + jnp.where(keep[None, :], Av, 0.0)
        out = Ysum / (Asum + EPS)[..., None]
        out = out.reshape(b, HEADS, pad_to_len, DIM_HEAD).transpose(0, 2, 1, 3).reshape(b, pad_to_len, HEADS * DIM_HEAD)
        out = out @ w_out.T + b_out
        return out[:, :n]

    def _L0_ffn_ref(hidden_states, gate_w, shared_gate_w, shared_up_w, shared_down_w, routed_gate_w, routed_up_w, routed_down_w):
        import jax, jax.numpy as jnp
        import numpy as np
        H = 128
        I = 256
        E = 32
        B, S = (4, 256)

        def _grouped_mm(a, w, group_sizes):
            return jax.lax.ragged_dot(a, w, group_sizes)

        def _swiglu(x, gw, uw, dw):
            return jax.nn.silu(x @ gw) * (x @ uw) @ dw
        b, s, h = hidden_states.shape
        x = hidden_states.reshape(-1, h)
        shared_out = _swiglu(x, shared_gate_w, shared_up_w, shared_down_w)
        logits = x @ gate_w
        topk_ids = jnp.argmax(logits, axis=-1)
        topk_val = jnp.max(logits, axis=-1)
        scores = jax.nn.sigmoid(topk_val)[:, None]
        xs = x * scores
        tokens_per_expert = jnp.zeros((E,), jnp.int32).at[topk_ids].add(1)
        order = jnp.argsort(topk_ids)
        sorted_x = xs[order]
        g = _grouped_mm(sorted_x, routed_gate_w, tokens_per_expert)
        u = _grouped_mm(sorted_x, routed_up_w, tokens_per_expert)
        d = _grouped_mm(jax.nn.silu(g) * u, routed_down_w, tokens_per_expert)
        inv = jnp.argsort(order)
        routed_out = d[inv]
        return (shared_out + routed_out).reshape(b, s, h)
    x = L0_attn_a_x
    x = x + _L0_attn_a_ref(_layernorm(x, axis=-1), L0_attn_a_time_maa_x, L0_attn_a_time_maa_w, L0_attn_a_time_maa_k, L0_attn_a_time_maa_v, L0_attn_a_time_maa_r, L0_attn_a_maa_w1, L0_attn_a_maa_w2, L0_attn_a_decay_w1, L0_attn_a_decay_w2, L0_attn_a_time_decay, L0_attn_a_time_faaaa, L0_attn_a_Wr, L0_attn_a_Wk, L0_attn_a_Wv, L0_attn_a_Wo, L0_attn_a_ln_g, L0_attn_a_ln_b)
    x = x + _L0_ffn_ref(_layernorm(x, axis=-1), L0_ffn_gate_w, L0_ffn_shared_gate_w, L0_ffn_shared_up_w, L0_ffn_shared_down_w, L0_ffn_routed_gate_w, L0_ffn_routed_up_w, L0_ffn_routed_down_w)
    x = x + _L0_attn_b_ref(_layernorm(x, axis=-1), L0_attn_b_w_qkv, L0_attn_b_w_out, L0_attn_b_b_out)
    x = x + _L0_ffn_ref(_layernorm(x, axis=-1), L0_ffn_gate_w, L0_ffn_shared_gate_w, L0_ffn_shared_up_w, L0_ffn_shared_down_w, L0_ffn_routed_gate_w, L0_ffn_routed_up_w, L0_ffn_routed_down_w)
    return x

_drawn_inputs = setup_inputs


def setup_inputs(seed=0):
    import zlib

    import numpy as np

    out = dict(_drawn_inputs(seed))
    spreads = {'L0_attn_a_ln_g': (1.0, 0.2), 'L0_attn_a_ln_b': (0.0, 0.1)}
    factors = {'L0_attn_a_time_maa_x': 8.0,
     'L0_attn_a_time_maa_w': 8.0,
     'L0_attn_a_maa_w1': 8.0,
     'L0_attn_a_maa_w2': 8.0,
     'L0_attn_a_decay_w1': 8.0,
     'L0_attn_a_decay_w2': 8.0,
     'L0_attn_a_time_faaaa': 2.729,
     'L0_attn_b_b_out': 3.94,
     'L0_ffn_gate_w': 8.0,
     'L0_ffn_shared_gate_w': 4.879,
     'L0_ffn_shared_up_w': 4.771,
     'L0_ffn_shared_down_w': 4.813,
     'L0_ffn_routed_gate_w': 8.0,
     'L0_ffn_routed_up_w': 8.0,
     'L0_ffn_routed_down_w': 8.0}
    for name, (base, spread) in spreads.items():
        noise = np.random.default_rng([zlib.crc32(name.encode()), seed]).standard_normal(out[name].shape)
        drawn = base * np.exp(spread * noise) if base else spread * noise
        out[name] = jnp.asarray(drawn.astype(out[name].dtype))
    for name, factor in factors.items():
        out[name] = (out[name] * factor).astype(out[name].dtype)
    return out
```

```python
from contextlib import ExitStack

import concourse.bass as bass
from concourse import mybir

F32 = mybir.dt.float32
I32 = mybir.dt.int32
U32 = mybir.dt.uint32
ALU = mybir.AluOpType
ACT = mybir.ActivationFunctionType
AX = mybir.AxisListType.X

P = 128
C = 128
BATCH = 2
SEQ = 1024
TOK = BATCH * SEQ
TILES = TOK // P
CHUNK = 512
CT = CHUNK // P
STEPS = TOK // CHUNK
HALVES = SEQ // CHUNK
EPS = 1e-5
ARENA = 24300
CREDIT = 1

HEADS_A = 16
N_A = C // HEADS_A
DECAY = 64
MIX = 32

HEADS_B = 16
D_B = 64
PAIRS = HEADS_B * D_B // P
LEVELS = 5
COARSE = sum(TOK // 2 ** (l + 1) for l in range(1, LEVELS + 1))
OCT = 1024
SUB = OCT // P
SLOT_Y = D_B + 1

EXPERTS = 32
INNER = 256
WROW = 2 * INNER + INNER // P * C
SLOTS = 48
assert SLOTS >= TOK // P + EXPERTS - 1 and SLOTS % 4 == 0

CONST = {}
_at = 0
for _n, _w in [("ident", P), ("head_ones", P), ("later", P), ("ones", P), ("expert_rank", EXPERTS),
               ("tile_reset", EXPERTS * TILES), ("slot_no", SLOTS), ("tile_start", TILES),
               ("mask_causal", 32), ("mask_block", 32), ("half", TILES), ("pick", N_A * P)]:
    CONST[_n] = (_at, _w)
    _at += _w
CONST_COLS = _at


class Chain:

    def __init__(self, eng, sem):
        self.eng, self.sem, self.n, self.moving = eng, sem, 0, 0

    def __call__(self, ins):
        ins.then_inc(self.sem, 1)
        self.n += 1
        self.eng.wait_ge(self.sem, self.moving + self.n)

    def enter(self, i, per):
        self.moving, self.start, self.per = i * per, self.n, per

    def leave(self, times):
        assert self.n - self.start == self.per, (self.n - self.start, self.per)
        self.moving, self.n = 0, self.start + self.per * times


def hybrid_block(nc, w, out):
    with ExitStack() as ctx:
        sem_cache = {}

        def sb(name, shape, dt=F32):
            return ctx.enter_context(nc.sbuf_tensor(name, shape, dt))

        def sem(name):
            return ctx.enter_context(nc.semaphore(name))

        bank = [ctx.enter_context(nc.psum_tensor(f"bank{i}", [P, 512], F32)) for i in range(8)]

        experts = sb("experts", [P, EXPERTS * WROW])
        x_tok = sb("x_tok", [P, TOK])
        const = sb("const", [P, CONST["pick"][0]])
        vectors = sb("vectors", [P, 9])
        gate_w = sb("gate_w", [P, EXPERTS])
        shared_up = sb("shared_up", [P, 2 * INNER])
        shared_down = sb("shared_down", [P, INNER // P * C])
        zeros = sb("zeros", [P, C])
        stat = sb("stat", [P, 4 * CT])
        arena = sb("arena", [P, ARENA])

        used = [0]

        def carve(n):
            at = used[0]
            used[0] += n
            assert used[0] <= ARENA, used[0]
            return arena[:, at:at + n]

        def constant(name):
            at, width = CONST[name]
            return const[:, at:at + width]

        ident, ones = constant("ident"), constant("ones")
        (maa_x, maa_w, maa_k, maa_v, maa_r, t_decay, faaaa, ln_g, ln_b) = (vectors[:, i:i + 1] for i in range(9))

        sorted_x = nc.dram_tensor("sorted_x", (SLOTS * P, C), F32, kind="Internal").ap()
        sorted_y = nc.dram_tensor("sorted_y", (SLOTS * P, C), F32, kind="Internal").ap()

        loaded, loaded_x, loaded_experts = sem("loaded"), sem("loaded_x"), sem("loaded_experts")
        zero_row, zeroed, stored = sem("zero_row"), sem("zeroed"), sem("stored")
        dve_chain, act_chain, pool_chain = sem("dve_chain"), sem("act_chain"), sem("pool_chain")

        ln_var, ln_rstd = sem("ln_var"), sem("ln_rstd")
        ln_count = {"dve": 0, "pool": 0}

        def tiles_of(ap):
            return ap.rearrange("p (a b) -> p a b", b=C)

        def over(col):
            return col.unsqueeze(2).to_broadcast([P, CT, C])

        mean, var, rstd = (stat[:, CT * i:CT * i + CT] for i in range(3))

        def norm(dve, chain, src, centred, square, target, n, free=None):
            chain(dve.reduce_sum(mean, src, AX))
            chain(dve.scalar_tensor_tensor(tiles_of(centred), over(mean), -1.0 / C, src, ALU.mult, ALU.add))
            chain(dve.tensor_tensor(square, centred, centred, ALU.mult))
            chain(dve.reduce_sum(var, tiles_of(square), AX))
            dve.tensor_scalar(var, var, 1.0 / C, EPS, ALU.mult, ALU.add).then_inc(ln_var, 1)
            dve.wait_ge(ln_rstd, n + 1)
            if free is not None:
                free()
            return dve.tensor_tensor(tiles_of(target), tiles_of(centred), over(rstd), ALU.mult)

        def norm_power(pool, n):
            pool.wait_ge(ln_var, n + 1)
            pool.tensor_tensor(rstd, var, constant("half")[:, 0:CT], ALU.pow).then_inc(ln_rstd, 1)

        w1 = carve(4 * MIX)
        w2 = carve(C)
        dw1 = carve(DECAY)
        dw2 = carve(C)
        dw2_mean = carve(C)
        wrkvo = carve(4 * C)
        wv_wide = carve(N_A * C)
        pick = carve(N_A * P)
        a_decay = carve(2)
        a_norm = [carve(CHUNK) for _ in range(3)]
        a_x = [carve(CHUNK + 1) for _ in range(2)]
        a_xx, a_xxx, a_mix = carve(CHUNK), carve(CHUNK), carve(CHUNK)
        a_in = [carve(CHUNK) for _ in range(4)]
        a_th, a_d = carve(CHUNK), carve(CHUNK)
        a_k, a_v, a_r = carve(CHUNK), carve(CHUNK), carve(CHUNK)
        a_kv = [carve(CHUNK) for _ in range(2)]
        a_state = carve(N_A * (CHUNK + 1)).rearrange("p (m t) -> p m t", m=N_A)
        a_g = [carve(CHUNK) for _ in range(2)]
        a_ruk, a_diag = carve(CHUNK), carve(CHUNK)
        a_y, a_ynt = carve(CHUNK), carve(CHUNK)
        used_a = used[0]

        s = {n: sem("a_" + n) for n in (
            "weights xn xt xs xxx mix_in mix wf tf xf decay_in th dlog d proj rkv rowed kv bank_free state g y_done "
            "ruk diag_in diag dv y yt y2 yn_t yn_copied o x1 carry decay_mean").split()}

        XT_BANK, MISC, ROT, YB, OB = bank[0], bank[1], bank[2:6], bank[6], bank[7]

        credited = [s[n] for n in "diag kv xf o y_done yn_t rowed g diag_in state".split()]

        def a_steps(eng, chain=None, per=0):
            with eng.Fori(0, BATCH) as b:
                if chain:
                    chain.enter(b, per)
                for half in range(HALVES):
                    yield b * HALVES + half, half
            if chain:
                chain.leave(BATCH)

        def a_pe(pe):
            pe.wait_ge(s["weights"], 1)
            pe.wait_ge(loaded, LOADS * 16)
            pe.matmul(MISC[:, 0:1], constant("head_ones"), t_decay, start=True, stop=True).then_inc(s["decay_in"], 1)
            for g, half in a_steps(pe):
                pe.wait_ge(s["xn"], 2 * g + 1)
                for t in range(CT):
                    i = pe.transpose(XT_BANK[:, t * P:t * P + P], a_norm[2][:, t * C:t * C + C], ident)
                i.then_inc(s["xt"], 1)
                pe.wait_ge(s["xxx"], g + 1)
                if half == 0:
                    pe.wait_ge(s["decay_mean"], 1)
                pe.wait_ge(s["diag"], g + CREDIT)
                pe.matmul(MISC[:, :], w1, a_xxx, start=True, stop=True).then_inc(s["mix_in"], 1)
                pe.wait_ge(s["mix"], g + 1)
                pe.wait_ge(s["kv"], N_A * g + CREDIT)
                for f in range(4):
                    pe.matmul(ROT[f][:, :], w2[f * MIX:f * MIX + MIX, :], a_mix[f * MIX:f * MIX + MIX, :],
                              start=True, stop=True).then_inc(s["wf"], 1)
                pe.wait_ge(s["xf"], 4 * g + 1 + CREDIT)
                pe.matmul(MISC[0:DECAY, :], dw1, a_in[0], start=True, stop=True).then_inc(s["decay_in"], 1)
                for f, at in ((1, 1), (2, 2), (3, 0)):
                    pe.wait_ge(s["xf"], 4 * g + f + 1 + CREDIT)
                    pe.matmul(ROT[f][:, :], wrkvo[:, at * C:at * C + C], a_in[f],
                              start=True, stop=True).then_inc(s["proj"], 1)
                pe.wait_ge(s["th"], g + 1)
                pe.matmul(MISC[:, :], dw2_mean[0:DECAY, :], a_th[0:DECAY, :], start=True, stop=True)\
                  .then_inc(s["dlog"], 1)
                for m in range(N_A + 2):
                    if m < N_A:
                        if 1 <= m < 4:
                            pe.wait_ge(s["rkv"], 3 * g + m)
                        if m >= 4:
                            pe.wait_ge(s["kv"], N_A * g + m - 3 + CREDIT)
                        pe.matmul(ROT[m % 4][:, :], wv_wide[:, m * C:m * C + C], a_in[2],
                                  start=True, stop=True).then_inc(s["rowed"], 1)
                    if m == 2:
                        pe.wait_ge(s["d"], g + 1)
                        pe.wait_ge(s["ruk"], g + 1)
                        pe.matmul(MISC[:, :], constant("head_ones"), a_ruk, start=True, stop=True)\
                          .then_inc(s["diag_in"], 1)
                    if m >= 2:
                        q = m - 2
                        pe.wait_ge(s["g"], N_A * g + q + 1 + CREDIT)
                        i = pe.matmul(YB[:, :], pick[:, q * P:q * P + P], a_g[q % 2],
                                      start=(q == 0), stop=(q == N_A - 1))
                        i.then_inc(s["y_done"], 1)
                pe.wait_ge(s["y"], g + 1)
                for t in range(CT):
                    i = pe.transpose(XT_BANK[:, t * P:t * P + P], a_y[:, t * P:t * P + P], ident)
                i.then_inc(s["yt"], 1)
                pe.wait_ge(s["xn"], 2 * g + 2)
                for t in range(CT):
                    i = pe.transpose(XT_BANK[:, t * P:t * P + P], a_norm[2][:, t * C:t * C + C], ident)
                i.then_inc(s["yn_t"], 1)
                pe.wait_ge(s["yn_copied"], g + 1)
                for t in range(CT):
                    i = pe.matmul(OB[:, t * C:t * C + C], a_ynt[:, t * P:t * P + P], wrkvo[:, 3 * C:4 * C],
                                  start=True, stop=True)
                i.then_inc(s["o"], 1)

        def a_act(act):
            chain = Chain(act, act_chain)
            act.wait_ge(s["decay_in"], 1)
            act.activation(a_decay[:, 0:1], MISC[:, 0:1], ACT.Copy, scale=1.0 / N_A).then_inc(s["decay_mean"], 1)
            act.wait_ge(s["decay_mean"], 1)
            act.wait_ge(s["weights"], 1)
            for g, half in a_steps(act, chain, 2):
                act.wait_ge(s["xt"], g + 1)
                act.wait_ge(s["xf"], 4 * g + CREDIT)
                if half:
                    act.wait_ge(s["xs"], g)
                    act.activation(a_x[1][:, 0:1], a_x[0][:, CHUNK:CHUNK + 1], ACT.Copy)
                act.activation(a_x[half][:, 1:CHUNK + 1], XT_BANK[:, :], ACT.Copy).then_inc(s["xs"], 1)
                act.wait_ge(s["mix_in"], g + 1)
                act.activation(a_mix, MISC[:, :], ACT.Tanh).then_inc(s["mix"], 1)
                act.wait_ge(s["decay_in"], g + 2)
                act.activation(a_th[0:DECAY, :], MISC[0:DECAY, :], ACT.Tanh).then_inc(s["th"], 1)
                for n, dst in ((1, a_k), (2, a_v), (3, a_r)):
                    act.wait_ge(s["proj"], 3 * g + n)
                    act.activation(dst, ROT[n][:, :], ACT.Copy).then_inc(s["rkv"], 1)
                act.wait_ge(s["dlog"], g + 1)
                chain(act.activation(a_d, MISC[:, :], ACT.Exp, bias=a_decay[:, 0:1]))
                act.activation(a_d, a_d, ACT.Exp, scale=-1.0).then_inc(s["d"], 1)
                act.wait_ge(s["diag_in"], g + 1 + CREDIT)
                act.activation(a_diag, MISC[:, :], ACT.Copy).then_inc(s["diag"], 1)
                act.wait_ge(s["yn_t"], g + 1 + CREDIT)
                act.wait_ge(s["o"], g + CREDIT)
                act.activation(a_ynt, XT_BANK[:, :], ACT.Identity, scale=ln_g, bias=ln_b)\
                   .then_inc(s["yn_copied"], 1)

        def a_pool(pool):
            for g, half in a_steps(pool):
                norm_power(pool, 2 * g)
                x = a_x[half][:, 1:CHUNK + 1]
                for f in range(4):
                    pool.wait_ge(s["tf"], 4 * g + f + 1)
                    pool.tensor_tensor(a_in[f], a_in[f], x, ALU.add).then_inc(s["xf"], 1)
                pool.wait_ge(s["rkv"], 3 * g + 3)
                for m in range(N_A):
                    pool.wait_ge(s["state"], N_A * g + m + 1 + CREDIT)
                    if m >= 2:
                        pool.wait_ge(s["y_done"], N_A * g + m - 1 + CREDIT)
                    if m < 2:
                        pool.wait_ge(s["y_done"], N_A * g + CREDIT)
                    pool.tensor_tensor(a_g[m % 2], a_r, a_state[:, m, 0:CHUNK], ALU.mult).then_inc(s["g"], 1)
                    if m == 3:
                        pool.wait_ge(s["diag"], g + 1 + CREDIT)
                        pool.tensor_tensor(a_diag, a_diag, a_v, ALU.mult).then_inc(s["dv"], 1)
                norm_power(pool, 2 * g + 1)

        def a_dve(dve):
            chain = Chain(dve, dve_chain)
            dve.wait_ge(loaded, LOADS * 16)
            chain(dve.memset(a_x[0][:, 0:1], 0.0))
            chain(dve.reduce_sum(dw2_mean[0:DECAY, 0:HEADS_A],
                                 dw2[0:DECAY, :].rearrange("p (h n) -> p h n", n=N_A), AX))
            chain(dve.tensor_scalar(dw2[0:DECAY, :].rearrange("p (h n) -> p h n", n=N_A),
                                    dw2_mean[0:DECAY, 0:HEADS_A].unsqueeze(2).to_broadcast([DECAY, HEADS_A, N_A]),
                                    1.0 / N_A, None, ALU.mult))
            chain(dve.tensor_copy(dw2_mean[0:DECAY, :], dw2[0:DECAY, :]))
            for m in range(N_A):
                i = dve.tensor_copy(
                    wv_wide[:, m * C:m * C + C].rearrange("p (h n) -> p h n", n=N_A),
                    wrkvo[:, 2 * C + m:3 * C:N_A].unsqueeze(2).to_broadcast([P, HEADS_A, N_A]))
                if m < N_A - 1:
                    chain(i)
            i.then_inc(s["weights"], 1)
            dve.wait_ge(loaded_x, 16)
            for g, half in a_steps(dve, chain, 2 * 11):
                chunk = x_tok[:, bass.ds(g * CHUNK, CHUNK)]
                norm(dve, chain, tiles_of(chunk), a_norm[0], a_norm[1], a_norm[2], 2 * g,
                     lambda: dve.wait_ge(s["yn_t"], g + CREDIT)).then_inc(s["xn"], 1)
                dve.wait_ge(s["xs"], g + 1)
                x = a_x[half][:, 1:CHUNK + 1]
                chain(dve.tensor_tensor(a_xx, a_x[half][:, 0:CHUNK], x, ALU.subtract))
                dve.scalar_tensor_tensor(a_xxx, a_xx, maa_x, x, ALU.mult, ALU.add).then_inc(s["xxx"], 1)
                for f, maa in enumerate((maa_w, maa_k, maa_v, maa_r)):
                    dve.wait_ge(s["wf"], 4 * g + f + 1)
                    if f == 2:
                        dve.wait_ge(s["rowed"], N_A * g + CREDIT)
                    dve.scalar_tensor_tensor(a_in[f], ROT[f][:, :], maa, a_xx, ALU.add, ALU.mult)\
                       .then_inc(s["tf"], 1)
                if half == 0:
                    chain(dve.memset(a_state[:, :, 0], 0.0))
                else:
                    dve.wait_ge(s["g"], N_A * g + CREDIT)
                    chain(dve.tensor_copy(a_state[:, :, 0], a_state[:, :, CHUNK]))
                dve.wait_ge(s["rkv"], 3 * g + 3)
                for m in range(N_A + 1):
                    if m < N_A:
                        dve.wait_ge(s["rowed"], N_A * g + m + 1 + CREDIT)
                        if m >= 2:
                            dve.wait_ge(s["state"], N_A * g + m - 1 + CREDIT)
                        dve.tensor_tensor(a_kv[m % 2], a_k, ROT[m % 4][:, :], ALU.mult).then_inc(s["kv"], 1)
                    if m == 1:
                        dve.wait_ge(s["diag_in"], g + CREDIT)
                        dve.scalar_tensor_tensor(a_ruk, a_r, faaaa, a_k, ALU.mult, ALU.mult).then_inc(s["ruk"], 1)
                    if m >= 1:
                        q = m - 1
                        if q == 0:
                            dve.wait_ge(s["d"], g + 1)
                        if q > 0:
                            dve.wait_ge(s["state"], N_A * g + q + CREDIT)
                        dve.wait_ge(s["kv"], N_A * g + q + 1 + CREDIT)
                        dve.tensor_tensor_scan(a_state[:, q, 1:CHUNK + 1], a_d, a_kv[q % 2], a_state[:, q, 0:1],
                                               ALU.mult, ALU.add).then_inc(s["state"], 1)
                dve.wait_ge(s["y_done"], N_A * g + N_A + CREDIT)
                dve.wait_ge(s["dv"], g + 1)
                dve.tensor_tensor(a_y, YB[:, :], a_diag, ALU.add).then_inc(s["y"], 1)
                dve.wait_ge(s["yt"], g + 1)
                norm(dve, chain, tiles_of(XT_BANK[:, :]), a_norm[0], a_norm[1], a_norm[2], 2 * g + 1)\
                    .then_inc(s["xn"], 1)
                dve.wait_ge(s["o"], g + 1 + CREDIT)
                chain(dve.tensor_tensor(chunk, chunk, OB[:, :], ALU.add))
            return chain

        used[0] = 0
        f_norm = [carve(CHUNK) for _ in range(3)]
        f_xt = carve(CHUNK)
        f_gated = [carve(CHUNK) for _ in range(2)]
        f_h = [carve(CHUNK) for _ in range(2)]
        f_xs = carve(TOK)
        f_one_hot = carve(EXPERTS * TILES)
        f_best = carve(TILES)
        f_score = carve(TILES)
        f_pick = [carve(CT * EXPERTS) for _ in range(2)]
        f_count, f_upto, f_before, f_place = (carve(EXPERTS * TILES) for _ in range(4))
        f_tiles, f_first, f_upto_slot, f_ones = (carve(EXPERTS) for _ in range(4))
        f_slot_cmp = carve(SLOTS * EXPERTS)
        f_slot_row, f_place_row = carve(SLOTS), carve(TILES)
        f_slot_at, f_row = sb("slot_at", [P, SLOTS], I32), sb("row", [P, TILES], U32)
        f_gx = [carve(C) for _ in range(4)]
        f_gxt = [carve(P) for _ in range(2)]
        f_sg = [carve(INNER) for _ in range(2)]
        f_sh = [carve(INNER) for _ in range(2)]
        f_sht = [carve(INNER) for _ in range(2)]
        f_gy = [carve(C) for _ in range(4)]
        f_back = carve(TOK)
        LN_F = [2 * STEPS, 2 * STEPS + STEPS + STEPS]
        LN_B = 2 * STEPS + STEPS

        t = {n: sem("f_" + n) for n in (
            "xn xt xt_copied logits shared gated h down best scored rank counts placed rows "
            "gx_t gxt gu sg sh sh_t sht y y_copied gathered").split()}
        scattered, slot_in = sem("f_scattered"), [sem(f"f_slot_in{j}") for j in range(4)]
        slot_out = [sem(f"f_slot_out{j}") for j in range(4)]
        credited += [t[n] for n in "down xt xt_copied gated h scored gx_t gxt gu sg sh sh_t sht y_copied".split()]
        credited += slot_out

        def f_pe(pe, k):
            with pe.Fori(0, STEPS) as c:
                g = c + STEPS * k
                pe.wait_ge(t["xn"], g + 1)
                for i in range(CT):
                    mm = pe.transpose(bank[0][:, i * P:i * P + P], f_norm[2][:, i * C:i * C + C], ident)
                mm.then_inc(t["xt"], 1)
                pe.wait_ge(t["xt_copied"], g + 1 + CREDIT)
                for i in range(CT):
                    mm = pe.matmul(bank[1][:, i * EXPERTS:i * EXPERTS + EXPERTS], f_xt[:, i * P:i * P + P], gate_w[:, :],
                                   start=True, stop=True)
                mm.then_inc(t["logits"], 1)
                pe.wait_ge(t["h"], 2 * g + CREDIT)
                for n in (0, 2, 1, 3):
                    pe.matmul(bank[2 + n][:, :], shared_up[:, n * P:n * P + P], f_xt, start=True, stop=True)\
                      .then_inc(t["shared"], 1)
                pe.wait_ge(t["h"], 2 * g + 2 + CREDIT)
                pe.wait_ge(t["down"], g + CREDIT)
                for i in range(CT):
                    for half in range(2):
                        mm = pe.matmul(bank[6][:, i * C:i * C + C], f_h[half][:, i * P:i * P + P],
                                       shared_down[:, half * C:half * C + C], start=(half == 0), stop=(half == 1))
                mm.then_inc(t["y"], 1)
            pe.wait_ge(t["best"], STEPS * (k + 1))
            pe.matmul(bank[0][:, :], constant("later"), f_one_hot, start=True, stop=True).then_inc(t["rank"], 1)
            pe.matmul(bank[1][:, :], ones, f_one_hot, start=True, stop=True).then_inc(t["counts"], 1)
            pe.wait_ge(t["rows"], k + 1)

            def weights(s, at, size):
                first = pe.value_load(f_slot_at[0:1, bass.ds(s, 1)], min_val=0, max_val=(EXPERTS - 1) * WROW)
                return experts[:, bass.ds(first + at, size)]

            def turn_in(s, j):
                n = SLOTS * k + s
                pe.wait_ge(slot_in[j], 16 * (SLOTS // 4 * k + 1) + 4 * (s - j))
                pe.wait_ge(t["gxt"], n - 1 + CREDIT)
                pe.transpose(bank[j % 2][:, 0:P], f_gx[j], ident).then_inc(t["gx_t"], 1)

            def gate_up(s, j):
                n = SLOTS * k + s
                w_up = weights(s, 0, 2 * INNER)
                pe.wait_ge(t["gxt"], n + 1 + CREDIT)
                pe.wait_ge(t["sh"], n - 1 + CREDIT)
                pe.matmul(bank[2 + j % 2][:, :], f_gxt[j % 2], w_up, start=True, stop=True)\
                  .then_inc(t["gu"], 1)

            def turn_h(s, j):
                n = SLOTS * k + s
                pe.wait_ge(t["sh"], n + 1 + CREDIT)
                pe.wait_ge(t["sht"], n - 1 + CREDIT)
                for half in range(2):
                    mm = pe.transpose(bank[4 + j % 2][:, half * P:half * P + P], f_sh[j % 2][:, half * P:half * P + P], ident)
                mm.then_inc(t["sh_t"], 1)

            def down(s, j):
                n = SLOTS * k + s
                w_down = weights(s, 2 * INNER, 2 * C)
                pe.wait_ge(t["sht"], n + 1 + CREDIT)
                pe.wait_ge(t["y_copied"], n - 1 + CREDIT)
                for half in range(2):
                    mm = pe.matmul(bank[6 + j % 2][:, 0:C], f_sht[j % 2][:, half * P:half * P + P],
                                   w_down[:, half * C:half * C + C], start=(half == 0), stop=(half == 1))
                mm.then_inc(t["y"], 1)

            pe.wait_ge(loaded_experts, 16 * EXPERT_LOADS)
            slots(pe, [(turn_in, 1), (gate_up, 0), (down, -2), (turn_h, -1)])

        def slots(eng, stages):
            lead = max(d for _, d in stages)
            lag = min(d for _, d in stages)
            first = 4
            last = SLOTS - 4

            def step(s, j):
                for stage, d in stages:
                    if isinstance(s, int) and not 0 <= s + d < SLOTS:
                        continue
                    stage(s + d, (j + d) % 4)

            for s in range(-lead, first):
                step(s, s % 4)
            with eng.Fori(first // 4, last // 4) as i:
                for j in range(4):
                    step(i * 4 + j, j)
            for s in range(last, SLOTS - lag):
                step(s, s % 4)

        def f_act(act, k):
            with act.Fori(0, STEPS) as c:
                g = c + STEPS * k
                act.wait_ge(t["xt"], g + 1 + CREDIT)
                act.wait_ge(t["down"], g + CREDIT)
                act.activation(f_xt, bank[0][:, :], ACT.Copy).then_inc(t["xt_copied"], 1)
                for n in range(2):
                    act.wait_ge(t["shared"], 4 * g + 2 * n + 1)
                    act.wait_ge(t["h"], 2 * g + CREDIT)
                    act.activation(f_gated[n], bank[2 + n][:, :], ACT.Silu).then_inc(t["gated"], 1)
            act.wait_ge(t["best"], STEPS * (k + 1))
            act.activation(f_score, f_best, ACT.Sigmoid).then_inc(t["scored"], 1)

            def copy_in(s, j):
                n = SLOTS * k + s
                act.wait_ge(t["gx_t"], n + 1 + CREDIT)
                act.wait_ge(t["gu"], n - 1 + CREDIT)
                act.activation(f_gxt[j % 2], bank[j % 2][:, 0:P], ACT.Copy).then_inc(t["gxt"], 1)

            def gate(s, j):
                n = SLOTS * k + s
                act.wait_ge(t["gu"], n + 1 + CREDIT)
                act.wait_ge(t["sh"], n - 1 + CREDIT)
                act.activation(f_sg[j % 2], bank[2 + j % 2][:, 0:INNER], ACT.Silu).then_inc(t["sg"], 1)

            def copy_y(s, j):
                n = SLOTS * k + s
                act.wait_ge(t["y"], STEPS * (k + 1) + n + 1)
                act.wait_ge(slot_out[j], 16 * (SLOTS // 4) * k + 4 * (s - j) + CREDIT)
                act.activation(f_gy[j], bank[6 + j % 2][:, 0:C], ACT.Copy).then_inc(t["y_copied"], 1)

            slots(act, [(copy_in, 1), (gate, 0), (copy_y, -2)])

        def f_dve(dve, chain, k):
            with dve.Fori(0, STEPS) as c:
                chain.enter(c, 9)
                g = c + STEPS * k
                chunk = x_tok[:, bass.ds(c * CHUNK, CHUNK)]
                norm(dve, chain, tiles_of(chunk), f_norm[0], f_norm[1], f_norm[2], c + LN_F[k],
                     lambda: dve.wait_ge(t["xt"], g + CREDIT)).then_inc(t["xn"], 1)
                dve.wait_ge(t["xn"], g + 1)
                chain(dve.tensor_copy(f_xs[:, bass.ds(c * CHUNK, CHUNK)], f_norm[2]))
                dve.wait_ge(t["logits"], g + 1)
                logit = bank[1][:, 0:CT * EXPERTS].rearrange("p (i e) -> p i e", e=EXPERTS)
                best = f_best[:, bass.ds(c * CT, CT)]
                chain(dve.reduce_max(best, logit, AX))
                wide = lambda a: a.unsqueeze(2).to_broadcast([P, CT, EXPERTS])
                is_best, key = (a.rearrange("p (i e) -> p i e", e=EXPERTS) for a in f_pick)
                falling = constant("expert_rank").unsqueeze(1).to_broadcast([P, CT, EXPERTS])
                chain(dve.tensor_tensor(is_best, logit, wide(best), ALU.is_ge))
                chain(dve.tensor_tensor(key, is_best, falling, ALU.mult))
                chain(dve.reduce_max(stat[:, 3 * CT:4 * CT], key, AX))
                dve.tensor_tensor(
                    f_one_hot.rearrange("p (e i) -> p i e", e=EXPERTS)[:, bass.ds(c * CT, CT), :],
                    falling, wide(stat[:, 3 * CT:4 * CT]), ALU.is_equal).then_inc(t["best"], 1)
                dve.wait_ge(t["best"], g + 1)
                for n in range(2):
                    dve.wait_ge(t["shared"], 4 * g + 2 * n + 2)
                    dve.wait_ge(t["gated"], 2 * g + n + 1 + CREDIT)
                    dve.tensor_tensor(f_h[n], f_gated[n], bank[4 + n][:, :], ALU.mult).then_inc(t["h"], 1)
                dve.wait_ge(t["y"], g + SLOTS * k + 1)
                dve.tensor_tensor(chunk, chunk, bank[6][:, :], ALU.add).then_inc(t["down"], 1)
                dve.wait_ge(t["down"], g + 1 + CREDIT)
            chain.leave(STEPS)
            by = lambda a: a.rearrange("p (e i) -> p e i", e=EXPERTS)
            spread = lambda a: a.unsqueeze(2).to_broadcast([P, EXPERTS, TILES])
            chain(dve.memset(f_ones, 1.0))
            dve.wait_ge(t["counts"], k + 1)
            chain(dve.tensor_copy(f_count, bank[1][:, :]))
            chain(dve.tensor_tensor_scan(f_upto, constant("tile_reset"), f_count, 0.0, ALU.mult, ALU.add))
            starts = constant("tile_start").unsqueeze(1).to_broadcast([P, EXPERTS, TILES])
            chain(dve.tensor_tensor(by(f_before), spread(by(f_upto)[:, :, TILES - 1]), starts, ALU.is_gt))
            chain(dve.reduce_sum(f_tiles, by(f_before), AX))
            chain(dve.tensor_tensor_scan(f_upto_slot, f_ones, f_tiles, 0.0, ALU.mult, ALU.add))
            chain(dve.tensor_tensor(f_first, f_upto_slot, f_tiles, ALU.subtract))
            chain(dve.tensor_scalar(f_first, f_first, float(P), None, ALU.mult))
            chain(dve.tensor_tensor(f_before, f_upto, f_count, ALU.subtract))
            dve.wait_ge(t["rank"], k + 1)
            chain(dve.tensor_tensor(f_place, f_before, bank[0][:, :], ALU.add))
            chain(dve.tensor_tensor(by(f_place), by(f_place), spread(f_first), ALU.add))
            chain(dve.tensor_tensor(f_place, f_place, f_one_hot, ALU.mult))
            chain(dve.reduce_sum(f_place_row, f_place.rearrange("p (e i) -> p i e", e=EXPERTS), AX))
            dve.tensor_copy(f_row[:, :], f_place_row).then_inc(t["placed"], 1)
            dve.wait_ge(t["placed"], 2 * k + 1)
            dve.wait_ge(t["scored"], k + 1 + CREDIT)
            x3 = f_xs.rearrange("p (i c) -> p i c", c=C)
            dve.tensor_tensor(x3, x3, f_score.unsqueeze(2).to_broadcast([P, TILES, C]), ALU.mult)\
               .then_inc(t["placed"], 1)
            by_slot = f_slot_cmp.rearrange("p (s e) -> p s e", e=EXPERTS)
            chain(dve.tensor_tensor(by_slot, f_upto_slot.unsqueeze(1).to_broadcast([P, SLOTS, EXPERTS]),
                                    constant("slot_no").unsqueeze(2).to_broadcast([P, SLOTS, EXPERTS]), ALU.is_le))
            chain(dve.reduce_sum(f_slot_row, by_slot, AX))
            chain(dve.tensor_scalar(f_slot_row, f_slot_row, EXPERTS - 1.0, float(WROW), ALU.min, ALU.mult))
            dve.tensor_copy(f_slot_at[:, :], f_slot_row).then_inc(t["rows"], 1)

            def product(s, j):
                n = SLOTS * k + s
                dve.wait_ge(t["sg"], n + 1 + CREDIT)
                dve.wait_ge(t["sh_t"], n - 1 + CREDIT)
                dve.tensor_tensor(f_sh[j % 2], f_sg[j % 2], bank[2 + j % 2][:, INNER:2 * INNER], ALU.mult)\
                   .then_inc(t["sh"], 1)

            def copy_h(s, j):
                n = SLOTS * k + s
                dve.wait_ge(t["sh_t"], n + 1 + CREDIT)
                dve.wait_ge(t["y"], STEPS * (k + 1) + n - 1)
                dve.tensor_copy(f_sht[j % 2], bank[4 + j % 2][:, 0:INNER]).then_inc(t["sht"], 1)

            slots(dve, [(copy_h, -1), (product, 0)])
            for i in range(CT):
                dve.wait_ge(t["gathered"], 16 * (TILES * k + TILES))
                part = slice(i * CHUNK, i * CHUNK + CHUNK)
                chain(dve.tensor_tensor(x_tok[:, part], x_tok[:, part], f_back[:, part], ALU.add))

        def f_pool(pool, k):
            with pool.Fori(0, STEPS) as c:
                norm_power(pool, c + LN_F[k])
            pool.wait_ge(t["placed"], 2 * (k + 1))
            pool.wait_ge(zeroed, 16)
            for i in range(TILES):
                pool.indirect_dma_start(out=sorted_x, out_offset=bass.IndirectOffsetOnAxis(ap=f_row[:, i:i + 1], axis=0),
                                        in_=f_xs[:, i * C:i * C + C], in_offset=None).then_inc(scattered, 16)
            for j in range(4):
                pool.wait_ge(slot_out[j], 16 * (SLOTS // 4) * (k + 1) + CREDIT)
            for i in range(TILES):
                pool.indirect_dma_start(out=f_back[:, i * C:i * C + C], out_offset=None, in_=sorted_y,
                                        in_offset=bass.IndirectOffsetOnAxis(ap=f_row[:, i:i + 1], axis=0))\
                    .then_inc(t["gathered"], 16)

        def f_sp(sp, k):
            sp.wait_ge(scattered, 16 * TILES * (k + 1))

            def fetch(s, j):
                n = SLOTS * k + s
                if not isinstance(n, int) or n >= 4:
                    sp.wait_ge(t["gx_t"], n - 3 + CREDIT)
                sp.dma_start(f_gx[j], sorted_x[bass.ds(s * P, P), :]).then_inc(slot_in[j], 16)

            def store(s, j):
                sp.wait_ge(t["y_copied"], SLOTS * k + s + 1 + CREDIT)
                sp.dma_start(sorted_y[bass.ds(s * P, P), :], f_gy[j]).then_inc(slot_out[j], 16)

            slots(sp, [(fetch, 3), (store, -3)])

        used[0] = 0
        b_x = carve(TOK)
        b_odd, b_even = carve(OCT), carve(OCT)
        b_q, b_k = carve(OCT), carve(OCT)
        b_v = [carve(2 * SUB * SLOT_Y).rearrange("p (s d) -> p s d", d=SLOT_Y) for _ in range(3)]
        b_s, b_st = carve(2 * SUB * 32), carve(2 * SUB * 32)
        b_max = carve(2 * SUB)
        b_wide_at = used[0]
        b_wide = [carve(2 * SUB * P).rearrange("p (s q) -> p s q", q=P) for _ in range(3)]
        b_y, b_sum = carve(OCT), carve(OCT)
        b_yt, b_at = carve(TOK), carve(TOK)
        b_w = carve(3 * P)
        b_wo = carve(C)
        b_bias = carve(C)
        b_norm = [b_yt[:, n * CHUNK:n * CHUNK + CHUNK] for n in range(3)]
        b_pool, at = [b_x], b_wide_at
        for level in range(1, LEVELS + 1):
            b_pool.append(arena[:, at:at + TOK // 2 ** level])
            at += TOK // 2 ** level
        FIRST_OF = [sum(TOK // 2 ** (l + 1) for l in range(1, level)) for level in range(1, LEVELS + 2)]

        h = {n: sem("b_" + n) for n in (
            "xn xt x pooled packed ready proj q_out s_half s_done masked st expd av y_out sum_out turned turn_act turn_dve "
            "normed o acc").split()}
        w_in, wo_in, bias_in = sem("b_w_in"), sem("b_wo_in"), sem("b_bias_in")
        credited += [h[n] for n in "xt x q_out s_half s_done masked expd av y_out sum_out turned turn_act turn_dve o acc".split()]

        def attention(eng, order, chain=None, per=0):
            lead, lag = max(d for _, d in order), min(d for _, d in order)

            def step(p, o):
                for stage, d in order:
                    u = 3 * p + o + d
                    if isinstance(u, int) and not 0 <= u < 3 * PAIRS:
                        continue
                    stage(p + (o + d) // 3, (o + d) % 3, u)

            for u in range(-lead, 3):
                step(u // 3, u % 3)
            with eng.Fori(1, PAIRS - 1) as p:
                if chain:
                    chain.enter(p - 1, per)
                for o in range(3):
                    step(p, o)
            if chain:
                chain.leave(PAIRS - 2)
            for u in range(3 * (PAIRS - 1), 3 * PAIRS - lag):
                step(u // 3, u % 3)

        def y_bank(n, dst):
            at, size = 6 * n, (6, 6, 4)[n]
            return (dst[:, at * D_B:(at + size) * D_B].rearrange("p (s d) -> p s d", d=D_B),
                    bank[5 + n][:, 0:size * SLOT_Y].rearrange("p (s d) -> p s d", d=SLOT_Y))

        def b_columns(o, odd):
            return b_x[:, o * OCT:o * OCT + OCT] if o < 2 else (b_odd if odd else b_even)

        def b_pe(pe):
            with pe.Fori(0, STEPS) as c:
                pe.wait_ge(h["xn"], c + 1)
                pe.wait_ge(h["x"], c + CREDIT)
                for i in range(CT):
                    mm = pe.transpose(bank[0][:, i * P:i * P + P], b_norm[2][:, i * C:i * C + C], ident)
                mm.then_inc(h["xt"], 1)
            pe.wait_ge(h["x"], STEPS + CREDIT)
            pe.wait_ge(h["packed"], 1)
            pe.wait_ge(h["ready"], 1)

            def turn(p, o, u):
                pe.wait_ge(h["sum_out"], 3 * u + 3 + CREDIT)
                if isinstance(u, int) and u + 2 >= 3 * PAIRS:
                    pe.wait_ge(h["q_out"], 6 * 3 * PAIRS + CREDIT)
                    pe.wait_ge(h["turn_act"], 8 * p + 4 * o + CREDIT)
                else:
                    pe.wait_ge(h["s_half"], u + 3 + CREDIT)
                for n, src in enumerate((b_y, b_sum)):
                    if not isinstance(u, int) or u + 2 < 3 * PAIRS:
                        pe.wait_ge(h["q_out"], 6 * (u + 2) + 4 + 2 * n + CREDIT)
                    for i in range(SUB):
                        mm = pe.transpose(bank[2 - 2 * n + i // 4][:, i % 4 * P:i % 4 * P + P], src[:, i * P:i * P + P], ident)
                        if i % 4 == 3:
                            mm.then_inc(h["turned"], 1)

            def project_qk(p, o, u):
                if o == 0:
                    pe.wait_ge(w_in, 16 * p + 16)
                if isinstance(u, int) and u < 3:
                    pe.wait_ge(h["q_out"], 6 * u + CREDIT)
                if o == 2:
                    pe.wait_ge(h["acc"], 4 * p + CREDIT)
                elif not isinstance(u, int) or u >= 3:
                    pe.wait_ge(h["turn_act"], 8 * p - 4 * (1 - o) + CREDIT)
                for n in range(2):
                    pe.matmul(bank[n][:, :], b_w[:, 0:P], b_columns(o, True)[:, n * 512:n * 512 + 512],
                              start=True, stop=True).then_inc(h["proj"], 1)
                for n in range(2):
                    pe.matmul(bank[2 + n][:, :], b_w[:, P:2 * P], b_columns(o, False)[:, n * 512:n * 512 + 512],
                              start=True, stop=True).then_inc(h["proj"], 1)

            def project_v(p, o, u):
                pe.wait_ge(h["q_out"], 6 * u + 2 + CREDIT)
                for i in range(SUB):
                    if i == 4:
                        pe.wait_ge(h["q_out"], 6 * u + 4 + CREDIT)
                    if i == 5:
                        pe.wait_ge(h["masked"], u + CREDIT)
                    mm = pe.matmul(bank[i // 4][:, i % 4 * P:i % 4 * P + P], b_columns(o, False)[:, i * P:i * P + P],
                                   b_w[:, 2 * P:3 * P], start=True, stop=True)
                    if i == 3:
                        mm.then_inc(h["proj"], 1)
                mm.then_inc(h["proj"], 1)

            def scores(head):
                for i in range(SUB):
                    for j in range(4):
                        rows = slice(head * D_B, head * D_B + D_B)
                        tok = slice(i * P + 32 * j, i * P + 32 * j + 32)
                        mm = pe.matmul(bank[4][32 * j:32 * j + 32, (2 * i + head) * 32:(2 * i + head) * 32 + 32],
                                       b_q[rows, tok], b_k[rows, tok], start=True, stop=True)
                return mm

            def scores_first(p, o, u):
                scores(0).then_inc(h["s_half"], 1)

            def scores_second(p, o, u):
                if isinstance(u, int):
                    pe.wait_ge(h["s_half"], u + 1 + CREDIT)
                scores(1).then_inc(h["s_done"], 1)

            def weighted(p, o, u):
                pe.wait_ge(h["expd"], 4 * u + 4 + CREDIT)
                pe.wait_ge(h["q_out"], 6 * u + 6 + CREDIT)
                pe.wait_ge(h["sum_out"], 3 * u + CREDIT)
                for n in range(2 * SUB):
                    at = n % 6 * SLOT_Y
                    mm = pe.matmul(bank[5 + n // 6][:, at:at + SLOT_Y], b_wide[o][:, n, :], b_v[o][:, n, :],
                                   start=True, stop=True)
                mm.then_inc(h["av"], 1)

            def project_out(p, o, u):
                if o != 2:
                    return
                pe.wait_ge(h["normed"], p + 1)
                pe.wait_ge(wo_in, 16 * p + 16)
                for i in range(TILES):
                    mm = pe.matmul(bank[i // 4][:, i % 4 * C:i % 4 * C + C], b_yt[:, i * P:i * P + P], b_wo,
                                   start=True, stop=True)
                    if i % 4 == 3:
                        mm.then_inc(h["o"], 1)

            attention(pe, [(project_qk, 1), (project_v, 1), (scores_first, 1), (turn, -1), (scores_second, 1), (weighted, 0), (project_out, -1)])

        def b_act(act):
            with act.Fori(0, STEPS) as c:
                act.wait_ge(h["xt"], c + 1 + CREDIT)
                act.activation(b_x[:, bass.ds(c * CHUNK, CHUNK)], bank[0][:, :], ACT.Copy).then_inc(h["x"], 1)
            for level in range(1, LEVELS + 1):
                act.wait_ge(h["pooled"], level)
                n = TOK // 2 ** (level + 1)
                blocks = b_pool[level].rearrange("p (g two i) -> p g two i", two=2, i=16)
                for side, dst, scale in ((0, b_even, 1.0), (1, b_odd, 0.25 ** level)):
                    i = act.activation(dst[:, FIRST_OF[level - 1]:FIRST_OF[level - 1] + n]
                                       .rearrange("p (g i) -> p g i", i=16), blocks[:, :, side, :], ACT.Copy, scale=scale)
            i.then_inc(h["packed"], 1)
            act.wait_ge(h["ready"], 1)

            def copy_turned(p, o, u):
                if o == 2:
                    return
                if o == 0:
                    act.wait_ge(h["o"], 4 * p + CREDIT)
                for n in range(4):
                    act.wait_ge(h["turned"], 4 * u + n + 1 + CREDIT)
                    dst = (b_yt, b_at)[n // 2][:, o * OCT + n % 2 * 512:o * OCT + n % 2 * 512 + 512]
                    act.activation(dst, bank[(2, 3, 0, 1)[n]][:, :], ACT.Copy).then_inc(h["turn_act"], 1)

            def copy_qk(p, o, u):
                act.wait_ge(h["s_done"], u + CREDIT)
                for n in range(4):
                    act.wait_ge(h["proj"], 6 * u + n + 1)
                    dst = (b_q, b_k)[n // 2][:, n % 2 * 512:n % 2 * 512 + 512]
                    act.activation(dst, bank[n][:, :], ACT.Copy, scale=(D_B ** -0.5, 1.0)[n // 2]).then_inc(h["q_out"], 1)

            def copy_v(p, o, u):
                if not isinstance(u, int) or u >= 3:
                    act.wait_ge(h["av"], u - 2 + CREDIT)
                for n in range(2):
                    act.wait_ge(h["proj"], 6 * u + 5 + n)
                    act.activation(b_v[o][:, 8 * n:8 * n + 8, 0:D_B],
                                   bank[n][:, :].rearrange("p (s d) -> p s d", d=D_B), ACT.Copy).then_inc(h["q_out"], 1)

            def copy_y(p, o, u):
                act.wait_ge(h["av"], u + 1 + CREDIT)
                act.wait_ge(h["turned"], 4 * u + CREDIT)
                for n in range(3):
                    dst, src = y_bank(n, b_y)
                    act.activation(dst, src[:, :, 0:D_B], ACT.Copy).then_inc(h["y_out"], 1)

            def exponents(p, o, u):
                act.wait_ge(h["st"], u + 1)
                if not isinstance(u, int) or u >= 3:
                    act.wait_ge(h["av"], u - 2 + CREDIT)
                for j in range(4):
                    q = slice(32 * j, 32 * j + 32)
                    act.activation(b_wide[o][q, :, q], b_st[q, :].rearrange("p (s q) -> p s q", q=32), ACT.Exp)\
                       .then_inc(h["expd"], 1)

            attention(act, [(copy_qk, 1), (copy_v, 1), (copy_turned, -1), (exponents, 1), (copy_y, 0)])

        def b_dve(dve, chain):
            with dve.Fori(0, STEPS) as c:
                chain.enter(c, 4)
                chunk = x_tok[:, bass.ds(c * CHUNK, CHUNK)]
                norm(dve, chain, tiles_of(chunk), b_norm[0], b_norm[1], b_norm[2], c + LN_B,
                     lambda: dve.wait_ge(h["xt"], c + CREDIT)).then_inc(h["xn"], 1)
            chain.leave(STEPS)
            dve.wait_ge(h["x"], STEPS + CREDIT)
            chain(dve.memset(b_odd[:, COARSE:OCT], 0.0))
            chain(dve.memset(b_even[:, COARSE:OCT], 0.0))
            for level in range(1, LEVELS + 1):
                two = b_pool[level - 1].rearrange("p (n two) -> p n two", two=2)
                dve.tensor_tensor(b_pool[level], two[:, :, 0], two[:, :, 1], ALU.add).then_inc(h["pooled"], 1)
                dve.wait_ge(h["pooled"], level)
            dve.wait_ge(h["packed"], 1)
            for o in range(3):
                chain(dve.memset(b_wide[o], 0.0))
                chain(dve.memset(b_v[o][:, :, D_B:SLOT_Y], 1.0))
            dve.wait_ge(bias_in, 16)
            x3 = x_tok[:, :].rearrange("p (i c) -> p i c", c=C)
            dve.tensor_tensor(x3, x3, b_bias.unsqueeze(1).to_broadcast([P, TILES, C]), ALU.add).then_inc(h["ready"], 1)
            dve.wait_ge(h["ready"], 1)

            def soften(p, o, u):
                mask = constant("mask_causal" if o < 2 else "mask_block")
                s3 = b_s.rearrange("p (s k) -> p s k", k=32)
                dve.wait_ge(h["s_done"], u + 1 + CREDIT)
                if not isinstance(u, int) or u > 0:
                    dve.wait_ge(h["st"], u)
                dve.tensor_tensor(s3, bank[4][:, :].rearrange("p (s k) -> p s k", k=32),
                                  mask.unsqueeze(1).to_broadcast([P, 2 * SUB, 32]), ALU.add).then_inc(h["masked"], 1)
                dve.wait_ge(h["masked"], u + 1 + CREDIT)
                chain(dve.reduce_max(b_max, s3, AX))
                chain(dve.tensor_tensor(s3, s3, b_max.unsqueeze(2).to_broadcast([P, 2 * SUB, 32]), ALU.subtract))
                dve.wait_ge(h["expd"], 4 * u + CREDIT)
                dve.transpose(b_st, b_s).then_inc(h["st"], 1)

            def join(p, o, u):
                if o != 2:
                    return
                dve.wait_ge(h["turn_act"], 8 * p + 8 + CREDIT)
                for n in range(2):
                    for b in range(2):
                        dve.wait_ge(h["turned"], 4 * u + 2 * n + b + 1 + CREDIT)
                        for level in ([1], [2, 3, 4, 5])[b]:
                            span = 2 ** level
                            count = TOK // (2 * span)
                            at = FIRST_OF[level - 1] - 512 * b
                            dst = (b_yt, b_at)[n].rearrange("p (g c s) -> p g c s", c=32, s=span)[:, :, 16:32, span - 1]
                            src = bank[2 - 2 * n + b][:, at:at + count].rearrange("p (g c) -> p g c", c=16)
                            i = dve.tensor_tensor(dst, dst, src, ALU.add)
                            if level < LEVELS and level != 1:
                                chain(i)
                        i.then_inc(h["turn_dve"], 1)
                        dve.wait_ge(h["turn_dve"], 4 * p + 2 * n + b + 1 + CREDIT)
                chain(dve.tensor_scalar(b_at, b_at, 1e-8, None, ALU.add))
                chain(dve.reciprocal(b_at, b_at))
                dve.tensor_tensor(b_yt, b_yt, b_at, ALU.mult).then_inc(h["normed"], 1)

            def copy_sums(p, o, u):
                dve.wait_ge(h["turned"], 4 * u + CREDIT)
                for n in range(3):
                    dst, src = y_bank(n, b_sum)
                    dve.wait_ge(h["y_out"], 3 * u + n + 1 + CREDIT)
                    dve.tensor_copy(dst, src[:, :, D_B:SLOT_Y].to_broadcast(list(dst.shape))).then_inc(h["sum_out"], 1)

            def gather_out(p, o, u):
                if o != 2:
                    return
                for n in range(4):
                    dve.wait_ge(h["o"], 4 * p + n + 1 + CREDIT)
                    part = slice(n * 512, n * 512 + 512)
                    dve.tensor_tensor(x_tok[:, part], x_tok[:, part], bank[n][:, :], ALU.add).then_inc(h["acc"], 1)

            attention(dve, [(soften, 1), (join, -1), (copy_sums, 0), (gather_out, -1)], chain, 3 * 2 + 8)
            dve.wait_ge(h["acc"], 4 * PAIRS + CREDIT)

        def b_pool_engine(pool):
            with pool.Fori(0, STEPS) as c:
                norm_power(pool, c + LN_B)

        def b_sp(sp):
            def weights_in(p):
                sp.dma_start(b_w.rearrange("p (n c) -> p n c", c=P), w["w_qkv"][bass.ds(p, 1)].rearrange("a c n j -> (a c) n j"))\
                  .then_inc(w_in, 16)

            def out_weights_in(p):
                sp.dma_start(b_wo, w["w_out"][bass.ds(p, 1)].rearrange("a c j -> (a c) j")).then_inc(wo_in, 16)

            sp.wait_ge(h["xn"], 1)
            sp.dma_start(b_bias, w["b_out"].to_broadcast([P, C])).then_inc(bias_in, 16)
            weights_in(0)
            out_weights_in(0)
            with sp.Fori(1, PAIRS) as p:
                sp.wait_ge(h["proj"], 18 * p)
                weights_in(p)
                sp.wait_ge(h["o"], 4 * p + CREDIT)
                out_weights_in(p)
        final = sem("final")
        block = ctx.enter_context(nc.Block())
        loads = [(const[:, :], w["constants"][:, 0:CONST["pick"][0]]), (pick, w["constants"][:, CONST["pick"][0]:CONST_COLS]),
                 (vectors[:, :], w["vectors"]), (w1, w["maa_w1"]), (w2, w["maa_w2"]), (dw1, w["decay_w1"]),
                 (dw2[0:DECAY, :], w["decay_w2"]), (wrkvo, w["wrkvo"]), (gate_w[:, :], w["gate_w"]),
                 (shared_up[:, :], w["shared_up"]),
                 (shared_down[:, :].rearrange("p (f c) -> p f c", c=C), w["shared_down"].rearrange("(f p) c -> p f c", p=P))]
        LOADS = len(loads)
        EXPERT_LOADS = 8

        @block.sync
        def _(sp):
            for c in credited:
                sp.sem_inc(c, CREDIT)
            sp.dma_start(tiles_of(x_tok[:, :]), w["x"].rearrange("i p c -> p i c")).then_inc(loaded_x, 16)
            for dst, src in loads:
                sp.dma_start(dst, src).then_inc(loaded, 16)
            for i in range(EXPERT_LOADS):
                part = slice(i * EXPERTS * WROW // EXPERT_LOADS, (i + 1) * EXPERTS * WROW // EXPERT_LOADS)
                sp.dma_start(experts[:, part], w["experts"][:, part]).then_inc(loaded_experts, 16)
            sp.wait_ge(zero_row, 1)
            sp.dma_start(sorted_x.rearrange("(s p) c -> p s c", p=P), zeros[:, :].unsqueeze(1).to_broadcast([P, SLOTS, C]))\
              .then_inc(zeroed, 16)
            f_sp(sp, 0)
            b_sp(sp)
            f_sp(sp, 1)
            sp.wait_ge(final, 1)
            sp.dma_start(out.rearrange("i p c -> p i c"), tiles_of(x_tok[:, :])).then_inc(stored, 16)
            sp.wait_ge(stored, 16)

        @block.tensor
        def _(pe):
            a_pe(pe)
            f_pe(pe, 0)
            b_pe(pe)
            f_pe(pe, 1)

        @block.scalar
        def _(act):
            a_act(act)
            f_act(act, 0)
            b_act(act)
            f_act(act, 1)

        @block.gpsimd
        def _(pool):
            pool.memset(zeros[:, :], 0.0).then_inc(zero_row, 1)
            a_pool(pool)
            f_pool(pool, 0)
            b_pool_engine(pool)
            f_pool(pool, 1)

        @block.vector
        def _(dve):
            chain = a_dve(dve)
            f_dve(dve, chain, 0)
            b_dve(dve, chain)
            f_dve(dve, chain, 1)
            dve.memset(stat[:, 12:13], 0.0).then_inc(final, 1)


def _constants():
    import numpy as np

    c = np.zeros((P, CONST_COLS), np.float32)

    def put(name, value):
        at, width = CONST[name]
        c[:, at:at + width] = np.broadcast_to(value, (P, width))

    row = np.arange(P)
    put("ident", np.eye(P))
    put("head_ones", row[:, None] // N_A == row[None, :] // N_A)
    pick = np.zeros((P, N_A, P))
    for m in range(N_A):
        pick[:, m] = (row[:, None] // N_A == row[None, :] // N_A) & (row[None, :] % N_A == m)
    put("pick", pick.reshape(P, -1))
    put("later", row[:, None] < row[None, :])
    put("ones", 1.0)
    put("expert_rank", (32.0 - np.arange(32))[None])
    put("tile_reset", (np.arange(512) % 16 != 0)[None])
    put("slot_no", np.arange(float(SLOTS))[None])
    put("tile_start", (P * np.arange(float(TILES)))[None])
    q, k = row[:, None] % 32, np.arange(32)[None]
    put("mask_causal", np.where((q // 16 == k // 16) & (k <= q), 0.0, -1e30))
    put("mask_block", np.where(q // 16 == k // 16, 0.0, -1e30))
    put("half", -0.5)
    return c


def kernel(**inputs):
    import numpy as np
    import concourse.bacc as bacc
    from concourse.bass_utils import run_bass_kernel_spmd as run

    nc = bacc.Bacc("TRN2", target_bir_lowering=False, num_devices=1)
    a = {n.replace("L0_", ""): np.asarray(v) for n, v in inputs.items()}
    col = lambda v: np.ascontiguousarray(v.reshape(C, 1))
    laid = {
        "x": a["attn_a_x"].reshape(TILES, P, C),
        "vectors": np.concatenate([col(a["attn_a_" + n]) for n in (
            "time_maa_x", "time_maa_w", "time_maa_k", "time_maa_v", "time_maa_r",
            "time_decay", "time_faaaa", "ln_g", "ln_b")], 1),
        "b_out": a["attn_b_b_out"].reshape(1, C),
        "maa_w1": a["attn_a_maa_w1"],
        "maa_w2": a["attn_a_maa_w2"].reshape(4 * MIX, C),
        "decay_w1": a["attn_a_decay_w1"],
        "decay_w2": a["attn_a_decay_w2"],
        "wrkvo": np.concatenate([a["attn_a_" + n] for n in ("Wr", "Wk", "Wv", "Wo")], 1),
        "w_qkv": np.ascontiguousarray(
            a["attn_b_w_qkv"].reshape(3, PAIRS, P, C).transpose(1, 3, 0, 2)),
        "w_out": np.ascontiguousarray(a["attn_b_w_out"].reshape(C, PAIRS, P).transpose(1, 2, 0)),
        "gate_w": a["ffn_gate_w"],
        "shared_up": np.concatenate([a["ffn_shared_gate_w"], a["ffn_shared_up_w"]], 1),
        "shared_down": a["ffn_shared_down_w"],
        "experts": np.concatenate([
            a["ffn_routed_gate_w"].transpose(1, 0, 2), a["ffn_routed_up_w"].transpose(1, 0, 2),
            a["ffn_routed_down_w"].reshape(EXPERTS, INNER // P, P, C).transpose(2, 0, 1, 3).reshape(P, EXPERTS, -1),
        ], 2).reshape(P, EXPERTS * WROW),
        "constants": _constants(),
    }
    arrays, aps = {}, {}
    for name, v in laid.items():
        v = np.ascontiguousarray(v)
        arrays["in_" + name] = v
        aps[name] = nc.dram_tensor("in_" + name, v.shape, mybir.dt.from_np(v.dtype), kind="ExternalInput").ap()
    out = nc.dram_tensor("out_0", (TILES, P, C), F32, kind="ExternalOutput").ap()
    hybrid_block(nc, aps, out)
    r = run(nc, [arrays], core_ids=[0])
    return r.results[0]["out_0"].reshape(BATCH, SEQ, C)
```

```python
from contextlib import ExitStack

import concourse.bass as bass
from concourse import mybir

F32 = mybir.dt.float32
BF16 = mybir.dt.bfloat16
I32 = mybir.dt.int32
U32 = mybir.dt.uint32
ALU = mybir.AluOpType
ACT = mybir.ActivationFunctionType
AX = mybir.AxisListType.X

P = 128
C = 128
BATCH = 2
SEQ = 1024
TOK = BATCH * SEQ
TILES = TOK // P
CHUNK = 512
CT = CHUNK // P
STEPS = TOK // CHUNK
HALVES = SEQ // CHUNK
EPS = 1e-5
ARENA = 24000
CREDIT = 1

HEADS_A = 16
N_A = C // HEADS_A
DECAY = 64
MIX = 32

HEADS_B = 16
D_B = 64
PAIRS = HEADS_B * D_B // P
LEVELS = 5
COARSE = sum(TOK // 2 ** (l + 1) for l in range(1, LEVELS + 1))
OCT = 1024
SUB = OCT // P


EXPERTS = 32
INNER = 256
WROW = 2 * INNER + INNER // P * C
SLOTS = 48
assert SLOTS >= TOK // P + EXPERTS - 1 and SLOTS % 4 == 0

CONST = {}
_at = 0
for _n, _w in [("ident", P), ("head_ones", P), ("later", P), ("expert_rank", EXPERTS),
               ("tile_reset", EXPERTS * TILES), ("slot_no", SLOTS), ("tile_start", TILES),
               ("mask_causal", 32), ("mask_block", 32), ("half", TILES), ("pick", N_A * P)]:
    CONST[_n] = (_at, _w)
    _at += _w
CONST_COLS = _at


class Chain:

    def __init__(self, eng, sem):
        self.eng, self.sem, self.n, self.moving = eng, sem, 0, 0

    def __call__(self, ins):
        ins.then_inc(self.sem, 1)
        self.n += 1
        self.eng.wait_ge(self.sem, self.moving + self.n)

    def enter(self, i, per):
        self.moving, self.start, self.per = i * per, self.n, per

    def leave(self, times):
        assert self.n - self.start == self.per, (self.n - self.start, self.per)
        self.moving, self.n = 0, self.start + self.per * times


def hybrid_block(nc, w, out):
    with ExitStack() as ctx:
        sem_cache = {}

        def sb(name, shape, dt=F32):
            return ctx.enter_context(nc.sbuf_tensor(name, shape, dt))

        def sem(name):
            return ctx.enter_context(nc.semaphore(name))

        psum = ctx.enter_context(nc.psum_tensor("psum", [P, 8 * 512], F32))
        bank = [psum[:, i * 512:i * 512 + 512] for i in range(8)]

        experts = sb("experts", [P, EXPERTS * WROW])
        x_tok = sb("x_tok", [P, TOK])
        const = sb("const", [P, CONST["pick"][0]])
        vectors = sb("vectors", [P, 9])
        gate_w = sb("gate_w", [P, EXPERTS])
        shared_up = sb("shared_up", [P, 2 * INNER])
        shared_down = sb("shared_down", [P, INNER // P * C])
        zeros = sb("zeros", [P, C])
        exact_bf = sb("exact_bf", [P, 2 * P], BF16)
        ones_bf, later_bf = exact_bf[:, 0:P], exact_bf[:, P:2 * P]
        stat = sb("stat", [P, 4 * CT])
        arena = sb("arena", [P, ARENA])

        used = [0]

        def carve(n):
            at = used[0]
            used[0] += n
            assert used[0] <= ARENA, used[0]
            return arena[:, at:at + n]

        def constant(name):
            at, width = CONST[name]
            return const[:, at:at + width]

        ident = constant("ident")
        (maa_x, maa_w, maa_k, maa_v, maa_r, t_decay, faaaa, ln_g, ln_b) = (vectors[:, i:i + 1] for i in range(9))

        sorted_x = nc.dram_tensor("sorted_x", (SLOTS * P, C), F32, kind="Internal").ap()
        sorted_y = nc.dram_tensor("sorted_y", (SLOTS * P, C), F32, kind="Internal").ap()

        loaded, loaded_x, loaded_experts = sem("loaded"), sem("loaded_x"), sem("loaded_experts")
        zero_row, zeroed, stored = sem("zero_row"), sem("zeroed"), sem("stored")
        dve_chain, act_chain, pool_chain = sem("dve_chain"), sem("act_chain"), sem("pool_chain")

        ln_var, ln_rstd = sem("ln_var"), sem("ln_rstd")
        ln_count = {"dve": 0, "pool": 0}

        def tiles_of(ap):
            return ap.rearrange("p (a b) -> p a b", b=C)

        def over(col):
            return col.unsqueeze(2).to_broadcast([P, CT, C])

        mean, var, rstd = (stat[:, CT * i:CT * i + CT] for i in range(3))

        def norm(dve, chain, src, centred, square, target, n, free=None):
            chain(dve.reduce_sum(mean, src, AX))
            chain(dve.scalar_tensor_tensor(tiles_of(centred), over(mean), -1.0 / C, src, ALU.mult, ALU.add))
            chain(dve.tensor_tensor(square, centred, centred, ALU.mult))
            chain(dve.reduce_sum(var, tiles_of(square), AX))
            dve.tensor_scalar(var, var, 1.0 / C, EPS, ALU.mult, ALU.add).then_inc(ln_var, 1)
            dve.wait_ge(ln_rstd, n + 1)
            if free is not None:
                free()
            return dve.tensor_tensor(tiles_of(target), tiles_of(centred), over(rstd), ALU.mult)

        def norm_power(pool, n):
            pool.wait_ge(ln_var, n + 1)
            pool.tensor_tensor(rstd, var, constant("half")[:, 0:CT], ALU.pow).then_inc(ln_rstd, 1)

        w1 = carve(4 * MIX)
        w2 = carve(C)
        dw1 = carve(DECAY)
        dw2 = carve(C)
        dw2_mean = carve(C)
        wrkvo = carve(4 * C)
        wv_wide = carve(N_A * C)
        pick = carve(N_A * P)
        a_decay = carve(2)
        a_norm = [carve(CHUNK) for _ in range(3)]
        a_x = [carve(CHUNK + 1) for _ in range(2)]
        a_xx, a_xxx, a_mix = carve(CHUNK), carve(CHUNK), carve(CHUNK)
        a_in = [carve(CHUNK) for _ in range(4)]
        a_th, a_d = carve(CHUNK), carve(CHUNK)
        a_k, a_v, a_r = carve(CHUNK), carve(CHUNK), carve(CHUNK)
        a_kv = [carve(CHUNK) for _ in range(2)]
        a_state = carve(N_A * (CHUNK + 1)).rearrange("p (m t) -> p m t", m=N_A)
        a_g = [carve(CHUNK) for _ in range(2)]
        a_ruk, a_diag = carve(CHUNK), carve(CHUNK)
        a_y, a_ynt = carve(CHUNK), carve(CHUNK)
        used_a = used[0]

        s = {n: sem("a_" + n) for n in (
            "weights xn xt xs xxx mix_in mix wf tf xf decay_in th dlog d proj rkv rowed kv bank_free state g y_done "
            "ruk diag_in diag dv y yt y2 yn_t yn_copied o x1 carry decay_mean").split()}

        XT_BANK, MISC, ROT, YB, OB = bank[0], bank[1], bank[2:6], bank[6], bank[7]

        credited = [s[n] for n in "diag kv xf o y_done yn_t rowed g diag_in state".split()]

        def a_steps(eng, chain=None, per=0):
            with eng.Fori(0, BATCH) as b:
                if chain:
                    chain.enter(b, per)
                for half in range(HALVES):
                    yield b * HALVES + half, half
            if chain:
                chain.leave(BATCH)

        def a_pe(pe):
            pe.wait_ge(s["weights"], 1)
            pe.wait_ge(loaded, LOADS * 16)
            pe.matmul(MISC[:, 0:1], constant("head_ones"), t_decay, start=True, stop=True).then_inc(s["decay_in"], 1)
            for g, half in a_steps(pe):
                pe.wait_ge(s["xn"], 2 * g + 1)
                for t in range(CT):
                    i = pe.transpose(XT_BANK[:, t * P:t * P + P], a_norm[2][:, t * C:t * C + C], ident)
                i.then_inc(s["xt"], 1)
                pe.wait_ge(s["xxx"], g + 1)
                if half == 0:
                    pe.wait_ge(s["decay_mean"], 1)
                pe.wait_ge(s["diag"], g + CREDIT)
                pe.matmul(MISC[:, :], w1, a_xxx, start=True, stop=True).then_inc(s["mix_in"], 1)
                pe.wait_ge(s["mix"], g + 1)
                pe.wait_ge(s["kv"], N_A * g + CREDIT)
                for f in range(4):
                    pe.matmul(ROT[f][:, :], w2[f * MIX:f * MIX + MIX, :], a_mix[f * MIX:f * MIX + MIX, :],
                              start=True, stop=True).then_inc(s["wf"], 1)
                pe.wait_ge(s["xf"], 4 * g + 1 + CREDIT)
                pe.matmul(MISC[0:DECAY, :], dw1, a_in[0], start=True, stop=True).then_inc(s["decay_in"], 1)
                for f, at in ((1, 1), (2, 2), (3, 0)):
                    pe.wait_ge(s["xf"], 4 * g + f + 1 + CREDIT)
                    pe.matmul(ROT[f][:, :], wrkvo[:, at * C:at * C + C], a_in[f],
                              start=True, stop=True).then_inc(s["proj"], 1)
                pe.wait_ge(s["th"], g + 1)
                pe.matmul(MISC[:, :], dw2_mean[0:DECAY, :], a_th[0:DECAY, :], start=True, stop=True)\
                  .then_inc(s["dlog"], 1)
                for m in range(N_A + 2):
                    if m < N_A:
                        if 1 <= m < 4:
                            pe.wait_ge(s["rkv"], 3 * g + m)
                        if m >= 4:
                            pe.wait_ge(s["kv"], N_A * g + m - 3 + CREDIT)
                        pe.matmul(ROT[m % 4][:, :], wv_wide[:, m * C:m * C + C], a_in[2],
                                  start=True, stop=True).then_inc(s["rowed"], 1)
                    if m == 2:
                        pe.wait_ge(s["d"], g + 1)
                        pe.wait_ge(s["ruk"], g + 1)
                        pe.matmul(MISC[:, :], constant("head_ones"), a_ruk, start=True, stop=True)\
                          .then_inc(s["diag_in"], 1)
                    if m >= 2:
                        q = m - 2
                        pe.wait_ge(s["g"], N_A * g + q + 1 + CREDIT)
                        i = pe.matmul(YB[:, :], pick[:, q * P:q * P + P], a_g[q % 2],
                                      start=(q == 0), stop=(q == N_A - 1))
                        i.then_inc(s["y_done"], 1)
                pe.wait_ge(s["y"], g + 1)
                for t in range(CT):
                    i = pe.transpose(XT_BANK[:, t * P:t * P + P], a_y[:, t * P:t * P + P], ident)
                i.then_inc(s["yt"], 1)
                pe.wait_ge(s["xn"], 2 * g + 2)
                for t in range(CT):
                    i = pe.transpose(XT_BANK[:, t * P:t * P + P], a_norm[2][:, t * C:t * C + C], ident)
                i.then_inc(s["yn_t"], 1)
                pe.wait_ge(s["yn_copied"], g + 1)
                for t in range(CT):
                    i = pe.matmul(OB[:, t * C:t * C + C], a_ynt[:, t * P:t * P + P], wrkvo[:, 3 * C:4 * C],
                                  start=True, stop=True)
                i.then_inc(s["o"], 1)

        def a_act(act):
            chain = Chain(act, act_chain)
            act.wait_ge(s["decay_in"], 1)
            act.activation(a_decay[:, 0:1], MISC[:, 0:1], ACT.Copy, scale=1.0 / N_A).then_inc(s["decay_mean"], 1)
            act.wait_ge(s["decay_mean"], 1)
            act.wait_ge(s["weights"], 1)
            for g, half in a_steps(act, chain, 2):
                act.wait_ge(s["xt"], g + 1)
                act.wait_ge(s["xf"], 4 * g + CREDIT)
                if half:
                    act.wait_ge(s["xs"], g)
                    act.activation(a_x[1][:, 0:1], a_x[0][:, CHUNK:CHUNK + 1], ACT.Copy)
                act.activation(a_x[half][:, 1:CHUNK + 1], XT_BANK[:, :], ACT.Copy).then_inc(s["xs"], 1)
                act.wait_ge(s["mix_in"], g + 1)
                act.activation(a_mix, MISC[:, :], ACT.Tanh).then_inc(s["mix"], 1)
                act.wait_ge(s["decay_in"], g + 2)
                act.activation(a_th[0:DECAY, :], MISC[0:DECAY, :], ACT.Tanh).then_inc(s["th"], 1)
                for n, dst in ((1, a_k), (2, a_v), (3, a_r)):
                    act.wait_ge(s["proj"], 3 * g + n)
                    act.activation(dst, ROT[n][:, :], ACT.Copy).then_inc(s["rkv"], 1)
                act.wait_ge(s["dlog"], g + 1)
                chain(act.activation(a_d, MISC[:, :], ACT.Exp, bias=a_decay[:, 0:1]))
                act.activation(a_d, a_d, ACT.Exp, scale=-1.0).then_inc(s["d"], 1)
                act.wait_ge(s["diag_in"], g + 1 + CREDIT)
                act.activation(a_diag, MISC[:, :], ACT.Copy).then_inc(s["diag"], 1)
                act.wait_ge(s["yn_t"], g + 1 + CREDIT)
                act.wait_ge(s["o"], g + CREDIT)
                act.activation(a_ynt, XT_BANK[:, :], ACT.Identity, scale=ln_g, bias=ln_b)\
                   .then_inc(s["yn_copied"], 1)

        def a_pool(pool):
            for g, half in a_steps(pool):
                norm_power(pool, 2 * g)
                x = a_x[half][:, 1:CHUNK + 1]
                for f in range(4):
                    pool.wait_ge(s["tf"], 4 * g + f + 1)
                    pool.tensor_tensor(a_in[f], a_in[f], x, ALU.add).then_inc(s["xf"], 1)
                pool.wait_ge(s["rkv"], 3 * g + 3)
                for m in range(N_A):
                    pool.wait_ge(s["state"], N_A * g + m + 1 + CREDIT)
                    if m >= 2:
                        pool.wait_ge(s["y_done"], N_A * g + m - 1 + CREDIT)
                    if m < 2:
                        pool.wait_ge(s["y_done"], N_A * g + CREDIT)
                    pool.tensor_tensor(a_g[m % 2], a_r, a_state[:, m, 0:CHUNK], ALU.mult).then_inc(s["g"], 1)
                    if m == 3:
                        pool.wait_ge(s["diag"], g + 1 + CREDIT)
                        pool.tensor_tensor(a_diag, a_diag, a_v, ALU.mult).then_inc(s["dv"], 1)
                norm_power(pool, 2 * g + 1)

        def a_dve(dve):
            chain = Chain(dve, dve_chain)
            dve.wait_ge(loaded, LOADS * 16)
            chain(dve.memset(a_x[0][:, 0:1], 0.0))
            chain(dve.reduce_sum(dw2_mean[0:DECAY, 0:HEADS_A],
                                 dw2[0:DECAY, :].rearrange("p (h n) -> p h n", n=N_A), AX))
            chain(dve.tensor_scalar(dw2[0:DECAY, :].rearrange("p (h n) -> p h n", n=N_A),
                                    dw2_mean[0:DECAY, 0:HEADS_A].unsqueeze(2).to_broadcast([DECAY, HEADS_A, N_A]),
                                    1.0 / N_A, None, ALU.mult))
            chain(dve.tensor_copy(dw2_mean[0:DECAY, :], dw2[0:DECAY, :]))
            for m in range(N_A):
                i = dve.tensor_copy(
                    wv_wide[:, m * C:m * C + C].rearrange("p (h n) -> p h n", n=N_A),
                    wrkvo[:, 2 * C + m:3 * C:N_A].unsqueeze(2).to_broadcast([P, HEADS_A, N_A]))
                if m < N_A - 1:
                    chain(i)
            i.then_inc(s["weights"], 1)
            dve.wait_ge(loaded_x, 16)
            for g, half in a_steps(dve, chain, 2 * 11):
                chunk = x_tok[:, bass.ds(g * CHUNK, CHUNK)]
                norm(dve, chain, tiles_of(chunk), a_norm[0], a_norm[1], a_norm[2], 2 * g,
                     lambda: dve.wait_ge(s["yn_t"], g + CREDIT)).then_inc(s["xn"], 1)
                dve.wait_ge(s["xs"], g + 1)
                x = a_x[half][:, 1:CHUNK + 1]
                chain(dve.tensor_tensor(a_xx, a_x[half][:, 0:CHUNK], x, ALU.subtract))
                dve.scalar_tensor_tensor(a_xxx, a_xx, maa_x, x, ALU.mult, ALU.add).then_inc(s["xxx"], 1)
                for f, maa in enumerate((maa_w, maa_k, maa_v, maa_r)):
                    dve.wait_ge(s["wf"], 4 * g + f + 1)
                    if f == 2:
                        dve.wait_ge(s["rowed"], N_A * g + CREDIT)
                    dve.scalar_tensor_tensor(a_in[f], ROT[f][:, :], maa, a_xx, ALU.add, ALU.mult)\
                       .then_inc(s["tf"], 1)
                if half == 0:
                    chain(dve.memset(a_state[:, :, 0], 0.0))
                else:
                    dve.wait_ge(s["g"], N_A * g + CREDIT)
                    chain(dve.tensor_copy(a_state[:, :, 0], a_state[:, :, CHUNK]))
                dve.wait_ge(s["rkv"], 3 * g + 3)
                for m in range(N_A + 1):
                    if m < N_A:
                        dve.wait_ge(s["rowed"], N_A * g + m + 1 + CREDIT)
                        if m >= 2:
                            dve.wait_ge(s["state"], N_A * g + m - 1 + CREDIT)
                        dve.tensor_tensor(a_kv[m % 2], a_k, ROT[m % 4][:, :], ALU.mult).then_inc(s["kv"], 1)
                    if m == 1:
                        dve.wait_ge(s["diag_in"], g + CREDIT)
                        dve.scalar_tensor_tensor(a_ruk, a_r, faaaa, a_k, ALU.mult, ALU.mult).then_inc(s["ruk"], 1)
                    if m >= 1:
                        q = m - 1
                        if q == 0:
                            dve.wait_ge(s["d"], g + 1)
                        if q > 0:
                            dve.wait_ge(s["state"], N_A * g + q + CREDIT)
                        dve.wait_ge(s["kv"], N_A * g + q + 1 + CREDIT)
                        dve.tensor_tensor_scan(a_state[:, q, 1:CHUNK + 1], a_d, a_kv[q % 2], a_state[:, q, 0:1],
                                               ALU.mult, ALU.add).then_inc(s["state"], 1)
                dve.wait_ge(s["y_done"], N_A * g + N_A + CREDIT)
                dve.wait_ge(s["dv"], g + 1)
                dve.tensor_tensor(a_y, YB[:, :], a_diag, ALU.add).then_inc(s["y"], 1)
                dve.wait_ge(s["yt"], g + 1)
                norm(dve, chain, tiles_of(XT_BANK[:, :]), a_norm[0], a_norm[1], a_norm[2], 2 * g + 1)\
                    .then_inc(s["xn"], 1)
                dve.wait_ge(s["o"], g + 1 + CREDIT)
                chain(dve.tensor_tensor(chunk, chunk, OB[:, :], ALU.add))
            return chain

        used[0] = 0
        f_norm = [carve(CHUNK) for _ in range(3)]
        f_xt = carve(CHUNK)
        f_xt_all = carve(TOK)
        f_gated = [carve(CHUNK) for _ in range(2)]
        f_h = [carve(CHUNK) for _ in range(2)]
        f_xs = carve(TOK)
        f_one_hot = sb("one_hot", [P, EXPERTS * TILES], BF16)
        f_best = carve(TILES)
        f_score = carve(TILES)
        f_pick = [carve(CT * EXPERTS) for _ in range(2)]
        f_upto, f_ends, f_place = (carve(EXPERTS * TILES) for _ in range(3))
        f_tiles, f_first, f_upto_slot, f_ones = (carve(EXPERTS) for _ in range(4))
        f_slot_cmp = carve(SLOTS * EXPERTS)
        f_slot_row, f_place_row = carve(SLOTS), carve(TILES)
        f_slot_at, f_row = sb("slot_at", [P, SLOTS], I32), sb("row", [P, TILES], U32)
        f_gx = [carve(C) for _ in range(4)]
        f_gxt = [carve(P) for _ in range(2)]
        f_sg = [carve(INNER) for _ in range(2)]
        f_sh = [carve(INNER) for _ in range(2)]
        f_sht = [carve(INNER) for _ in range(2)]
        f_gy = [carve(C) for _ in range(4)]
        f_back = carve(TOK)
        LN_F = [2 * STEPS, 2 * STEPS + STEPS + STEPS]
        LN_B = 2 * STEPS + STEPS

        t = {n: sem("f_" + n) for n in (
            "xn xt xt_copied xs logits shared gated h down best scored rank counts placed rows "
            "scaled gx_t gxt gu sg sh sh_t sht y y_copied gathered").split()}
        scattered, slot_in = sem("f_scattered"), [sem(f"f_slot_in{j}") for j in range(4)]
        slot_out = [sem(f"f_slot_out{j}") for j in range(4)]
        credited += [t[n] for n in "down y xt xt_copied xs gated h scored gx_t gxt gu sg sh sh_t sht y_copied".split()]
        credited += slot_out

        def chunks(eng, stages, last=None, chain=None, per=0):
            first = -min(d for _, d in stages + [(None, 0)])
            end = STEPS - 1 - (last is not None)

            def step(c, stages):
                for stage, d in stages:
                    if not isinstance(c, int) or c + d >= 0:
                        stage(c + d)

            for c in range(-1, first):
                step(c, stages)
            with eng.Fori(first, end) as c:
                if chain:
                    chain.enter(c - first, per)
                step(c, stages)
            if chain:
                chain.leave(end - first)
            if last:
                step(end, last)

        def f_pe(pe, k):
            def turn(c):
                g = c + STEPS * k
                pe.wait_ge(t["xn"], g + 1)
                pe.wait_ge(t["xt_copied"], g + CREDIT)
                for i in range(CT):
                    mm = pe.transpose(bank[0][:, i * P:i * P + P], f_norm[2][:, i * C:i * C + C], ident)
                mm.then_inc(t["xt"], 1)

            def logits(c):
                g = c + STEPS * k
                pe.wait_ge(t["xt_copied"], g + 1 + CREDIT)
                if not isinstance(g, int) or c > 0:
                    pe.wait_ge(t["best"], g)
                for i in range(CT):
                    mm = pe.matmul(bank[1][:, i * EXPERTS:i * EXPERTS + EXPERTS], f_xt[:, i * P:i * P + P], gate_w[:, :],
                                   start=True, stop=True)
                mm.then_inc(t["logits"], 1)

            def shared_in(c):
                g = c + STEPS * k
                pe.wait_ge(t["h"], 2 * g + CREDIT)
                for n in (0, 2, 1, 3):
                    pe.matmul(bank[2 + n][:, :], shared_up[:, n * P:n * P + P], f_xt_all[:, bass.ds(c * CHUNK, CHUNK)],
                              start=True, stop=True).then_inc(t["shared"], 1)

            def shared_out(c):
                g = c + STEPS * k
                pe.wait_ge(t["h"], 2 * g + 2 + CREDIT)
                pe.wait_ge(t["down"], g + CREDIT)
                for i in range(CT):
                    for half in range(2):
                        mm = pe.matmul(bank[6][:, i * C:i * C + C], f_h[half][:, i * P:i * P + P],
                                       shared_down[:, half * C:half * C + C], start=(half == 0), stop=(half == 1))
                mm.then_inc(t["y"], 1)

            chunks(pe, [(shared_in, 0), (turn, 1), (logits, 1), (shared_out, 0)],
                   last=[(shared_in, 0), (turn, 1), (logits, 1)])
            pe.wait_ge(t["best"], STEPS * (k + 1))
            pe.wait_ge(zero_row, 2)
            pe.matmul(bank[1][:, :], ones_bf, f_one_hot[:, :], start=True, stop=True).then_inc(t["counts"], 1)
            pe.matmul(bank[0][:, :], later_bf, f_one_hot[:, :], start=True, stop=True).then_inc(t["rank"], 1)
            shared_out(STEPS - 2)
            shared_in(STEPS - 1)
            shared_out(STEPS - 1)
            pe.wait_ge(t["rows"], k + 1)
            pe.wait_ge(t["down"], STEPS * (k + 1) + CREDIT)

            def weights(s, at, size):
                first = pe.value_load(f_slot_at[0:1, bass.ds(s, 1)], min_val=0, max_val=(EXPERTS - 1) * WROW)
                return experts[:, bass.ds(first + at, size)]

            def turn_in(s, j):
                n = SLOTS * k + s
                pe.wait_ge(slot_in[j], 16 * (SLOTS // 4 * k + 1) + 4 * (s - j))
                pe.wait_ge(t["gxt"], n - 1 + CREDIT)
                pe.transpose(bank[j % 2][:, 0:P], f_gx[j], ident).then_inc(t["gx_t"], 1)

            def gate_up(s, j):
                n = SLOTS * k + s
                w_up = weights(s, 0, 2 * INNER)
                pe.wait_ge(t["gxt"], n + 1 + CREDIT)
                pe.wait_ge(t["sh"], n - 1 + CREDIT)
                pe.matmul(bank[2 + j % 2][:, :], f_gxt[j % 2], w_up, start=True, stop=True)\
                  .then_inc(t["gu"], 1)

            def turn_h(s, j):
                n = SLOTS * k + s
                pe.wait_ge(t["sh"], n + 1 + CREDIT)
                pe.wait_ge(t["sht"], n - 1 + CREDIT)
                for half in range(2):
                    mm = pe.transpose(bank[4 + j % 2][:, half * P:half * P + P], f_sh[j % 2][:, half * P:half * P + P], ident)
                mm.then_inc(t["sh_t"], 1)

            def down(s, j):
                n = SLOTS * k + s
                w_down = weights(s, 2 * INNER, 2 * C)
                pe.wait_ge(t["sht"], n + 1 + CREDIT)
                pe.wait_ge(t["y_copied"], n - 1 + CREDIT)
                for half in range(2):
                    mm = pe.matmul(bank[6 + j % 2][:, 0:C], f_sht[j % 2][:, half * P:half * P + P],
                                   w_down[:, half * C:half * C + C], start=(half == 0), stop=(half == 1))
                mm.then_inc(t["y"], 1)

            pe.wait_ge(loaded_experts, 16 * EXPERT_LOADS)
            slots(pe, [(turn_in, 1), (gate_up, 0), (down, -2), (turn_h, -1)])

        def slots(eng, stages):
            lead = max(d for _, d in stages)
            lag = min(d for _, d in stages)
            first = 4
            last = SLOTS - 4

            def step(s, j):
                for stage, d in stages:
                    if isinstance(s, int) and not 0 <= s + d < SLOTS:
                        continue
                    stage(s + d, (j + d) % 4)

            for s in range(-lead, first):
                step(s, s % 4)
            with eng.Fori(first // 4, last // 4) as i:
                for j in range(4):
                    step(i * 4 + j, j)
            for s in range(last, SLOTS - lag):
                step(s, s % 4)

        def f_act(act, k):
            def copy_x(c):
                g = c + STEPS * k
                act.wait_ge(t["xt"], g + 1 + CREDIT)
                if not isinstance(g, int) or g > 0:
                    act.wait_ge(t["logits"], g)
                act.activation(f_xt, bank[0][:, :], ACT.Copy)
                act.activation(f_xt_all[:, bass.ds(c * CHUNK, CHUNK)], bank[0][:, :], ACT.Copy).then_inc(t["xt_copied"], 1)

            def gate_shared(c):
                g = c + STEPS * k
                for n in range(2):
                    act.wait_ge(t["shared"], 4 * g + 2 * n + 1)
                    act.wait_ge(t["h"], 2 * g + CREDIT)
                    act.activation(f_gated[n], bank[2 + n][:, :], ACT.Silu).then_inc(t["gated"], 1)

            chunks(act, [(gate_shared, 0), (copy_x, 1)])
            act.wait_ge(t["best"], STEPS * (k + 1))
            act.activation(f_score, f_best, ACT.Sigmoid).then_inc(t["scored"], 1)
            gate_shared(STEPS - 1)

            def copy_in(s, j):
                n = SLOTS * k + s
                act.wait_ge(t["gx_t"], n + 1 + CREDIT)
                act.wait_ge(t["gu"], n - 1 + CREDIT)
                act.activation(f_gxt[j % 2], bank[j % 2][:, 0:P], ACT.Copy).then_inc(t["gxt"], 1)

            def gate(s, j):
                n = SLOTS * k + s
                act.wait_ge(t["gu"], n + 1 + CREDIT)
                act.wait_ge(t["sh"], n - 1 + CREDIT)
                act.activation(f_sg[j % 2], bank[2 + j % 2][:, 0:INNER], ACT.Silu).then_inc(t["sg"], 1)

            def copy_y(s, j):
                n = SLOTS * k + s
                act.wait_ge(t["y"], STEPS * (k + 1) + n + 1 + CREDIT)
                act.wait_ge(slot_out[j], 16 * (SLOTS // 4) * k + 4 * (s - j) + CREDIT)
                act.activation(f_gy[j], bank[6 + j % 2][:, 0:C], ACT.Copy).then_inc(t["y_copied"], 1)

            slots(act, [(copy_in, 1), (gate, 0), (copy_y, -2)])

        def f_dve(dve, chain, k):
            def norm_chunk(c):
                g = c + STEPS * k

                def free():
                    dve.wait_ge(t["xt"], g + CREDIT)
                    dve.wait_ge(t["xs"], g + CREDIT)

                chunk = x_tok[:, bass.ds(c * CHUNK, CHUNK)]
                norm(dve, chain, tiles_of(chunk), f_norm[0], f_norm[1], f_norm[2], c + LN_F[k], free).then_inc(t["xn"], 1)

            def route(c):
                g = c + STEPS * k
                dve.wait_ge(t["logits"], g + 1)
                logit = bank[1][:, 0:CT * EXPERTS].rearrange("p (i e) -> p i e", e=EXPERTS)
                best = f_best[:, bass.ds(c * CT, CT)]
                chain(dve.reduce_max(best, logit, AX))
                wide = lambda a: a.unsqueeze(2).to_broadcast([P, CT, EXPERTS])
                is_best, key = (a.rearrange("p (i e) -> p i e", e=EXPERTS) for a in f_pick)
                falling = constant("expert_rank").unsqueeze(1).to_broadcast([P, CT, EXPERTS])
                chain(dve.tensor_tensor(is_best, logit, wide(best), ALU.is_ge))
                chain(dve.tensor_tensor(key, is_best, falling, ALU.mult))
                chain(dve.reduce_max(stat[:, 3 * CT:4 * CT], key, AX))
                dve.tensor_tensor(
                    f_one_hot[:, :].rearrange("p (e i) -> p i e", e=EXPERTS)[:, bass.ds(c * CT, CT), :],
                    falling, wide(stat[:, 3 * CT:4 * CT]), ALU.is_equal).then_inc(t["best"], 1)
                dve.wait_ge(t["best"], g + 1)

            def product_shared(c):
                g = c + STEPS * k
                dve.wait_ge(t["y"], g + SLOTS * k + CREDIT)
                for n in range(2):
                    dve.wait_ge(t["shared"], 4 * g + 2 * n + 2)
                    dve.wait_ge(t["gated"], 2 * g + n + 1 + CREDIT)
                    dve.tensor_tensor(f_h[n], f_gated[n], bank[4 + n][:, :], ALU.mult).then_inc(t["h"], 1)

            def add_shared(c):
                g = c + STEPS * k
                chunk = x_tok[:, bass.ds(c * CHUNK, CHUNK)]
                dve.wait_ge(t["y"], g + SLOTS * k + 1 + CREDIT)
                dve.tensor_tensor(chunk, chunk, bank[6][:, :], ALU.add).then_inc(t["down"], 1)

            chunks(dve, [(norm_chunk, 1), (add_shared, -1), (product_shared, 0), (route, 1)], chain=chain, per=8)
            by = lambda a: a.rearrange("p (e i) -> p e i", e=EXPERTS)
            spread = lambda a: a.unsqueeze(2).to_broadcast([P, EXPERTS, TILES])
            chain(dve.memset(f_ones, 1.0))
            dve.wait_ge(t["counts"], k + 1)
            chain(dve.tensor_tensor_scan(f_upto, constant("tile_reset"), bank[1][:, :], 0.0, ALU.mult, ALU.add))
            starts = constant("tile_start").unsqueeze(1).to_broadcast([P, EXPERTS, TILES])
            chain(dve.tensor_tensor(by(f_ends), spread(by(f_upto)[:, :, TILES - 1]), starts, ALU.is_gt))
            chain(dve.reduce_sum(f_tiles, by(f_ends), AX))
            chain(dve.tensor_tensor_scan(f_upto_slot, f_ones, f_tiles, 0.0, ALU.mult, ALU.add))
            chain(dve.tensor_tensor(f_first, f_upto_slot, f_tiles, ALU.subtract))
            chain(dve.tensor_scalar(f_first, f_first, float(P), None, ALU.mult))
            dve.wait_ge(t["rank"], k + 1)
            chain(dve.tensor_tensor(f_place, f_upto, bank[0][:, :], ALU.add))
            chain(dve.tensor_tensor(by(f_place), by(f_place), spread(f_first), ALU.add))
            chain(dve.tensor_tensor(f_place, f_place, f_one_hot[:, :], ALU.mult))
            chain(dve.reduce_sum(f_place_row, f_place.rearrange("p (e i) -> p i e", e=EXPERTS), AX))
            dve.tensor_copy(f_row[:, :], f_place_row).then_inc(t["placed"], 1)
            by_slot = f_slot_cmp.rearrange("p (s e) -> p s e", e=EXPERTS)
            chain(dve.tensor_tensor(by_slot, f_upto_slot.unsqueeze(1).to_broadcast([P, SLOTS, EXPERTS]),
                                    constant("slot_no").unsqueeze(2).to_broadcast([P, SLOTS, EXPERTS]), ALU.is_le))
            chain(dve.reduce_sum(f_slot_row, by_slot, AX))
            chain(dve.tensor_scalar(f_slot_row, f_slot_row, EXPERTS - 1.0, float(WROW), ALU.min, ALU.mult))
            dve.tensor_copy(f_slot_at[:, :], f_slot_row).then_inc(t["rows"], 1)
            add_shared(STEPS - 2)
            product_shared(STEPS - 1)
            add_shared(STEPS - 1)

            def product(s, j):
                n = SLOTS * k + s
                dve.wait_ge(t["sg"], n + 1 + CREDIT)
                dve.wait_ge(t["sh_t"], n - 1 + CREDIT)
                dve.tensor_tensor(f_sh[j % 2], f_sg[j % 2], bank[2 + j % 2][:, INNER:2 * INNER], ALU.mult)\
                   .then_inc(t["sh"], 1)

            def copy_h(s, j):
                n = SLOTS * k + s
                dve.wait_ge(t["sh_t"], n + 1 + CREDIT)
                dve.wait_ge(t["y"], STEPS * (k + 1) + n - 1 + CREDIT)
                dve.tensor_copy(f_sht[j % 2], bank[4 + j % 2][:, 0:INNER]).then_inc(t["sht"], 1)

            slots(dve, [(copy_h, -1), (product, 0)])
            dve.wait_ge(t["down"], STEPS * (k + 1) + CREDIT)
            for i in range(CT):
                dve.wait_ge(t["gathered"], 16 * (TILES * k + TILES))
                part = slice(i * CHUNK, i * CHUNK + CHUNK)
                chain(dve.tensor_tensor(x_tok[:, part], x_tok[:, part], f_back[:, part], ALU.add))

        def f_pool(pool, k):
            def power(c):
                norm_power(pool, c + LN_F[k])

            def keep_x(c):
                pool.wait_ge(t["xn"], c + STEPS * k + 1)
                pool.tensor_copy(f_xs[:, bass.ds(c * CHUNK, CHUNK)], f_norm[2]).then_inc(t["xs"], 1)

            chunks(pool, [(power, 1), (keep_x, 1)])
            x3 = f_xs.rearrange("p (i c) -> p i c", c=C)
            pool.wait_ge(t["xs"], STEPS * (k + 1) + CREDIT)
            pool.wait_ge(t["scored"], k + 1 + CREDIT)
            pool.tensor_tensor(x3, x3, f_score.unsqueeze(2).to_broadcast([P, TILES, C]), ALU.mult).then_inc(t["scaled"], 1)
            pool.wait_ge(t["scaled"], k + 1)
            pool.wait_ge(t["placed"], k + 1)
            pool.wait_ge(zeroed, 16)
            for i in range(TILES):
                pool.indirect_dma_start(out=sorted_x, out_offset=bass.IndirectOffsetOnAxis(ap=f_row[:, i:i + 1], axis=0),
                                        in_=f_xs[:, i * C:i * C + C], in_offset=None).then_inc(scattered, 16)
            for j in range(4):
                pool.wait_ge(slot_out[j], 16 * (SLOTS // 4) * (k + 1) + CREDIT)
            for i in range(TILES):
                pool.indirect_dma_start(out=f_back[:, i * C:i * C + C], out_offset=None, in_=sorted_y,
                                        in_offset=bass.IndirectOffsetOnAxis(ap=f_row[:, i:i + 1], axis=0))\
                    .then_inc(t["gathered"], 16)

        def f_sp(sp, k):
            sp.wait_ge(scattered, 16 * TILES * (k + 1))

            def fetch(s, j):
                n = SLOTS * k + s
                if not isinstance(n, int) or n >= 4:
                    sp.wait_ge(t["gx_t"], n - 3 + CREDIT)
                sp.dma_start(f_gx[j], sorted_x[bass.ds(s * P, P), :]).then_inc(slot_in[j], 16)

            def store(s, j):
                sp.wait_ge(t["y_copied"], SLOTS * k + s + 1 + CREDIT)
                sp.dma_start(sorted_y[bass.ds(s * P, P), :], f_gy[j]).then_inc(slot_out[j], 16)

            slots(sp, [(fetch, 3), (store, -3)])

        used[0] = 0
        b_x = carve(TOK)
        b_odd, b_even = carve(OCT), carve(OCT)
        b_q, b_k = carve(OCT), carve(OCT)
        b_v = [carve(SUB * 3 * D_B).rearrange("p (i c) -> p i c", c=3 * D_B) for _ in range(2)]
        b_s, b_st = carve(2 * SUB * 32), carve(2 * SUB * 32)
        b_max = carve(2 * SUB)
        b_wide = [carve(2 * SUB * P).rearrange("p (s q) -> p s q", q=P) for _ in range(2)]
        b_yt = carve(TOK)
        pools_at = used[0]
        b_at = carve(TOK)
        b_yc, b_ac = carve(OCT), carve(OCT)
        b_yn = carve(TOK)
        b_w, b_w_next = carve(3 * P), carve(3 * P)
        b_wo = carve(C)
        b_bias = carve(C)
        b_norm = [b_yt[:, n * CHUNK:n * CHUNK + CHUNK] for n in range(3)]
        b_pool, at = [b_x], pools_at
        for level in range(1, LEVELS + 1):
            b_pool.append(arena[:, at:at + TOK // 2 ** level])
            at += TOK // 2 ** level
        FIRST_OF = [sum(TOK // 2 ** (l + 1) for l in range(1, level)) for level in range(1, LEVELS + 2)]

        h = {n: sem("b_" + n) for n in (
            "xn xt x pooled packed ready w_copied proj q_out s_done masked st expd av y_out a_out summed divided normed o acc").split()}
        w_in, wo_in, bias_in = sem("b_w_in"), sem("b_wo_in"), sem("b_bias_in")
        credited += [h[n] for n in "xt x q_out s_done masked expd av y_out a_out summed divided normed o acc".split()]

        def attention(eng, order, chain=None, per=0):
            lead, lag = max(d for _, d in order), min(d for _, d in order)

            def step(p, k):
                for stage, d in order:
                    u = 3 * p + k + d
                    if isinstance(u, int) and not 0 <= u < 3 * PAIRS:
                        continue
                    stage(p + (k + d) // 3, (k + d) % 3, u, (k + d) % 2)

            for k in range(-lead, 6):
                step(0, k)
            with eng.Fori(1, PAIRS // 2 - 1) as i:
                if chain:
                    chain.enter(i - 1, per)
                for k in range(6):
                    step(2 * i, k)
            if chain:
                chain.leave(PAIRS // 2 - 2)
            for k in range(6 - lag):
                step(PAIRS - 2, k)

        def by_head(name, head):
            rows = slice(0, D_B) if (name == "y") == (head == 0) else slice(D_B, P)
            return psum[rows, (4 + 2 * head) * 512:(6 + 2 * head) * 512]

        def outputs_used(eng, p, o):
            if isinstance(p, int) and p == 0:
                return
            eng.wait_ge(h["normed"], (2 * p + o - 1 if o < 2 else 2 * p) + CREDIT)

        def b_columns(o, odd):
            return b_x[:, o * OCT:o * OCT + OCT] if o < 2 else (b_odd if odd else b_even)

        def b_pe(pe):
            with pe.Fori(0, STEPS) as c:
                pe.wait_ge(h["xn"], c + 1)
                pe.wait_ge(h["x"], c + CREDIT)
                for i in range(CT):
                    mm = pe.transpose(bank[0][:, i * P:i * P + P], b_norm[2][:, i * C:i * C + C], ident)
                mm.then_inc(h["xt"], 1)
            pe.wait_ge(h["x"], STEPS + CREDIT)
            pe.wait_ge(h["packed"], 1)
            pe.wait_ge(h["ready"], 1)

            def project_qk(p, o, u, r):
                if o == 0:
                    pe.wait_ge(h["w_copied"], p + 1)
                if o == 1 and (not isinstance(p, int) or p >= 2):
                    pe.wait_ge(h["acc"], 4 * (p - 1) + CREDIT)
                for n in range(4):
                    if not isinstance(u, int) or u > 0 or n > 0:
                        pe.wait_ge(h["q_out"], 6 * u + n - 1 + CREDIT)
                    pe.matmul(bank[n % 2][:, :], b_w[:, n // 2 * P:n // 2 * P + P],
                              b_columns(o, n < 2)[:, n % 2 * 512:n % 2 * 512 + 512],
                              start=True, stop=True).then_inc(h["proj"], 1)

            def project_v(p, o, u, r):
                for i in range(SUB):
                    if i % 4 == 0:
                        pe.wait_ge(h["q_out"], 6 * u + 3 + i // 4 + CREDIT)
                    if i == 5:
                        pe.wait_ge(h["masked"], u + CREDIT)
                    mm = pe.matmul(bank[i // 4][:, i % 4 * P:i % 4 * P + P], b_columns(o, False)[:, i * P:i * P + P],
                                   b_w[:, 2 * P:3 * P], start=True, stop=True)
                    if i % 4 == 3:
                        mm.then_inc(h["proj"], 1)

            def scores(p, o, u, r):
                for i in range(SUB):
                    for half in range(2):
                        for head in range(2):
                            rows = slice(head * D_B, head * D_B + D_B)
                            tok = slice(i * P + 64 * half, i * P + 64 * half + 64)
                            mm = pe.matmul(bank[2 + head][64 * half:64 * half + 64, i * 64:i * 64 + 64],
                                           b_q[rows, tok], b_k[rows, tok], start=True, stop=True)
                mm.then_inc(h["s_done"], 1)

            def weighted(p, o, u, r):
                pe.wait_ge(h["expd"], u + 1 + CREDIT)
                pe.wait_ge(h["q_out"], 6 * u + 6 + CREDIT)
                pe.wait_ge(h["y_out"], 2 * u + CREDIT)
                pe.wait_ge(h["a_out"], 2 * u + CREDIT)
                for head in range(2):
                    for i in range(SUB):
                        mm = pe.matmul(bank[4 + 2 * head + i // 4][:, i % 4 * P:i % 4 * P + P],
                                       b_v[r][:, i, head * D_B:head * D_B + P], b_wide[r][:, head * SUB + i, :],
                                       start=True, stop=True)
                mm.then_inc(h["av"], 1)

            def project_out(p, o, u, r):
                if o != 2:
                    return
                pe.wait_ge(h["normed"], 2 * p + 2 + CREDIT)
                pe.wait_ge(wo_in, 16 * p + 16)
                last = isinstance(u, int) and u + 4 >= 3 * PAIRS
                pe.wait_ge(h["q_out"], (18 * PAIRS if last else 6 * (u + 4) + 6) + CREDIT)
                for i in range(TILES):
                    if i % 4 == 0 and i >= 8:
                        pe.wait_ge(h["acc"], 4 * p + i // 4 - 1 + CREDIT)
                    mm = pe.matmul(bank[i // 4 % 2][:, i % 4 * C:i % 4 * C + C], b_yn[:, i * P:i * P + P], b_wo,
                                   start=True, stop=True)
                    if i % 4 == 3:
                        mm.then_inc(h["o"], 1)

            attention(pe, [(project_qk, 1), (project_v, 1), (scores, 1), (project_out, -3), (weighted, 0)])

        def b_act(act):
            with act.Fori(0, STEPS) as c:
                act.wait_ge(h["xt"], c + 1 + CREDIT)
                act.activation(b_x[:, bass.ds(c * CHUNK, CHUNK)], bank[0][:, :], ACT.Copy).then_inc(h["x"], 1)
            for level in range(1, LEVELS + 1):
                act.wait_ge(h["pooled"], level)
                n = TOK // 2 ** (level + 1)
                blocks = b_pool[level].rearrange("p (g two i) -> p g two i", two=2, i=16)
                for side, dst, scale in ((0, b_even, 1.0), (1, b_odd, 0.25 ** level)):
                    i = act.activation(dst[:, FIRST_OF[level - 1]:FIRST_OF[level - 1] + n]
                                       .rearrange("p (g i) -> p g i", i=16), blocks[:, :, side, :], ACT.Copy, scale=scale)
            i.then_inc(h["packed"], 1)
            act.wait_ge(h["ready"], 1)

            def copy_weights(p):
                act.wait_ge(w_in, 16 * p + 16)
                act.activation(b_w, b_w_next, ACT.Copy).then_inc(h["w_copied"], 1)

            def copy_qk(p, o, u, r):
                act.wait_ge(h["s_done"], u + CREDIT)
                for n in range(4):
                    act.wait_ge(h["proj"], 6 * u + n + 1)
                    dst = (b_q, b_k)[n // 2][:, n % 2 * 512:n % 2 * 512 + 512]
                    act.activation(dst, bank[n % 2][:, :], ACT.Copy, scale=(D_B ** -0.5, 1.0)[n // 2]).then_inc(h["q_out"], 1)

            def copy_v(p, o, u, r):
                act.wait_ge(h["av"], (max(u - 1, 0) if isinstance(u, int) else u - 1) + CREDIT)
                heads = b_v[r].rearrange("p i (a d) -> p i a d", d=D_B)[:, :, 0:3:2, :]
                for n in range(2):
                    act.wait_ge(h["proj"], 6 * u + 5 + n)
                    act.activation(heads[:, 4 * n:4 * n + 4],
                                   bank[n][:, :].rearrange("p (i a d) -> p i a d", a=2, d=D_B), ACT.Copy)\
                       .then_inc(h["q_out"], 1)
                if o == 2 and not (isinstance(u, int) and u == 3 * PAIRS - 1):
                    copy_weights(p + 1)

            def exponents(p, o, u, r):
                act.wait_ge(h["st"], u + 1)
                act.wait_ge(h["av"], (max(u - 1, 0) if isinstance(u, int) else u - 1) + CREDIT)
                for j in range(4):
                    q = slice(32 * j, 32 * j + 32)
                    i = act.activation(b_wide[r][q, :, q], b_st[q, :].rearrange("p (s q) -> p s q", q=32), ACT.Exp)
                i.then_inc(h["expd"], 1)

            def copy_y(p, o, u, r):
                act.wait_ge(h["av"], u + 1 + CREDIT)
                outputs_used(act, p, o)
                dst = b_yt[:, o * OCT:o * OCT + OCT] if o < 2 else b_yc
                for head in range(2):
                    act.activation(dst[head * D_B:head * D_B + D_B, :], by_head("y", head), ACT.Copy).then_inc(h["y_out"], 1)

            copy_weights(0)
            attention(act, [(copy_qk, 1), (exponents, 0), (copy_v, 1), (copy_y, 0)])

        def b_dve(dve, chain):
            with dve.Fori(0, STEPS) as c:
                chain.enter(c, 4)
                chunk = x_tok[:, bass.ds(c * CHUNK, CHUNK)]
                norm(dve, chain, tiles_of(chunk), b_norm[0], b_norm[1], b_norm[2], c + LN_B,
                     lambda: dve.wait_ge(h["xt"], c + CREDIT)).then_inc(h["xn"], 1)
            chain.leave(STEPS)
            dve.wait_ge(h["x"], STEPS + CREDIT)
            chain(dve.memset(b_odd[:, COARSE:OCT], 0.0))
            chain(dve.memset(b_even[:, COARSE:OCT], 0.0))
            for level in range(1, LEVELS + 1):
                two = b_pool[level - 1].rearrange("p (n two) -> p n two", two=2)
                dve.tensor_tensor(b_pool[level], two[:, :, 0], two[:, :, 1], ALU.add).then_inc(h["pooled"], 1)
                dve.wait_ge(h["pooled"], level)
            dve.wait_ge(bias_in, 16)
            x3 = x_tok[:, :].rearrange("p (i c) -> p i c", c=C)
            chain(dve.tensor_tensor(x3, x3, b_bias.unsqueeze(1).to_broadcast([P, TILES, C]), ALU.add))
            dve.wait_ge(h["packed"], 1)

            def soften(p, o, u, r):
                mask = constant("mask_causal" if o < 2 else "mask_block")
                s3 = b_s.rearrange("p (s k) -> p s k", k=32)
                dve.wait_ge(h["s_done"], u + 1 + CREDIT)
                if not isinstance(u, int) or u > 0:
                    dve.wait_ge(h["st"], u)
                for j in range(4):
                    rows = slice(32 * j, 32 * j + 32)
                    blocks = psum[rows, 2 * 512:4 * 512].rearrange("p (s k) -> p s k", k=64)[:, :, j % 2 * 32:j % 2 * 32 + 32]
                    i = dve.tensor_tensor(s3[rows], blocks, mask[rows].unsqueeze(1).to_broadcast([32, 2 * SUB, 32]), ALU.add)
                i.then_inc(h["masked"], 1)
                dve.wait_ge(h["masked"], u + 1 + CREDIT)
                chain(dve.reduce_max(b_max, s3, AX))
                chain(dve.tensor_tensor(s3, s3, b_max.unsqueeze(2).to_broadcast([P, 2 * SUB, 32]), ALU.subtract))
                dve.wait_ge(h["expd"], u + CREDIT)
                dve.transpose(b_st, b_s).then_inc(h["st"], 1)

            def copy_sums(p, o, u, r):
                dve.wait_ge(h["av"], u + 1 + CREDIT)
                outputs_used(dve, p, o)
                dst = b_at[:, o * OCT:o * OCT + OCT] if o < 2 else b_ac
                for head in range(2):
                    if o < 2:
                        i = dve.tensor_scalar(dst[head * D_B:head * D_B + D_B, :], by_head("a", head), 1e-8, None, ALU.add)
                    else:
                        i = dve.tensor_copy(dst[head * D_B:head * D_B + D_B, :], by_head("a", head))
                    i.then_inc(h["a_out"], 1)

            def divide(batch):
                def stage(p, o, u, r):
                    if o == 2:
                        if batch == 0:
                            dve.wait_ge(h["summed"], p + 1 + CREDIT)
                        part = b_at[:, batch * OCT:batch * OCT + OCT]
                        dve.reciprocal(part, part).then_inc(h["divided"], 1)
                return stage

            def gather_out(p, o, u, r):
                if o != 2:
                    return
                for n in range(4):
                    dve.wait_ge(h["o"], 4 * p + n + 1 + CREDIT)
                    part = slice(n * 512, n * 512 + 512)
                    dve.tensor_tensor(x_tok[:, part], x_tok[:, part], bank[n % 2][:, :], ALU.add).then_inc(h["acc"], 1)

            attention(dve, [(divide(0), -1), (divide(1), -2), (soften, 1), (gather_out, -3), (copy_sums, 0)], chain, 6 * 2)
            dve.wait_ge(h["acc"], 4 * PAIRS + CREDIT)

        def b_pool_engine(pool):
            with pool.Fori(0, STEPS) as c:
                norm_power(pool, c + LN_B)
            for r in range(2):
                pool.memset(b_wide[r], 0.0)
                i = pool.memset(b_v[r][:, :, D_B:2 * D_B], 1.0)
            i.then_inc(h["ready"], 1)
            chain = Chain(pool, pool_chain)

            def join(p, o, u, r):
                if o != 2:
                    return
                for sums in (True, False):
                    pool.wait_ge(h["a_out" if sums else "y_out"], 2 * u + 2 + CREDIT)
                    fine, coarse = (b_at, b_ac) if sums else (b_yt, b_yc)
                    for level in range(1, LEVELS + 1):
                        span = 2 ** level
                        at, count = FIRST_OF[level - 1], TOK // (2 * span)
                        dst = fine.rearrange("p (g c s) -> p g c s", c=32, s=span)[:, :, 16:32, span - 1]
                        i = pool.tensor_tensor(dst, dst, coarse[:, at:at + count].rearrange("p (g c) -> p g c", c=16), ALU.add)
                        if sums and level == LEVELS:
                            i.then_inc(h["summed"], 1)
                        else:
                            chain(i)

            def scale(p, o, u, r):
                if o != 2:
                    return
                pool.wait_ge(h["o"], 4 * p + CREDIT)
                for b in range(BATCH):
                    part = slice(b * OCT, b * OCT + OCT)
                    pool.wait_ge(h["divided"], 2 * p + b + 1 + CREDIT)
                    pool.tensor_tensor(b_yn[:, part], b_yt[:, part], b_at[:, part], ALU.mult).then_inc(h["normed"], 1)

            attention(pool, [(join, 0), (scale, 0)], chain, 2 * (2 * LEVELS - 1))

        def b_sp(sp):
            def weights_in(p):
                sp.dma_start(b_w_next.rearrange("p (n c) -> p n c", c=P), w["w_qkv"][bass.ds(p, 1)].rearrange("a c n j -> (a c) n j"))\
                  .then_inc(w_in, 16)

            def out_weights_in(p):
                sp.dma_start(b_wo, w["w_out"][bass.ds(p, 1)].rearrange("a c j -> (a c) j")).then_inc(wo_in, 16)

            sp.wait_ge(h["xn"], 1)
            sp.dma_start(b_bias, w["b_out"].to_broadcast([P, C])).then_inc(bias_in, 16)
            weights_in(0)
            out_weights_in(0)
            sp.wait_ge(h["w_copied"], 1)
            weights_in(1)
            with sp.Fori(2, PAIRS) as p:
                sp.wait_ge(h["w_copied"], p)
                weights_in(p)
                sp.wait_ge(h["o"], 4 * (p - 1) + CREDIT)
                out_weights_in(p - 1)
            sp.wait_ge(h["o"], 4 * (PAIRS - 1) + CREDIT)
            out_weights_in(PAIRS - 1)
        final = sem("final")
        block = ctx.enter_context(nc.Block())
        loads = [(const[:, :], w["constants"][:, 0:CONST["pick"][0]]), (pick, w["constants"][:, CONST["pick"][0]:CONST_COLS]),
                 (vectors[:, :], w["vectors"]), (w1, w["maa_w1"]), (w2, w["maa_w2"]), (dw1, w["decay_w1"]),
                 (dw2[0:DECAY, :], w["decay_w2"]), (wrkvo, w["wrkvo"]), (gate_w[:, :], w["gate_w"]),
                 (shared_up[:, :], w["shared_up"]),
                 (shared_down[:, :].rearrange("p (f c) -> p f c", c=C), w["shared_down"].rearrange("(f p) c -> p f c", p=P))]
        LOADS = len(loads)
        EXPERT_LOADS = 8

        @block.sync
        def _(sp):
            for c in credited:
                sp.sem_inc(c, CREDIT)
            sp.dma_start(tiles_of(x_tok[:, :]), w["x"].rearrange("i p c -> p i c")).then_inc(loaded_x, 16)
            for dst, src in loads:
                sp.dma_start(dst, src).then_inc(loaded, 16)
            for i in range(EXPERT_LOADS):
                part = slice(i * EXPERTS * WROW // EXPERT_LOADS, (i + 1) * EXPERTS * WROW // EXPERT_LOADS)
                sp.dma_start(experts[:, part], w["experts"][:, part]).then_inc(loaded_experts, 16)
            sp.wait_ge(zero_row, 1)
            sp.dma_start(sorted_x.rearrange("(s p) c -> p s c", p=P), zeros[:, :].unsqueeze(1).to_broadcast([P, SLOTS, C]))\
              .then_inc(zeroed, 16)
            f_sp(sp, 0)
            b_sp(sp)
            f_sp(sp, 1)
            sp.wait_ge(final, 1)
            sp.dma_start(out.rearrange("i p c -> p i c"), tiles_of(x_tok[:, :])).then_inc(stored, 16)
            sp.wait_ge(stored, 16)

        @block.tensor
        def _(pe):
            a_pe(pe)
            f_pe(pe, 0)
            b_pe(pe)
            f_pe(pe, 1)

        @block.scalar
        def _(act):
            a_act(act)
            f_act(act, 0)
            b_act(act)
            f_act(act, 1)

        @block.gpsimd
        def _(pool):
            pool.memset(zeros[:, :], 0.0).then_inc(zero_row, 1)
            pool.memset(ones_bf, 1.0)
            pool.wait_ge(loaded, LOADS * 16)
            pool.tensor_copy(later_bf, constant("later")).then_inc(zero_row, 1)
            a_pool(pool)
            f_pool(pool, 0)
            b_pool_engine(pool)
            f_pool(pool, 1)

        @block.vector
        def _(dve):
            chain = a_dve(dve)
            f_dve(dve, chain, 0)
            b_dve(dve, chain)
            f_dve(dve, chain, 1)
            dve.memset(stat[:, 12:13], 0.0).then_inc(final, 1)


def _constants():
    import numpy as np

    c = np.zeros((P, CONST_COLS), np.float32)

    def put(name, value):
        at, width = CONST[name]
        c[:, at:at + width] = np.broadcast_to(value, (P, width))

    row = np.arange(P)
    put("ident", np.eye(P))
    put("head_ones", row[:, None] // N_A == row[None, :] // N_A)
    pick = np.zeros((P, N_A, P))
    for m in range(N_A):
        pick[:, m] = (row[:, None] // N_A == row[None, :] // N_A) & (row[None, :] % N_A == m)
    put("pick", pick.reshape(P, -1))
    put("later", (row[:, None] < row[None, :]) - 1.0)
    put("expert_rank", (32.0 - np.arange(32))[None])
    put("tile_reset", (np.arange(512) % 16 != 0)[None])
    put("slot_no", np.arange(float(SLOTS))[None])
    put("tile_start", (P * np.arange(float(TILES)))[None])
    q, k = row[:, None] % 32, np.arange(32)[None]
    put("mask_causal", np.where((q // 16 == k // 16) & (k <= q), 0.0, -1e30))
    put("mask_block", np.where(q // 16 == k // 16, 0.0, -1e30))
    put("half", -0.5)
    return c


def kernel(**inputs):
    import numpy as np
    import concourse.bacc as bacc
    from concourse.bass_utils import run_bass_kernel_spmd as run

    nc = bacc.Bacc("TRN2", target_bir_lowering=False, num_devices=1)
    a = {n.replace("L0_", ""): np.asarray(v) for n, v in inputs.items()}
    col = lambda v: np.ascontiguousarray(v.reshape(C, 1))
    laid = {
        "x": a["attn_a_x"].reshape(TILES, P, C),
        "vectors": np.concatenate([col(a["attn_a_" + n]) for n in (
            "time_maa_x", "time_maa_w", "time_maa_k", "time_maa_v", "time_maa_r",
            "time_decay", "time_faaaa", "ln_g", "ln_b")], 1),
        "b_out": a["attn_b_b_out"].reshape(1, C),
        "maa_w1": a["attn_a_maa_w1"],
        "maa_w2": a["attn_a_maa_w2"].reshape(4 * MIX, C),
        "decay_w1": a["attn_a_decay_w1"],
        "decay_w2": a["attn_a_decay_w2"],
        "wrkvo": np.concatenate([a["attn_a_" + n] for n in ("Wr", "Wk", "Wv", "Wo")], 1),
        "w_qkv": np.ascontiguousarray(
            a["attn_b_w_qkv"].reshape(3, PAIRS, P, C).transpose(1, 3, 0, 2)),
        "w_out": np.ascontiguousarray(a["attn_b_w_out"].reshape(C, PAIRS, P).transpose(1, 2, 0)),
        "gate_w": a["ffn_gate_w"],
        "shared_up": np.concatenate([a["ffn_shared_gate_w"], a["ffn_shared_up_w"]], 1),
        "shared_down": a["ffn_shared_down_w"],
        "experts": np.concatenate([
            a["ffn_routed_gate_w"].transpose(1, 0, 2), a["ffn_routed_up_w"].transpose(1, 0, 2),
            a["ffn_routed_down_w"].reshape(EXPERTS, INNER // P, P, C).transpose(2, 0, 1, 3).reshape(P, EXPERTS, -1),
        ], 2).reshape(P, EXPERTS * WROW),
        "constants": _constants(),
    }
    arrays, aps = {}, {}
    for name, v in laid.items():
        v = np.ascontiguousarray(v)
        arrays["in_" + name] = v
        aps[name] = nc.dram_tensor("in_" + name, v.shape, mybir.dt.from_np(v.dtype), kind="ExternalInput").ap()
    out = nc.dram_tensor("out_0", (TILES, P, C), F32, kind="ExternalOutput").ap()
    hybrid_block(nc, aps, out)
    r = run(nc, [arrays], core_ids=[0])
    return r.results[0]["out_0"].reshape(BATCH, SEQ, C)
```

```python
from contextlib import ExitStack

import concourse.bass as bass
from concourse import mybir

F32 = mybir.dt.float32
BF16 = mybir.dt.bfloat16
I32 = mybir.dt.int32
U32 = mybir.dt.uint32
ALU = mybir.AluOpType
ACT = mybir.ActivationFunctionType
AX = mybir.AxisListType.X

P = 128
C = 128
BATCH = 2
SEQ = 1024
TOK = BATCH * SEQ
TILES = TOK // P
CHUNK = 512
CT = CHUNK // P
STEPS = TOK // CHUNK
HALVES = SEQ // CHUNK
EPS = 1e-5
ARENA = 24000
CREDIT = 1

HEADS_A = 16
N_A = C // HEADS_A
DECAY = 64
MIX = 32

HEADS_B = 16
D_B = 64
PAIRS = HEADS_B * D_B // P
LEVELS = 5
COARSE = sum(TOK // 2 ** (l + 1) for l in range(1, LEVELS + 1))
OCT = 1024
SUB = OCT // P

EXPERTS = 32
INNER = 256
WROW = 2 * INNER + INNER // P * C
SLOTS = 48
assert SLOTS >= TOK // P + EXPERTS - 1 and SLOTS % 4 == 0

CONST = {}
_at = 0
for _n, _w in [("ident", P), ("head_ones", P), ("later", P), ("expert_rank", EXPERTS),
               ("tile_reset", EXPERTS * TILES), ("slot_no", SLOTS), ("tile_start", TILES),
               ("mask_causal", 32), ("mask_block", 32), ("half", TILES), ("pick", N_A * P)]:
    CONST[_n] = (_at, _w)
    _at += _w
CONST_COLS = _at


class Chain:

    def __init__(self, eng, sem):
        self.eng, self.sem, self.n, self.moving = eng, sem, 0, 0

    def __call__(self, ins):
        ins.then_inc(self.sem, 1)
        self.n += 1
        self.eng.wait_ge(self.sem, self.moving + self.n)

    def enter(self, i, per):
        self.moving, self.start, self.per = i * per, self.n, per

    def leave(self, times):
        assert self.n - self.start == self.per, (self.n - self.start, self.per)
        self.moving, self.n = 0, self.start + self.per * times


def hybrid_block(nc, w, out):
    with ExitStack() as ctx:
        def sb(name, shape, dt=F32):
            return ctx.enter_context(nc.sbuf_tensor(name, shape, dt))

        def sem(name):
            return ctx.enter_context(nc.semaphore(name))

        psum = ctx.enter_context(nc.psum_tensor("psum", [P, 8 * 512], F32))
        bank = [psum[:, i * 512:i * 512 + 512] for i in range(8)]

        experts = sb("experts", [P, EXPERTS * WROW])
        x_tok = sb("x_tok", [P, TOK])
        const = sb("const", [P, CONST["pick"][0]])
        vectors = sb("vectors", [P, 9])
        gate_w = sb("gate_w", [P, EXPERTS])
        shared_up = sb("shared_up", [P, 2 * INNER])
        shared_down = sb("shared_down", [P, INNER // P * C])
        zeros = sb("zeros", [P, C])
        exact_bf = sb("exact_bf", [P, 2 * P], BF16)
        ones_bf, later_bf = exact_bf[:, 0:P], exact_bf[:, P:2 * P]
        stat = sb("stat", [P, 4 * CT])
        arena = sb("arena", [P, ARENA])

        used = [0]

        def carve(n):
            at = used[0]
            used[0] += n
            assert used[0] <= ARENA, used[0]
            return arena[:, at:at + n]

        def constant(name):
            at, width = CONST[name]
            return const[:, at:at + width]

        ident = constant("ident")
        (maa_x, maa_w, maa_k, maa_v, maa_r, t_decay, faaaa, ln_g, ln_b) = (vectors[:, i:i + 1] for i in range(9))

        sorted_x = nc.dram_tensor("sorted_x", (SLOTS * P, C), F32, kind="Internal").ap()
        sorted_y = nc.dram_tensor("sorted_y", (SLOTS * P, C), F32, kind="Internal").ap()

        loaded, loaded_later = sem("loaded"), sem("loaded_later")
        loaded_x, loaded_experts = sem("loaded_x"), sem("loaded_experts")
        zero_row, zeroed, stored = sem("zero_row"), sem("zeroed"), sem("stored")
        dve_chain, act_chain, pool_chain = sem("dve_chain"), sem("act_chain"), sem("pool_chain")

        ln_var, ln_rstd = sem("ln_var"), sem("ln_rstd")

        def tiles_of(ap):
            return ap.rearrange("p (a b) -> p a b", b=C)

        def over(col):
            return col.unsqueeze(2).to_broadcast([P, CT, C])

        mean, var, rstd = (stat[:, CT * i:CT * i + CT] for i in range(3))

        def norm_first(dve, chain, src, centred, square):
            chain(dve.reduce_sum(mean, src, AX))
            chain(dve.scalar_tensor_tensor(tiles_of(centred), over(mean), -1.0 / C, src, ALU.mult, ALU.add))
            chain(dve.tensor_tensor(square, centred, centred, ALU.mult))
            chain(dve.reduce_sum(var, tiles_of(square), AX))
            dve.tensor_scalar(var, var, 1.0 / C, EPS, ALU.mult, ALU.add).then_inc(ln_var, 1)

        def norm_last(dve, centred, target, n):
            dve.wait_ge(ln_rstd, n + 1)
            return dve.tensor_tensor(tiles_of(target), tiles_of(centred), over(rstd), ALU.mult)

        def norm(dve, chain, src, centred, square, target, n, free):
            norm_first(dve, chain, src, centred, square)
            free()
            return norm_last(dve, centred, target, n)

        def norm_power(pool, n):
            pool.wait_ge(ln_var, n + 1)
            pool.tensor_tensor(rstd, var, constant("half")[:, 0:CT], ALU.pow).then_inc(ln_rstd, 1)

        w1 = carve(4 * MIX)
        w2 = carve(C)
        dw1 = carve(DECAY)
        dw2 = carve(C)
        dw2_mean = carve(C)
        wrkvo = carve(4 * C)
        wv_wide = carve(N_A * C)
        pick = carve(N_A * P)
        a_decay = carve(2)
        a_norm = [carve(CHUNK) for _ in range(3)]
        a_x = [carve(CHUNK + 1) for _ in range(2)]
        a_xx, a_xxx, a_mix = carve(CHUNK), carve(CHUNK), carve(CHUNK)
        in_w, in_k, in_v, in_r = carve(CHUNK), carve(CHUNK), [carve(CHUNK) for _ in range(2)], carve(CHUNK)
        a_in = [[in_w, in_k, in_v[half], in_r] for half in range(2)]
        a_th = carve(CHUNK)
        a_d, a_k, a_v, a_r = ([carve(CHUNK) for _ in range(2)] for _ in range(4))
        a_kv = [carve(CHUNK) for _ in range(2)]
        a_state = carve(N_A * (CHUNK + 1)).rearrange("p (m t) -> p m t", m=N_A)
        a_g = [carve(CHUNK) for _ in range(2)]
        a_ruk, a_diag = carve(CHUNK), carve(CHUNK)
        a_y, a_ynt = carve(CHUNK), carve(CHUNK)

        s = {n: sem("a_" + n) for n in (
            "weights xn xt xs xxx mix_in mix wf tf xf decay_in th dlog d proj rkv rowed kv state g y_done "
            "ruk diag_in diag dv y yt yn_t yn_copied o added decay_mean").split()}

        XT_BANK, MISC, FRONT, ROWED, YB, OB = bank[0], bank[1], bank[2:4], bank[4:6], bank[6], bank[7]

        credited = [s[n] for n in "diag kv xf tf o y_done yn_t yn_copied rkv g diag_in state xs d added".split()]


        def a_pe(pe):
            pe.wait_ge(s["weights"], 1)
            pe.wait_ge(loaded, LOADS * 16)
            pe.matmul(MISC[:, 0:1], constant("head_ones"), t_decay, start=True, stop=True).then_inc(s["decay_in"], 1)
            def turn_x(g, half):
                pe.wait_ge(s["xn"], 2 * (g - half) + half + 1)
                if half == 0:
                    pe.wait_ge(s["yn_copied"], g + CREDIT)
                else:
                    pe.wait_ge(s["xs"], g + CREDIT)
                for t in range(CT):
                    i = pe.transpose(XT_BANK[:, t * P:t * P + P], a_norm[2][:, t * C:t * C + C], ident)
                i.then_inc(s["xt"], 1)

            def mix_in(g, half):
                pe.wait_ge(s["xxx"], g + 1)
                pe.wait_ge(s["d"], g + CREDIT)
                pe.matmul(MISC[:, :], w1, a_xxx, start=True, stop=True).then_inc(s["mix_in"], 1)

            def mix_out(g, half, f):
                if f == 0:
                    pe.wait_ge(s["mix"], g + 1)
                if f < 2:
                    pe.wait_ge(s["rkv"], 3 * g + CREDIT)
                else:
                    pe.wait_ge(s["tf"], 4 * g + f - 1 + CREDIT)
                pe.matmul(FRONT[f % 2][:, :], w2[f * MIX:f * MIX + MIX, :], a_mix[f * MIX:f * MIX + MIX, :],
                          start=True, stop=True).then_inc(s["wf"], 1)

            def decay_hidden(g, half):
                pe.wait_ge(s["xf"], 4 * g + 1 + CREDIT)
                pe.matmul(MISC[0:DECAY, :], dw1, a_in[half][0], start=True, stop=True).then_inc(s["decay_in"], 1)

            def project(g, half, n):
                pe.wait_ge(s["xf"], 4 * g + n + 2 + CREDIT)
                if n == 0:
                    pe.wait_ge(s["tf"], 4 * g + 4 + CREDIT)
                if n == 2:
                    pe.wait_ge(s["rkv"], 3 * g + 1 + CREDIT)
                at = (1, 2, 0)[n]
                pe.matmul(FRONT[n % 2][:, :], wrkvo[:, at * C:at * C + C], a_in[half][n + 1],
                          start=True, stop=True).then_inc(s["proj"], 1)

            def decay_out(g, half):
                pe.wait_ge(s["th"], g + 1)
                pe.matmul(MISC[:, :], dw2_mean[0:DECAY, :], a_th[0:DECAY, :], start=True, stop=True)\
                  .then_inc(s["dlog"], 1)

            def recurrence(g, half, m):
                if m < N_A:
                    pe.wait_ge(s["kv"], N_A * g + max(m - 1, 0) + CREDIT)
                    pe.matmul(ROWED[m % 2][:, :], wv_wide[:, m * C:m * C + C], a_in[half][2],
                              start=True, stop=True).then_inc(s["rowed"], 1)
                if m == 2:
                    pe.wait_ge(s["ruk"], g + 1)
                    if half == 0:
                        pe.wait_ge(s["added"], g + CREDIT)
                    else:
                        pe.wait_ge(s["diag"], g + CREDIT)
                    pe.matmul(OB[:, :], constant("head_ones"), a_ruk, start=True, stop=True).then_inc(s["diag_in"], 1)
                if m >= 2:
                    q = m - 2
                    pe.wait_ge(s["g"], N_A * g + q + 1 + CREDIT)
                    pe.matmul(YB[:, :], pick[:, q * P:q * P + P], a_g[q % 2],
                              start=(q == 0), stop=(q == N_A - 1)).then_inc(s["y_done"], 1)

            def turn_y(g, half):
                pe.wait_ge(s["y"], g + 1)
                if half == 0:
                    pe.wait_ge(s["xs"], g + 2 + CREDIT)
                else:
                    pe.wait_ge(s["yn_copied"], g + CREDIT)
                for t in range(CT):
                    i = pe.transpose(XT_BANK[:, t * P:t * P + P], a_y[:, t * P:t * P + P], ident)
                i.then_inc(s["yt"], 1)

            def turn_back(g, half):
                pe.wait_ge(s["xn"], 2 * (g - half) + half + 3)
                for t in range(CT):
                    i = pe.transpose(XT_BANK[:, t * P:t * P + P], a_norm[2][:, t * C:t * C + C], ident)
                i.then_inc(s["yn_t"], 1)

            def project_y(g, half):
                pe.wait_ge(s["yn_copied"], g + 1 + CREDIT)
                pe.wait_ge(s["diag"], 2 - half + g + CREDIT)
                pe.wait_ge(s["added"], g + CREDIT)
                for t in range(CT):
                    i = pe.matmul(OB[:, t * C:t * C + C], a_ynt[:, t * P:t * P + P], wrkvo[:, 3 * C:4 * C],
                                  start=True, stop=True)
                i.then_inc(s["o"], 1)

            pe.wait_ge(s["decay_mean"], 1)
            with pe.Fori(0, BATCH) as b:
                g, g1 = b * HALVES, b * HALVES + 1
                turn_x(g, 0)
                mix_in(g, 0)
                for f in range(4):
                    mix_out(g, 0, f)
                decay_hidden(g, 0)
                for n in range(3):
                    project(g, 0, n)
                decay_out(g, 0)
                turn_x(g1, 1)
                pe.wait_ge(loaded_later, LATER_LOADS * 16)
                for m in range(N_A + 2):
                    recurrence(g, 0, m)
                    if m == 1:
                        mix_in(g1, 1)
                    if 2 <= m < 6:
                        mix_out(g1, 1, m - 2)
                    if m == 6:
                        decay_hidden(g1, 1)
                    if m > 6:
                        project(g1, 1, m - 7)
                decay_out(g1, 1)
                for m in range(N_A + 2):
                    recurrence(g1, 1, m)
                    if m == 1:
                        turn_y(g, 0)
                    if m == 6:
                        turn_back(g, 0)
                    if m == 8:
                        project_y(g, 0)
                turn_y(g1, 1)
                turn_back(g1, 1)
                project_y(g1, 1)

        def a_act(act):
            chain = Chain(act, act_chain)
            act.wait_ge(s["decay_in"], 1)
            act.activation(a_decay[:, 0:1], MISC[:, 0:1], ACT.Copy, scale=1.0 / N_A).then_inc(s["decay_mean"], 1)
            act.wait_ge(s["decay_mean"], 1)
            act.wait_ge(s["weights"], 1)

            def copy_x(g, half):
                act.wait_ge(s["xt"], g + 1)
                act.wait_ge(s["xf"], 4 * (g - half) + CREDIT)
                if half:
                    act.wait_ge(s["xs"], g + CREDIT)
                    act.activation(a_x[1][:, 0:1], a_x[0][:, CHUNK:CHUNK + 1], ACT.Copy)
                act.activation(a_x[half][:, 1:CHUNK + 1], XT_BANK[:, :], ACT.Copy).then_inc(s["xs"], 1)

            def mix(g, half):
                act.wait_ge(s["mix_in"], g + 1)
                act.activation(a_mix, MISC[:, :], ACT.Tanh).then_inc(s["mix"], 1)

            def projected(g, half):
                act.wait_ge(s["decay_in"], g + 2)
                act.activation(a_th[0:DECAY, :], MISC[0:DECAY, :], ACT.Tanh).then_inc(s["th"], 1)
                for n, dst in enumerate((a_k, a_v, a_r)):
                    act.wait_ge(s["proj"], 3 * g + n + 1)
                    act.activation(dst[half], FRONT[n % 2][:, :], ACT.Copy).then_inc(s["rkv"], 1)
                act.wait_ge(s["dlog"], g + 1)
                chain(act.activation(a_d[half], MISC[:, :], ACT.Exp, bias=a_decay[:, 0:1]))
                act.activation(a_d[half], a_d[half], ACT.Exp, scale=-1.0).then_inc(s["d"], 1)

            def copy_diagonal(g, half):
                act.wait_ge(s["diag_in"], g + 1 + CREDIT)
                act.activation(a_diag, OB[:, :], ACT.Copy).then_inc(s["diag"], 1)

            def copy_y(g, half):
                act.wait_ge(s["yn_t"], g + 1 + CREDIT)
                act.wait_ge(s["o"], g + CREDIT)
                act.activation(a_ynt, XT_BANK[:, :], ACT.Identity, scale=ln_g, bias=ln_b)\
                   .then_inc(s["yn_copied"], 1)

            with act.Fori(0, BATCH) as b:
                chain.enter(b, 2)
                g, g1 = b * HALVES, b * HALVES + 1
                copy_x(g, 0)
                mix(g, 0)
                projected(g, 0)
                copy_x(g1, 1)
                mix(g1, 1)
                copy_diagonal(g, 0)
                projected(g1, 1)
                copy_diagonal(g1, 1)
                copy_y(g, 0)
                copy_y(g1, 1)
            chain.leave(BATCH)

        def a_pool(pool):
            def add_x(g, half, f):
                pool.wait_ge(s["tf"], 4 * g + f + 1 + CREDIT)
                x = a_in[half][f]
                pool.tensor_tensor(x, x, a_x[half][:, 1:CHUNK + 1], ALU.add).then_inc(s["xf"], 1)

            def recurrence(g, half, m):
                if m == 0:
                    pool.wait_ge(s["rkv"], 3 * g + 3 + CREDIT)
                pool.wait_ge(s["state"], N_A * g + m + 1 + CREDIT)
                pool.wait_ge(s["y_done"], N_A * g + max(m - 1, 0) + CREDIT)
                pool.tensor_tensor(a_g[m % 2], a_r[half], a_state[:, m, 0:CHUNK], ALU.mult).then_inc(s["g"], 1)
                if m == 3:
                    pool.wait_ge(s["diag"], g + 1 + CREDIT)
                    pool.tensor_tensor(a_diag, a_diag, a_v[half], ALU.mult).then_inc(s["dv"], 1)

            with pool.Fori(0, BATCH) as b:
                g, g1 = b * HALVES, b * HALVES + 1
                norm_power(pool, 2 * g)
                for f in range(4):
                    add_x(g, 0, f)
                norm_power(pool, 2 * g + 1)
                for m in range(N_A):
                    recurrence(g, 0, m)
                    if 3 <= m < 7:
                        add_x(g1, 1, m - 3)
                for m in range(N_A):
                    recurrence(g1, 1, m)
                    if m == 2:
                        norm_power(pool, 2 * g + 2)
                norm_power(pool, 2 * g + 3)

        def a_dve(dve):
            chain = Chain(dve, dve_chain)
            dve.wait_ge(loaded, LOADS * 16)
            chain(dve.memset(a_x[0][:, 0:1], 0.0))
            chain(dve.reduce_sum(dw2_mean[0:DECAY, 0:HEADS_A],
                                 dw2[0:DECAY, :].rearrange("p (h n) -> p h n", n=N_A), AX))
            chain(dve.tensor_scalar(dw2[0:DECAY, :].rearrange("p (h n) -> p h n", n=N_A),
                                    dw2_mean[0:DECAY, 0:HEADS_A].unsqueeze(2).to_broadcast([DECAY, HEADS_A, N_A]),
                                    1.0 / N_A, None, ALU.mult))
            chain(dve.tensor_copy(dw2_mean[0:DECAY, :], dw2[0:DECAY, :]))
            for m in range(N_A):
                i = dve.tensor_copy(
                    wv_wide[:, m * C:m * C + C].rearrange("p (h n) -> p h n", n=N_A),
                    wrkvo[:, 2 * C + m:3 * C:N_A].unsqueeze(2).to_broadcast([P, HEADS_A, N_A]))
                if m < N_A - 1:
                    chain(i)
            i.then_inc(s["weights"], 1)
            dve.wait_ge(loaded_x, 16)
            def norm_x(g, half):
                def free():
                    if half == 0:
                        dve.wait_ge(s["yn_t"], g + CREDIT)
                    else:
                        dve.wait_ge(s["xt"], g)

                norm(dve, chain, tiles_of(x_tok[:, bass.ds(g * CHUNK, CHUNK)]), a_norm[0], a_norm[1], a_norm[2],
                     2 * (g - half) + half, free).then_inc(s["xn"], 1)

            def shift(g, half):
                dve.wait_ge(s["xs"], g + 1 + CREDIT)
                x = a_x[half][:, 1:CHUNK + 1]
                chain(dve.tensor_tensor(a_xx, a_x[half][:, 0:CHUNK], x, ALU.subtract))
                dve.scalar_tensor_tensor(a_xxx, a_xx, maa_x, x, ALU.mult, ALU.add).then_inc(s["xxx"], 1)

            def mix(g, half, f):
                dve.wait_ge(s["wf"], 4 * g + f + 1)
                dve.scalar_tensor_tensor(a_in[half][f], FRONT[f % 2][:, :], (maa_w, maa_k, maa_v, maa_r)[f], a_xx,
                                         ALU.add, ALU.mult).then_inc(s["tf"], 1)

            def first_states(g, half):
                dve.wait_ge(s["g"], N_A * g + CREDIT)
                if half == 0:
                    chain(dve.memset(a_state[:, :, 0], 0.0))
                else:
                    chain(dve.tensor_copy(a_state[:, :, 0], a_state[:, :, CHUNK]))

            def recurrence(g, half, m):
                if m == 0:
                    dve.wait_ge(s["rkv"], 3 * g + 3 + CREDIT)
                if m < N_A:
                    dve.wait_ge(s["rowed"], N_A * g + m + 1)
                    if m >= 2:
                        dve.wait_ge(s["state"], N_A * g + m - 1 + CREDIT)
                    dve.tensor_tensor(a_kv[m % 2], a_k[half], ROWED[m % 2][:, :], ALU.mult).then_inc(s["kv"], 1)
                if m == 1:
                    dve.wait_ge(s["diag_in"], g + CREDIT)
                    dve.scalar_tensor_tensor(a_ruk, a_r[half], faaaa, a_k[half], ALU.mult, ALU.mult)\
                       .then_inc(s["ruk"], 1)
                if m >= 1:
                    q = m - 1
                    if q == 0:
                        dve.wait_ge(s["d"], g + 1 + CREDIT)
                    dve.wait_ge(s["state"], N_A * g + q + CREDIT)
                    dve.wait_ge(s["kv"], N_A * g + q + 1 + CREDIT)
                    dve.tensor_tensor_scan(a_state[:, q, 1:CHUNK + 1], a_d[half], a_kv[q % 2], a_state[:, q, 0:1],
                                           ALU.mult, ALU.add).then_inc(s["state"], 1)

            def outputs(g, half):
                dve.wait_ge(s["y_done"], N_A * g + N_A + CREDIT)
                dve.wait_ge(s["dv"], g + 1)
                dve.tensor_tensor(a_y, YB[:, :], a_diag, ALU.add).then_inc(s["y"], 1)

            def norm_y_first(g, half):
                dve.wait_ge(s["yt"], g + 1)
                norm_first(dve, chain, tiles_of(XT_BANK[:, :]), a_norm[0], a_norm[1])

            def norm_y_last(g, half):
                if half == 0:
                    dve.wait_ge(s["xt"], g + 2)
                else:
                    dve.wait_ge(s["yn_t"], g + CREDIT)
                norm_last(dve, a_norm[0], a_norm[2], 2 * (g - half) + half + 2).then_inc(s["xn"], 1)

            def add_output(g, half):
                dve.wait_ge(s["o"], g + 1 + CREDIT)
                chunk = x_tok[:, bass.ds(g * CHUNK, CHUNK)]
                dve.tensor_tensor(chunk, chunk, OB[:, :], ALU.add).then_inc(s["added"], 1)

            with dve.Fori(0, BATCH) as b:
                chain.enter(b, 4 * 4 + 2 + 2)
                g, g1 = b * HALVES, b * HALVES + 1
                norm_x(g, 0)
                shift(g, 0)
                for f in range(4):
                    mix(g, 0, f)
                norm_x(g1, 1)
                first_states(g, 0)
                for m in range(N_A + 1):
                    recurrence(g, 0, m)
                    if m == 0:
                        shift(g1, 1)
                    if 3 <= m < 7:
                        mix(g1, 1, m - 3)
                first_states(g1, 1)
                for m in range(N_A + 1):
                    recurrence(g1, 1, m)
                    if m == 0:
                        outputs(g, 0)
                    if m == 2:
                        norm_y_first(g, 0)
                    if m == 5:
                        norm_y_last(g, 0)
                add_output(g, 0)
                outputs(g1, 1)
                norm_y_first(g1, 1)
                norm_y_last(g1, 1)
                add_output(g1, 1)
            chain.leave(BATCH)
            dve.wait_ge(s["added"], TOK // CHUNK + CREDIT)
            return chain

        used[0] = 0
        f_norm = [carve(CHUNK) for _ in range(3)]
        f_xt = carve(CHUNK)
        f_xt_all = carve(TOK)
        f_gated = [carve(CHUNK) for _ in range(2)]
        f_h = [carve(CHUNK) for _ in range(2)]
        f_xs = carve(TOK)
        f_one_hot = sb("one_hot", [P, EXPERTS * TILES], BF16)
        f_best = carve(TILES)
        f_score = carve(TILES)
        f_pick = [carve(CT * EXPERTS) for _ in range(2)]
        f_upto, f_ends, f_place = (carve(EXPERTS * TILES) for _ in range(3))
        f_tiles, f_first, f_upto_slot, f_ones = (carve(EXPERTS) for _ in range(4))
        f_slot_cmp = carve(SLOTS * EXPERTS)
        f_slot_row, f_place_row = carve(SLOTS), carve(TILES)
        f_slot_at, f_row = sb("slot_at", [P, SLOTS], I32), sb("row", [P, TILES], U32)
        f_gx = [carve(C) for _ in range(4)]
        f_gxt = [carve(P) for _ in range(2)]
        f_sg = [carve(INNER) for _ in range(2)]
        f_sh = [carve(INNER) for _ in range(2)]
        f_sht = [carve(INNER) for _ in range(2)]
        f_gy = [carve(C) for _ in range(4)]
        f_back = carve(TOK)
        LN_F, LN_B = [2 * STEPS, 4 * STEPS], 3 * STEPS

        t = {n: sem("f_" + n) for n in (
            "xn xt xt_copied xs logits shared gated h down best scored rank counts placed rows "
            "scaled gx_t gxt gu sg sh sh_t sht y y_copied").split()}
        gathered = [sem(f"f_gathered{c}") for c in range(STEPS)]
        scattered, slot_in = sem("f_scattered"), [sem(f"f_slot_in{j}") for j in range(4)]
        slot_out = [sem(f"f_slot_out{j}") for j in range(4)]
        credited += [t[n] for n in "down y xt xt_copied xs gated h scored gx_t gxt gu sg sh sh_t sht y_copied".split()]
        credited += slot_out

        def chunks(eng, stages, last=None, chain=None, per=0):
            first = -min(d for _, d in stages + [(None, 0)])
            end = STEPS - 1 - (last is not None)

            def step(c, stages):
                for stage, d in stages:
                    if not isinstance(c, int) or c + d >= 0:
                        stage(c + d)

            for c in range(-1, first):
                step(c, stages)
            with eng.Fori(first, end) as c:
                if chain:
                    chain.enter(c - first, per)
                step(c, stages)
            if chain:
                chain.leave(end - first)
            if last:
                step(end, last)

        def f_pe(pe, k):
            def turn(c):
                g = c + STEPS * k
                pe.wait_ge(t["xn"], g + 1)
                pe.wait_ge(t["xt_copied"], g + CREDIT)
                for i in range(CT):
                    mm = pe.transpose(bank[0][:, i * P:i * P + P], f_norm[2][:, i * C:i * C + C], ident)
                mm.then_inc(t["xt"], 1)

            def logits(c):
                g = c + STEPS * k
                pe.wait_ge(t["xt_copied"], g + 1 + CREDIT)
                if not isinstance(g, int) or c > 0:
                    pe.wait_ge(t["best"], g)
                for i in range(CT):
                    mm = pe.matmul(bank[1][:, i * EXPERTS:i * EXPERTS + EXPERTS], f_xt[:, i * P:i * P + P], gate_w[:, :],
                                   start=True, stop=True)
                mm.then_inc(t["logits"], 1)

            def shared_in(c):
                g = c + STEPS * k
                pe.wait_ge(t["h"], 2 * g + CREDIT)
                for n in (0, 2, 1, 3):
                    pe.matmul(bank[2 + n][:, :], shared_up[:, n * P:n * P + P], f_xt_all[:, bass.ds(c * CHUNK, CHUNK)],
                              start=True, stop=True).then_inc(t["shared"], 1)

            def shared_out(c):
                g = c + STEPS * k
                pe.wait_ge(t["h"], 2 * g + 2 + CREDIT)
                pe.wait_ge(t["down"], g + CREDIT)
                for i in range(CT):
                    for half in range(2):
                        mm = pe.matmul(bank[6][:, i * C:i * C + C], f_h[half][:, i * P:i * P + P],
                                       shared_down[:, half * C:half * C + C], start=(half == 0), stop=(half == 1))
                mm.then_inc(t["y"], 1)

            chunks(pe, [(shared_in, 0), (turn, 1), (logits, 1), (shared_out, 0)],
                   last=[(shared_in, 0), (turn, 1), (logits, 1)])
            pe.wait_ge(t["best"], STEPS * (k + 1))
            pe.wait_ge(zero_row, 2)
            pe.matmul(bank[1][:, :], ones_bf, f_one_hot[:, :], start=True, stop=True).then_inc(t["counts"], 1)
            pe.matmul(bank[0][:, :], later_bf, f_one_hot[:, :], start=True, stop=True).then_inc(t["rank"], 1)
            shared_out(STEPS - 2)
            shared_in(STEPS - 1)
            shared_out(STEPS - 1)
            pe.wait_ge(t["rows"], k + 1)
            pe.wait_ge(t["down"], STEPS * (k + 1) + CREDIT)

            expert_at = {}

            def find(stage):
                def load(s, j):
                    expert_at[stage] = pe.value_load(f_slot_at[0:1, bass.ds(s, 1)], min_val=0,
                                                     max_val=(EXPERTS - 1) * WROW)
                return load

            def turn_in(s, j):
                n = SLOTS * k + s
                pe.wait_ge(slot_in[j], 16 * (SLOTS // 4 * k + 1) + 4 * (s - j))
                pe.wait_ge(t["gxt"], n - 1 + CREDIT)
                pe.transpose(bank[j % 2][:, 0:P], f_gx[j], ident).then_inc(t["gx_t"], 1)

            def gate_up(s, j):
                n = SLOTS * k + s
                w_up = experts[:, bass.ds(expert_at["up"], 2 * INNER)]
                pe.wait_ge(t["gxt"], n + 1 + CREDIT)
                pe.wait_ge(t["sh"], n - 1 + CREDIT)
                pe.matmul(bank[2 + j % 2][:, :], f_gxt[j % 2], w_up, start=True, stop=True)\
                  .then_inc(t["gu"], 1)

            def turn_h(s, j):
                n = SLOTS * k + s
                pe.wait_ge(t["sh"], n + 1 + CREDIT)
                pe.wait_ge(t["sht"], n - 1 + CREDIT)
                for half in range(2):
                    part = slice(half * P, half * P + P)
                    mm = pe.transpose(bank[4 + j % 2][:, part], f_sh[j % 2][:, part], ident)
                mm.then_inc(t["sh_t"], 1)

            def down(s, j):
                n = SLOTS * k + s
                w_down = experts[:, bass.ds(expert_at["down"] + 2 * INNER, 2 * C)]
                pe.wait_ge(t["sht"], n + 1 + CREDIT)
                pe.wait_ge(t["y_copied"], n - 1 + CREDIT)
                for half in range(2):
                    mm = pe.matmul(bank[6 + j % 2][:, 0:C], f_sht[j % 2][:, half * P:half * P + P],
                                   w_down[:, half * C:half * C + C], start=(half == 0), stop=(half == 1))
                mm.then_inc(t["y"], 1)

            pe.wait_ge(loaded_experts, 16 * EXPERT_LOADS)
            slots(pe, [(find("up"), 0), (find("down"), -2), (turn_in, 1), (gate_up, 0), (down, -2), (turn_h, -1)])

        def slots(eng, stages):
            lead = max(d for _, d in stages)
            lag = min(d for _, d in stages)
            first, last = 4, SLOTS - 4

            def step(s, j):
                for stage, d in stages:
                    if isinstance(s, int) and not 0 <= s + d < SLOTS:
                        continue
                    stage(s + d, (j + d) % 4)

            for s in range(-lead, first):
                step(s, s % 4)
            with eng.Fori(first // 4, last // 4) as i:
                for j in range(4):
                    step(i * 4 + j, j)
            for s in range(last, SLOTS - lag):
                step(s, s % 4)

        def f_act(act, k):
            def copy_x(c):
                g = c + STEPS * k
                act.wait_ge(t["xt"], g + 1 + CREDIT)
                if not isinstance(g, int) or g > 0:
                    act.wait_ge(t["logits"], g)
                act.activation(f_xt, bank[0][:, :], ACT.Copy)
                act.activation(f_xt_all[:, bass.ds(c * CHUNK, CHUNK)], bank[0][:, :], ACT.Copy).then_inc(t["xt_copied"], 1)

            def gate_shared(c):
                g = c + STEPS * k
                for n in range(2):
                    act.wait_ge(t["shared"], 4 * g + 2 * n + 1)
                    act.wait_ge(t["h"], 2 * g + CREDIT)
                    act.activation(f_gated[n], bank[2 + n][:, :], ACT.Silu).then_inc(t["gated"], 1)

            chunks(act, [(gate_shared, 0), (copy_x, 1)])
            act.wait_ge(t["best"], STEPS * (k + 1))
            act.activation(f_score, f_best, ACT.Sigmoid).then_inc(t["scored"], 1)
            gate_shared(STEPS - 1)

            def copy_in(s, j):
                n = SLOTS * k + s
                act.wait_ge(t["gx_t"], n + 1 + CREDIT)
                act.wait_ge(t["gu"], n - 1 + CREDIT)
                act.activation(f_gxt[j % 2], bank[j % 2][:, 0:P], ACT.Copy).then_inc(t["gxt"], 1)

            def gate(s, j):
                n = SLOTS * k + s
                act.wait_ge(t["gu"], n + 1 + CREDIT)
                act.wait_ge(t["sh"], n - 1 + CREDIT)
                act.activation(f_sg[j % 2], bank[2 + j % 2][:, 0:INNER], ACT.Silu).then_inc(t["sg"], 1)

            def copy_y(s, j):
                n = SLOTS * k + s
                act.wait_ge(t["y"], STEPS * (k + 1) + n + 1 + CREDIT)
                act.wait_ge(slot_out[j], 16 * (SLOTS // 4) * k + 4 * (s - j) + CREDIT)
                act.activation(f_gy[j], bank[6 + j % 2][:, 0:C], ACT.Copy).then_inc(t["y_copied"], 1)

            slots(act, [(copy_in, 1), (gate, 0), (copy_y, -2)])

        def f_dve(dve, chain, k):
            def norm_chunk(c):
                g = c + STEPS * k

                def free():
                    dve.wait_ge(t["xt"], g + CREDIT)
                    dve.wait_ge(t["xs"], g + CREDIT)

                chunk = x_tok[:, bass.ds(c * CHUNK, CHUNK)]
                norm(dve, chain, tiles_of(chunk), f_norm[0], f_norm[1], f_norm[2], c + LN_F[k], free).then_inc(t["xn"], 1)

            def route(c):
                g = c + STEPS * k
                dve.wait_ge(t["logits"], g + 1)
                logit = bank[1][:, 0:CT * EXPERTS].rearrange("p (i e) -> p i e", e=EXPERTS)
                best = f_best[:, bass.ds(c * CT, CT)]
                chain(dve.reduce_max(best, logit, AX))
                wide = lambda a: a.unsqueeze(2).to_broadcast([P, CT, EXPERTS])
                is_best, key = (a.rearrange("p (i e) -> p i e", e=EXPERTS) for a in f_pick)
                falling = constant("expert_rank").unsqueeze(1).to_broadcast([P, CT, EXPERTS])
                chain(dve.tensor_tensor(is_best, logit, wide(best), ALU.is_ge))
                chain(dve.tensor_tensor(key, is_best, falling, ALU.mult))
                chain(dve.reduce_max(stat[:, 3 * CT:4 * CT], key, AX))
                dve.tensor_tensor(
                    f_one_hot[:, :].rearrange("p (e i) -> p i e", e=EXPERTS)[:, bass.ds(c * CT, CT), :],
                    falling, wide(stat[:, 3 * CT:4 * CT]), ALU.is_equal).then_inc(t["best"], 1)
                dve.wait_ge(t["best"], g + 1)

            def product_shared(c):
                g = c + STEPS * k
                dve.wait_ge(t["y"], g + SLOTS * k + CREDIT)
                for n in range(2):
                    dve.wait_ge(t["shared"], 4 * g + 2 * n + 2)
                    dve.wait_ge(t["gated"], 2 * g + n + 1 + CREDIT)
                    dve.tensor_tensor(f_h[n], f_gated[n], bank[4 + n][:, :], ALU.mult).then_inc(t["h"], 1)

            def add_shared(c):
                g = c + STEPS * k
                chunk = x_tok[:, bass.ds(c * CHUNK, CHUNK)]
                dve.wait_ge(t["y"], g + SLOTS * k + 1 + CREDIT)
                dve.tensor_tensor(chunk, chunk, bank[6][:, :], ALU.add).then_inc(t["down"], 1)

            chunks(dve, [(norm_chunk, 1), (add_shared, -1), (product_shared, 0), (route, 1)], chain=chain, per=8)
            by = lambda a: a.rearrange("p (e i) -> p e i", e=EXPERTS)
            spread = lambda a: a.unsqueeze(2).to_broadcast([P, EXPERTS, TILES])
            chain(dve.memset(f_ones, 1.0))
            dve.wait_ge(t["counts"], k + 1)
            chain(dve.tensor_tensor_scan(f_upto, constant("tile_reset"), bank[1][:, :], 0.0, ALU.mult, ALU.add))
            starts = constant("tile_start").unsqueeze(1).to_broadcast([P, EXPERTS, TILES])
            chain(dve.tensor_tensor(by(f_ends), spread(by(f_upto)[:, :, TILES - 1]), starts, ALU.is_gt))
            chain(dve.reduce_sum(f_tiles, by(f_ends), AX))
            chain(dve.tensor_tensor_scan(f_upto_slot, f_ones, f_tiles, 0.0, ALU.mult, ALU.add))
            chain(dve.tensor_tensor(f_first, f_upto_slot, f_tiles, ALU.subtract))
            chain(dve.tensor_scalar(f_first, f_first, float(P), None, ALU.mult))
            dve.wait_ge(t["rank"], k + 1)
            chain(dve.tensor_tensor(f_place, f_upto, bank[0][:, :], ALU.add))
            chain(dve.tensor_tensor(by(f_place), by(f_place), spread(f_first), ALU.add))
            chain(dve.tensor_tensor(f_place, f_place, f_one_hot[:, :], ALU.mult))
            chain(dve.reduce_sum(f_place_row, f_place.rearrange("p (e i) -> p i e", e=EXPERTS), AX))
            dve.tensor_copy(f_row[:, :], f_place_row).then_inc(t["placed"], 1)
            by_slot = f_slot_cmp.rearrange("p (s e) -> p s e", e=EXPERTS)
            chain(dve.tensor_tensor(by_slot, f_upto_slot.unsqueeze(1).to_broadcast([P, SLOTS, EXPERTS]),
                                    constant("slot_no").unsqueeze(2).to_broadcast([P, SLOTS, EXPERTS]), ALU.is_le))
            chain(dve.reduce_sum(f_slot_row, by_slot, AX))
            chain(dve.tensor_scalar(f_slot_row, f_slot_row, EXPERTS - 1.0, float(WROW), ALU.min, ALU.mult))
            dve.tensor_copy(f_slot_at[:, :], f_slot_row).then_inc(t["rows"], 1)
            add_shared(STEPS - 2)
            product_shared(STEPS - 1)
            add_shared(STEPS - 1)

            def product(s, j):
                n = SLOTS * k + s
                dve.wait_ge(t["sg"], n + 1 + CREDIT)
                dve.wait_ge(t["sh_t"], n - 1 + CREDIT)
                dve.tensor_tensor(f_sh[j % 2], f_sg[j % 2], bank[2 + j % 2][:, INNER:2 * INNER], ALU.mult)\
                   .then_inc(t["sh"], 1)

            def copy_h(s, j):
                n = SLOTS * k + s
                dve.wait_ge(t["sh_t"], n + 1 + CREDIT)
                dve.wait_ge(t["y"], STEPS * (k + 1) + n - 1 + CREDIT)
                dve.tensor_copy(f_sht[j % 2], bank[4 + j % 2][:, 0:INNER]).then_inc(t["sht"], 1)

            slots(dve, [(copy_h, -1), (product, 0)])
            dve.wait_ge(t["down"], STEPS * (k + 1) + CREDIT)

        def add_experts(dve, k, c):
            dve.wait_ge(gathered[c], 16 * CT * (k + 1))
            part = slice(c * CHUNK, c * CHUNK + CHUNK)
            return dve.tensor_tensor(x_tok[:, part], x_tok[:, part], f_back[:, part], ALU.add)

        def f_pool(pool, k):
            def power(c):
                norm_power(pool, c + LN_F[k])

            def keep_x(c):
                pool.wait_ge(t["xn"], c + STEPS * k + 1)
                pool.tensor_copy(f_xs[:, bass.ds(c * CHUNK, CHUNK)], f_norm[2]).then_inc(t["xs"], 1)

            chunks(pool, [(power, 1), (keep_x, 1)])
            x3 = f_xs.rearrange("p (i c) -> p i c", c=C)
            pool.wait_ge(t["xs"], STEPS * (k + 1) + CREDIT)
            pool.wait_ge(t["scored"], k + 1 + CREDIT)
            pool.tensor_tensor(x3, x3, f_score.unsqueeze(2).to_broadcast([P, TILES, C]), ALU.mult).then_inc(t["scaled"], 1)
            pool.wait_ge(t["scaled"], k + 1)
            pool.wait_ge(t["placed"], k + 1)
            pool.wait_ge(zeroed, 16)
            for i in range(TILES):
                pool.indirect_dma_start(out=sorted_x, out_offset=bass.IndirectOffsetOnAxis(ap=f_row[:, i:i + 1], axis=0),
                                        in_=f_xs[:, i * C:i * C + C], in_offset=None).then_inc(scattered, 16)
            for j in range(4):
                pool.wait_ge(slot_out[j], 16 * (SLOTS // 4) * (k + 1) + CREDIT)

        def gather(pool, c):
            for i in range(c * CT, c * CT + CT):
                pool.indirect_dma_start(out=f_back[:, i * C:i * C + C], out_offset=None, in_=sorted_y,
                                        in_offset=bass.IndirectOffsetOnAxis(ap=f_row[:, i:i + 1], axis=0))\
                    .then_inc(gathered[c], 16)

        def f_sp(sp, k):
            sp.wait_ge(scattered, 16 * TILES * (k + 1))

            def fetch(s, j):
                n = SLOTS * k + s
                if not isinstance(n, int) or n >= 4:
                    sp.wait_ge(t["gx_t"], n - 3 + CREDIT)
                sp.dma_start(f_gx[j], sorted_x[bass.ds(s * P, P), :]).then_inc(slot_in[j], 16)

            def store(s, j):
                sp.wait_ge(t["y_copied"], SLOTS * k + s + 1 + CREDIT)
                sp.dma_start(sorted_y[bass.ds(s * P, P), :], f_gy[j]).then_inc(slot_out[j], 16)

            slots(sp, [(fetch, 3), (store, -3)])

        used[0] = 0
        b_x = carve(TOK)
        b_odd, b_even = carve(OCT), carve(OCT)
        b_q, b_k = carve(OCT), carve(OCT)
        b_v = [carve(SUB * 3 * D_B).rearrange("p (i c) -> p i c", c=3 * D_B) for _ in range(2)]
        b_s, b_st = carve(2 * SUB * 32), carve(2 * SUB * 32)
        b_max = carve(2 * SUB)
        b_wide = [carve(2 * SUB * P).rearrange("p (s q) -> p s q", q=P) for _ in range(2)]
        b_yt = carve(TOK)
        pools_at = used[0]
        b_at = carve(TOK)
        b_yc, b_ac = carve(OCT), carve(OCT)
        b_yn = carve(TOK)
        b_w, b_w_next = carve(3 * P), carve(3 * P)
        b_wo = carve(C)
        b_bias = carve(C)
        b_norm = [b_q[:, 0:CHUNK], b_q[:, CHUNK:OCT], b_k[:, 0:CHUNK]]
        b_pool, at = [b_x], pools_at
        for level in range(1, LEVELS + 1):
            b_pool.append(arena[:, at:at + TOK // 2 ** level])
            at += TOK // 2 ** level
        FIRST_OF = [sum(TOK // 2 ** (l + 1) for l in range(1, level)) for level in range(1, LEVELS + 2)]

        h = {n: sem("b_" + n) for n in (
            "xn xt x pooled packed ready w_copied proj q_out s_done masked st expd av y_out a_out divided normed o "
            "acc").split()}
        w_in, wo_in, bias_in = sem("b_w_in"), sem("b_wo_in"), sem("b_bias_in")
        credited += [h[n] for n in "xt x q_out s_done masked expd av y_out a_out divided normed o acc".split()]

        def attention(eng, order, chain=None, per=0):
            lead, lag = max(d for _, d in order), min(d for _, d in order)

            def step(p, k):
                for stage, d in order:
                    u = 3 * p + k + d
                    if isinstance(u, int) and not 0 <= u < 3 * PAIRS:
                        continue
                    stage(p + (k + d) // 3, (k + d) % 3, u, (k + d) % 2)

            for k in range(-lead, 6):
                step(0, k)
            with eng.Fori(1, PAIRS // 2 - 1) as i:
                if chain:
                    chain.enter(i - 1, per)
                for k in range(6):
                    step(2 * i, k)
            if chain:
                chain.leave(PAIRS // 2 - 2)
            for k in range(6 - lag):
                step(PAIRS - 2, k)

        def by_head(name, head):
            rows = slice(0, D_B) if (name == "y") == (head == 0) else slice(D_B, P)
            return psum[rows, (4 + 2 * head) * 512:(6 + 2 * head) * 512]

        def add_levels(eng, chain, fine, coarse):
            for level in range(1, LEVELS + 1):
                span = 2 ** level
                at, count = FIRST_OF[level - 1], TOK // (2 * span)
                dst = fine.rearrange("p (g c s) -> p g c s", c=32, s=span)[:, :, 16:32, span - 1]
                chain(eng.tensor_tensor(dst, dst, coarse[:, at:at + count].rearrange("p (g c) -> p g c", c=16), ALU.add))

        def outputs_used(eng, p, o):
            if isinstance(p, int) and p == 0:
                return
            eng.wait_ge(h["normed"], (2 * p + o - 1 if o < 2 else 2 * p) + CREDIT)

        def b_columns(o, odd):
            return b_x[:, o * OCT:o * OCT + OCT] if o < 2 else (b_odd if odd else b_even)

        def b_pe(pe):
            with pe.Fori(0, STEPS) as c:
                pe.wait_ge(h["xn"], c + 1)
                pe.wait_ge(h["x"], c + CREDIT)
                for i in range(CT):
                    mm = pe.transpose(bank[0][:, i * P:i * P + P], b_norm[2][:, i * C:i * C + C], ident)
                mm.then_inc(h["xt"], 1)
            pe.wait_ge(h["x"], STEPS + CREDIT)
            pe.wait_ge(h["packed"], 1)
            pe.wait_ge(h["ready"], 1)

            def project_qk(p, o, u, r):
                if o == 0:
                    pe.wait_ge(h["w_copied"], p + 1)
                if o == 1 and (not isinstance(p, int) or p >= 2):
                    pe.wait_ge(h["acc"], 4 * (p - 1) + CREDIT)
                for n in range(4):
                    if not isinstance(u, int) or u > 0 or n > 0:
                        pe.wait_ge(h["q_out"], 6 * u + n - 1 + CREDIT)
                    pe.matmul(bank[n % 2][:, :], b_w[:, n // 2 * P:n // 2 * P + P],
                              b_columns(o, n < 2)[:, n % 2 * 512:n % 2 * 512 + 512],
                              start=True, stop=True).then_inc(h["proj"], 1)

            def project_v(p, o, u, r):
                for i in range(SUB):
                    if i % 4 == 0:
                        pe.wait_ge(h["q_out"], 6 * u + 3 + i // 4 + CREDIT)
                    if i == 5:
                        pe.wait_ge(h["masked"], u + CREDIT)
                    mm = pe.matmul(bank[i // 4][:, i % 4 * P:i % 4 * P + P], b_columns(o, False)[:, i * P:i * P + P],
                                   b_w[:, 2 * P:3 * P], start=True, stop=True)
                    if i % 4 == 3:
                        mm.then_inc(h["proj"], 1)

            def scores(p, o, u, r):
                for i in range(SUB):
                    for half in range(2):
                        for head in range(2):
                            rows = slice(head * D_B, head * D_B + D_B)
                            tok = slice(i * P + 64 * half, i * P + 64 * half + 64)
                            mm = pe.matmul(bank[2 + head][64 * half:64 * half + 64, i * 64:i * 64 + 64],
                                           b_q[rows, tok], b_k[rows, tok], start=True, stop=True)
                mm.then_inc(h["s_done"], 1)

            def weighted(p, o, u, r):
                pe.wait_ge(h["expd"], u + 1 + CREDIT)
                pe.wait_ge(h["q_out"], 6 * u + 6 + CREDIT)
                pe.wait_ge(h["y_out"], 2 * u + CREDIT)
                pe.wait_ge(h["a_out"], 2 * u + CREDIT)
                for head in range(2):
                    for i in range(SUB):
                        mm = pe.matmul(bank[4 + 2 * head + i // 4][:, i % 4 * P:i % 4 * P + P],
                                       b_v[r][:, i, head * D_B:head * D_B + P], b_wide[r][:, head * SUB + i, :],
                                       start=True, stop=True)
                mm.then_inc(h["av"], 1)

            def project_out(p, o, u, r):
                if o != 2:
                    return
                pe.wait_ge(h["normed"], 2 * p + 2 + CREDIT)
                pe.wait_ge(wo_in, 16 * p + 16)
                last = isinstance(u, int) and u + 4 >= 3 * PAIRS
                pe.wait_ge(h["q_out"], (18 * PAIRS if last else 6 * (u + 4) + 6) + CREDIT)
                for i in range(TILES):
                    if i % 4 == 0 and i >= 8:
                        pe.wait_ge(h["acc"], 4 * p + i // 4 - 1 + CREDIT)
                    mm = pe.matmul(bank[i // 4 % 2][:, i % 4 * C:i % 4 * C + C], b_yn[:, i * P:i * P + P], b_wo,
                                   start=True, stop=True)
                    if i % 4 == 3:
                        mm.then_inc(h["o"], 1)

            attention(pe, [(project_qk, 1), (project_v, 1), (scores, 1), (project_out, -3), (weighted, 0)])

        def b_act(act):
            with act.Fori(0, STEPS) as c:
                act.wait_ge(h["xt"], c + 1 + CREDIT)
                act.activation(b_x[:, bass.ds(c * CHUNK, CHUNK)], bank[0][:, :], ACT.Copy).then_inc(h["x"], 1)
            for level in range(1, LEVELS + 1):
                act.wait_ge(h["pooled"], level)
                n = TOK // 2 ** (level + 1)
                blocks = b_pool[level].rearrange("p (g two i) -> p g two i", two=2, i=16)
                for side, dst, scale in ((0, b_even, 1.0), (1, b_odd, 0.25 ** level)):
                    i = act.activation(dst[:, FIRST_OF[level - 1]:FIRST_OF[level - 1] + n]
                                       .rearrange("p (g i) -> p g i", i=16), blocks[:, :, side, :], ACT.Copy, scale=scale)
            i.then_inc(h["packed"], 1)
            act.wait_ge(h["ready"], 1)

            def copy_weights(p):
                act.wait_ge(w_in, 16 * p + 16)
                act.activation(b_w, b_w_next, ACT.Copy).then_inc(h["w_copied"], 1)

            def copy_bank(u, n):
                act.wait_ge(h["proj"], 6 * u + n + 1)
                dst = (b_q, b_k)[n // 2][:, n % 2 * 512:n % 2 * 512 + 512]
                act.activation(dst, bank[n % 2][:, :], ACT.Copy, scale=(D_B ** -0.5, 1.0)[n // 2]).then_inc(h["q_out"], 1)

            def copy_q(p, o, u, r):
                act.wait_ge(h["s_done"], u + CREDIT)
                for n in range(2):
                    copy_bank(u, n)

            def copy_k(p, o, u, r):
                for n in range(2, 4):
                    copy_bank(u, n)

            def copy_v(p, o, u, r):
                act.wait_ge(h["av"], (max(u - 1, 0) if isinstance(u, int) else u - 1) + CREDIT)
                heads = b_v[r].rearrange("p i (a d) -> p i a d", d=D_B)[:, :, 0:3:2, :]
                for n in range(2):
                    act.wait_ge(h["proj"], 6 * u + 5 + n)
                    act.activation(heads[:, 4 * n:4 * n + 4],
                                   bank[n][:, :].rearrange("p (i a d) -> p i a d", a=2, d=D_B), ACT.Copy)\
                       .then_inc(h["q_out"], 1)
                if o == 2 and not (isinstance(u, int) and u == 3 * PAIRS - 1):
                    copy_weights(p + 1)

            def exponents(p, o, u, r):
                act.wait_ge(h["st"], u + 1)
                act.wait_ge(h["av"], (max(u - 1, 0) if isinstance(u, int) else u - 1) + CREDIT)
                for j in range(4):
                    q = slice(32 * j, 32 * j + 32)
                    i = act.activation(b_wide[r][q, :, q], b_st[q, :].rearrange("p (s q) -> p s q", q=32), ACT.Exp)
                i.then_inc(h["expd"], 1)

            def copy_y(p, o, u, r):
                if o > 0:
                    copy_outputs(p, o, u)

            def copy_first_y(p, o, u, r):
                if o == 0:
                    copy_outputs(p, o, u)

            def copy_outputs(p, o, u):
                act.wait_ge(h["av"], u + 1 + CREDIT)
                outputs_used(act, p, o)
                dst = b_yt[:, o * OCT:o * OCT + OCT] if o < 2 else b_yc
                for head in range(2):
                    act.activation(dst[head * D_B:head * D_B + D_B, :], by_head("y", head), ACT.Copy).then_inc(h["y_out"], 1)

            copy_weights(0)
            attention(act, [(copy_q, 1), (copy_k, 1), (copy_y, -1), (exponents, 0), (copy_first_y, -1), (copy_v, 1)])

        def b_dve(dve, chain):
            for c in range(STEPS):
                chain(add_experts(dve, 0, c))
                norm(dve, chain, tiles_of(x_tok[:, c * CHUNK:c * CHUNK + CHUNK]), *b_norm, c + LN_B,
                     lambda: dve.wait_ge(h["xt"], c + CREDIT)).then_inc(h["xn"], 1)
            dve.wait_ge(h["x"], STEPS + CREDIT)
            chain(dve.memset(b_odd[:, COARSE:OCT], 0.0))
            chain(dve.memset(b_even[:, COARSE:OCT], 0.0))
            for level in range(1, LEVELS + 1):
                two = b_pool[level - 1].rearrange("p (n two) -> p n two", two=2)
                dve.tensor_tensor(b_pool[level], two[:, :, 0], two[:, :, 1], ALU.add).then_inc(h["pooled"], 1)
                dve.wait_ge(h["pooled"], level)
            dve.wait_ge(bias_in, 16)
            x3 = x_tok[:, :].rearrange("p (i c) -> p i c", c=C)
            chain(dve.tensor_tensor(x3, x3, b_bias.unsqueeze(1).to_broadcast([P, TILES, C]), ALU.add))
            dve.wait_ge(h["packed"], 1)

            def soften(p, o, u, r):
                mask = constant("mask_causal" if o < 2 else "mask_block")
                s3 = b_s.rearrange("p (s k) -> p s k", k=32)
                dve.wait_ge(h["s_done"], u + 1 + CREDIT)
                if not isinstance(u, int) or u > 0:
                    dve.wait_ge(h["st"], u)
                for j in range(4):
                    rows = slice(32 * j, 32 * j + 32)
                    blocks = psum[rows, 2 * 512:4 * 512].rearrange("p (s k) -> p s k", k=64)
                    blocks = blocks[:, :, j % 2 * 32:j % 2 * 32 + 32]
                    i = dve.tensor_tensor(s3[rows], blocks, mask[rows].unsqueeze(1).to_broadcast([32, 2 * SUB, 32]), ALU.add)
                i.then_inc(h["masked"], 1)
                dve.wait_ge(h["masked"], u + 1 + CREDIT)
                chain(dve.reduce_max(b_max, s3, AX))
                chain(dve.tensor_tensor(s3, s3, b_max.unsqueeze(2).to_broadcast([P, 2 * SUB, 32]), ALU.subtract))
                dve.wait_ge(h["expd"], u + CREDIT)
                dve.transpose(b_st, b_s).then_inc(h["st"], 1)

            def copy_sums(p, o, u, r):
                dve.wait_ge(h["av"], u + 1 + CREDIT)
                outputs_used(dve, p, o)
                dst = b_at[:, o * OCT:o * OCT + OCT] if o < 2 else b_ac
                for head in range(2):
                    if o < 2:
                        i = dve.tensor_scalar(dst[head * D_B:head * D_B + D_B, :], by_head("a", head), 1e-8, None, ALU.add)
                    else:
                        i = dve.tensor_copy(dst[head * D_B:head * D_B + D_B, :], by_head("a", head))
                    i.then_inc(h["a_out"], 1)

            def divide(batch):
                def stage(p, o, u, r):
                    if o == 2:
                        if batch == 0:
                            dve.wait_ge(h["a_out"], 2 * u + 2 + CREDIT)
                            add_levels(dve, chain, b_at, b_ac)
                        part = b_at[:, batch * OCT:batch * OCT + OCT]
                        dve.reciprocal(part, part).then_inc(h["divided"], 1)
                return stage

            def gather_out(p, o, u, r):
                if o != 2:
                    return
                for n in range(4):
                    dve.wait_ge(h["o"], 4 * p + n + 1 + CREDIT)
                    part = slice(n * 512, n * 512 + 512)
                    dve.tensor_tensor(x_tok[:, part], x_tok[:, part], bank[n % 2][:, :], ALU.add).then_inc(h["acc"], 1)

            attention(dve, [(divide(0), -1), (divide(1), -2), (soften, 1), (gather_out, -3), (copy_sums, 0)],
                      chain, 2 * (3 * 2 + LEVELS))
            dve.wait_ge(h["acc"], 4 * PAIRS + CREDIT)

        def b_pool_engine(pool):
            gather(pool, 0)
            for c in range(STEPS):
                if c + 1 < STEPS:
                    gather(pool, c + 1)
                norm_power(pool, c + LN_B)
            for r in range(2):
                pool.memset(b_wide[r], 0.0)
                i = pool.memset(b_v[r][:, :, D_B:2 * D_B], 1.0)
            i.then_inc(h["ready"], 1)
            chain = Chain(pool, pool_chain)

            def join(p, o, u, r):
                if o != 2:
                    return
                pool.wait_ge(h["y_out"], 2 * u + 2 + CREDIT)
                add_levels(pool, chain, b_yt, b_yc)

            def scale(p, o, u, r):
                if o != 2:
                    return
                pool.wait_ge(h["o"], 4 * p + CREDIT)
                for b in range(BATCH):
                    part = slice(b * OCT, b * OCT + OCT)
                    pool.wait_ge(h["divided"], 2 * p + b + 1 + CREDIT)
                    pool.tensor_tensor(b_yn[:, part], b_yt[:, part], b_at[:, part], ALU.mult).then_inc(h["normed"], 1)

            attention(pool, [(join, 0), (scale, 0)], chain, 2 * LEVELS)

        def b_sp(sp):
            def weights_in(p):
                sp.dma_start(b_w_next.rearrange("p (n c) -> p n c", c=P),
                             w["w_qkv"][bass.ds(p, 1)].rearrange("a c n j -> (a c) n j")).then_inc(w_in, 16)

            def out_weights_in(p):
                sp.dma_start(b_wo, w["w_out"][bass.ds(p, 1)].rearrange("a c j -> (a c) j")).then_inc(wo_in, 16)

            sp.wait_ge(h["xn"], 1)
            sp.dma_start(b_bias, w["b_out"].to_broadcast([P, C])).then_inc(bias_in, 16)
            weights_in(0)
            out_weights_in(0)
            sp.wait_ge(h["w_copied"], 1)
            weights_in(1)
            with sp.Fori(2, PAIRS) as p:
                sp.wait_ge(h["w_copied"], p)
                weights_in(p)
                sp.wait_ge(h["o"], 4 * (p - 1) + CREDIT)
                out_weights_in(p - 1)
            sp.wait_ge(h["o"], 4 * (PAIRS - 1) + CREDIT)
            out_weights_in(PAIRS - 1)

        final = sem("final")
        block = ctx.enter_context(nc.Block())
        loads = [(const[:, :], w["constants"][:, 0:CONST["pick"][0]]), (vectors[:, :], w["vectors"]),
                 (w1, w["maa_w1"]), (w2, w["maa_w2"]), (dw1, w["decay_w1"]), (dw2[0:DECAY, :], w["decay_w2"]),
                 (wrkvo, w["wrkvo"])]
        later = [(pick, w["constants"][:, CONST["pick"][0]:CONST_COLS]), (gate_w[:, :], w["gate_w"]),
                 (shared_up[:, :], w["shared_up"]),
                 (shared_down[:, :].rearrange("p (f c) -> p f c", c=C), w["shared_down"].rearrange("(f p) c -> p f c", p=P))]
        LOADS, LATER_LOADS = len(loads), len(later)
        EXPERT_LOADS = 8

        @block.sync
        def _(sp):
            for c in credited:
                sp.sem_inc(c, CREDIT)
            sp.dma_start(tiles_of(x_tok[:, :]), w["x"].rearrange("i p c -> p i c")).then_inc(loaded_x, 16)
            for dst, src in loads:
                sp.dma_start(dst, src).then_inc(loaded, 16)
            for dst, src in later:
                sp.dma_start(dst, src).then_inc(loaded_later, 16)
            for i in range(EXPERT_LOADS):
                part = slice(i * EXPERTS * WROW // EXPERT_LOADS, (i + 1) * EXPERTS * WROW // EXPERT_LOADS)
                sp.dma_start(experts[:, part], w["experts"][:, part]).then_inc(loaded_experts, 16)
            sp.wait_ge(zero_row, 1)
            sp.dma_start(sorted_x.rearrange("(s p) c -> p s c", p=P), zeros[:, :].unsqueeze(1).to_broadcast([P, SLOTS, C]))\
              .then_inc(zeroed, 16)
            f_sp(sp, 0)
            b_sp(sp)
            f_sp(sp, 1)
            for c in range(STEPS):
                sp.wait_ge(final, c + 1)
                sp.dma_start(out[c * CT:c * CT + CT].rearrange("i p c -> p i c"),
                             tiles_of(x_tok[:, c * CHUNK:c * CHUNK + CHUNK])).then_inc(stored, 16)
            sp.wait_ge(stored, 16 * STEPS)

        @block.tensor
        def _(pe):
            a_pe(pe)
            f_pe(pe, 0)
            b_pe(pe)
            f_pe(pe, 1)

        @block.scalar
        def _(act):
            a_act(act)
            f_act(act, 0)
            b_act(act)
            f_act(act, 1)

        @block.gpsimd
        def _(pool):
            pool.memset(zeros[:, :], 0.0).then_inc(zero_row, 1)
            pool.memset(ones_bf, 1.0)
            pool.wait_ge(loaded, LOADS * 16)
            pool.tensor_copy(later_bf, constant("later")).then_inc(zero_row, 1)
            a_pool(pool)
            f_pool(pool, 0)
            b_pool_engine(pool)
            f_pool(pool, 1)
            for c in range(STEPS):
                gather(pool, c)

        @block.vector
        def _(dve):
            chain = a_dve(dve)
            f_dve(dve, chain, 0)
            b_dve(dve, chain)
            f_dve(dve, chain, 1)
            for c in range(STEPS):
                add_experts(dve, 1, c).then_inc(final, 1)


def _constants():
    import numpy as np

    c = np.zeros((P, CONST_COLS), np.float32)

    def put(name, value):
        at, width = CONST[name]
        c[:, at:at + width] = np.broadcast_to(value, (P, width))

    row = np.arange(P)
    put("ident", np.eye(P))
    put("head_ones", row[:, None] // N_A == row[None, :] // N_A)
    pick = np.zeros((P, N_A, P))
    for m in range(N_A):
        pick[:, m] = (row[:, None] // N_A == row[None, :] // N_A) & (row[None, :] % N_A == m)
    put("pick", pick.reshape(P, -1))
    put("later", (row[:, None] < row[None, :]) - 1.0)
    put("expert_rank", (32.0 - np.arange(32))[None])
    put("tile_reset", (np.arange(512) % 16 != 0)[None])
    put("slot_no", np.arange(float(SLOTS))[None])
    put("tile_start", (P * np.arange(float(TILES)))[None])
    q, k = row[:, None] % 32, np.arange(32)[None]
    put("mask_causal", np.where((q // 16 == k // 16) & (k <= q), 0.0, -1e30))
    put("mask_block", np.where(q // 16 == k // 16, 0.0, -1e30))
    put("half", -0.5)
    return c


def kernel(**inputs):
    import numpy as np
    import concourse.bacc as bacc
    from concourse.bass_utils import run_bass_kernel_spmd as run

    nc = bacc.Bacc("TRN2", target_bir_lowering=False, num_devices=1)
    a = {n.replace("L0_", ""): np.asarray(v) for n, v in inputs.items()}
    col = lambda v: np.ascontiguousarray(v.reshape(C, 1))
    laid = {
        "x": a["attn_a_x"].reshape(TILES, P, C),
        "vectors": np.concatenate([col(a["attn_a_" + n]) for n in (
            "time_maa_x", "time_maa_w", "time_maa_k", "time_maa_v", "time_maa_r",
            "time_decay", "time_faaaa", "ln_g", "ln_b")], 1),
        "b_out": a["attn_b_b_out"].reshape(1, C),
        "maa_w1": a["attn_a_maa_w1"],
        "maa_w2": a["attn_a_maa_w2"].reshape(4 * MIX, C),
        "decay_w1": a["attn_a_decay_w1"],
        "decay_w2": a["attn_a_decay_w2"],
        "wrkvo": np.concatenate([a["attn_a_" + n] for n in ("Wr", "Wk", "Wv", "Wo")], 1),
        "w_qkv": np.ascontiguousarray(
            a["attn_b_w_qkv"].reshape(3, PAIRS, P, C).transpose(1, 3, 0, 2)),
        "w_out": np.ascontiguousarray(a["attn_b_w_out"].reshape(C, PAIRS, P).transpose(1, 2, 0)),
        "gate_w": a["ffn_gate_w"],
        "shared_up": np.concatenate([a["ffn_shared_gate_w"], a["ffn_shared_up_w"]], 1),
        "shared_down": a["ffn_shared_down_w"],
        "experts": np.concatenate([
            a["ffn_routed_gate_w"].transpose(1, 0, 2), a["ffn_routed_up_w"].transpose(1, 0, 2),
            a["ffn_routed_down_w"].reshape(EXPERTS, INNER // P, P, C).transpose(2, 0, 1, 3).reshape(P, EXPERTS, -1),
        ], 2).reshape(P, EXPERTS * WROW),
        "constants": _constants(),
    }
    arrays, aps = {}, {}
    for name, v in laid.items():
        v = np.ascontiguousarray(v)
        arrays["in_" + name] = v
        aps[name] = nc.dram_tensor("in_" + name, v.shape, mybir.dt.from_np(v.dtype), kind="ExternalInput").ap()
    out = nc.dram_tensor("out_0", (TILES, P, C), F32, kind="ExternalOutput").ap()
    hybrid_block(nc, aps, out)
    r = run(nc, [arrays], core_ids=[0])
    return r.results[0]["out_0"].reshape(BATCH, SEQ, C)
```
